# Optimizing a Trainium2 kernel written in Bass

```python
import numpy as np
import jax
import jax.numpy as jnp

def _softmax(x, axis=-1):
    return jax.nn.softmax(x, axis=axis)

def _gelu(x):
    return jax.nn.gelu(x, approximate=True)

def _silu(x):
    return jax.nn.silu(x)

def _sigmoid(x):
    return jax.nn.sigmoid(x)

def _layernorm(x, axis=-1, eps=1e-05):
    m = jnp.mean(x, axis=axis, keepdims=True)
    v = jnp.var(x, axis=axis, keepdims=True)
    return (x - m) / jnp.sqrt(v + eps)

def _scatter_add(tgt, idx, src, axis=0):
    return tgt.at[idx].add(src)

def _segment_sum(src, seg, n):
    return jax.ops.segment_sum(src, seg, n)
kernel_name = 'mk_seq_preln_d2_jaxref_r8_3e2ecb'

def setup_inputs(seed: int=0):
    np.random.seed(seed)
    _w = jnp.asarray

    def _L0_attn_setup():
        import jax, jax.numpy as jnp
        import numpy as np
        B, S, D, O = (8, 256, 128, 128)
        key = jax.random.key(seed)
        k_in, k_a, k_bc = jax.random.split(key, 3)
        inputs = jax.random.normal(k_in, (B, S, D), dtype=jnp.float32)
        A = jax.random.uniform(k_a, (D,), minval=-0.99, maxval=0.99, dtype=jnp.float32)
        BC = jax.random.normal(k_bc, (D, O), dtype=jnp.float32) / D
        return {'inputs': inputs, 'A': A, 'BC': BC}
    _L0_attn_in = _L0_attn_setup()

    def _L0_ffn_setup():
        import jax, jax.numpy as jnp
        import numpy as np
        DIM = 128
        DEPTH = 2
        HEADS = 8
        DIM_HEAD = 64
        WINDOW = 64
        INNER = HEADS * DIM_HEAD
        HID = int(DIM * 4 * 2 / 3)
        B, N = (2, 1024)
        QK_SCALE = 8.0

        def shift_token(t):
            t1, t2 = jnp.split(t, 2, axis=-1)
            t2 = jnp.pad(t2, ((0, 0), (1, 0), (0, 0)))[:, :-1]
            return jnp.concatenate([t1, t2], axis=-1)

        def l2norm(t):
            return t / jnp.clip(jnp.linalg.norm(t, axis=-1, keepdims=True), 1e-12)

        def rotate_half(x):
            x1, x2 = jnp.split(x, 2, axis=-1)
            return jnp.concatenate([-x2, x1], axis=-1)

        def rotary_xpos(q, k):
            n = q.shape[-2]
            half_idx = jnp.arange(0, DIM_HEAD, 2, dtype=jnp.float32)
            inv_freq = 1.0 / 10000.0 ** (half_idx / DIM_HEAD)
            t = jnp.arange(n, dtype=jnp.float32)
            freqs = t[:, None] * inv_freq[None, :]
            freqs = jnp.concatenate([freqs, freqs], axis=-1)
            base = (half_idx + 0.4 * DIM_HEAD) / (1.4 * DIM_HEAD)
            power = (t - n // 2) / float(WINDOW // 2)
            scale = base[None, :] ** power[:, None]
            scale = jnp.concatenate([scale, scale], axis=-1)
            cos, sin = (jnp.cos(freqs), jnp.sin(freqs))
            q = q * cos * scale + rotate_half(q) * sin * scale
            k = k * cos / scale + rotate_half(k) * sin / scale
            return (q, k)

        def local_attention(q, k, v):
            b, h, n, d = q.shape
            w = n // WINDOW
            bq = q.reshape(b, h, w, WINDOW, d) * QK_SCALE
            bk = k.reshape(b, h, w, WINDOW, d)
            bv = v.reshape(b, h, w, WINDOW, d)

            def look_around(t):
                p = jnp.pad(t, ((0, 0), (0, 0), (1, 0), (0, 0), (0, 0)))
                return jnp.concatenate([p[:, :, :w], p[:, :, 1:]], axis=3)
            bk, bv = (look_around(bk), look_around(bv))
            bt = jnp.arange(n).reshape(w, WINDOW)
            btp = jnp.pad(bt, ((1, 0), (0, 0)), constant_values=-1)
            btk = jnp.concatenate([btp[:w], btp[1:]], axis=1)
            sim = jnp.einsum('bhwid,bhwjd->bhwij', bq, bk)
            i = bt[:, :, None]
            j = btk[:, None, :]
            mask = (i < j) | (i > j + WINDOW) | (j == -1)
            sim = jnp.where(mask, -jnp.finfo(sim.dtype).max, sim)
            attn = jax.nn.softmax(sim, axis=-1)
            out = jnp.einsum('bhwij,bhwjd->bhwid', attn, bv)
            return out.reshape(b, h, n, d)

        def _layer(x, wqkv, qs, ksc, wo, lg, lb, w1, b1, w2, b2):
            b, n, _ = x.shape
            h = shift_token(x)
            qkv = h @ wqkv
            q, k, v = jnp.split(qkv, 3, axis=-1)
            to_heads = lambda t: t.reshape(b, n, HEADS, DIM_HEAD).transpose(0, 2, 1, 3)
            q, k, v = (to_heads(q), to_heads(k), to_heads(v))
            q = l2norm(q) * qs
            k = l2norm(k) * ksc
            q, k = rotary_xpos(q, k)
            o = local_attention(q, k, v)
            o = o.transpose(0, 2, 1, 3).reshape(b, n, INNER)
            x = x + o @ wo
            h = shift_token(x)
            mu = h.mean(-1, keepdims=True)
            var = h.var(-1, keepdims=True)
            h = (h - mu) / jnp.sqrt(var + 1e-05) * lg + lb
            h = h @ w1 + b1
            a, g = jnp.split(h, 2, axis=-1)
            h = a * jax.nn.gelu(g, approximate=False)
            x = x + h @ w2 + b2
            return x
        key = jax.random.key(seed)
        ks = jax.random.split(key, 6)
        return {'x': jax.random.normal(ks[0], (B, N, DIM), jnp.float32), 'wqkv': jax.random.normal(ks[1], (DEPTH, DIM, 3 * INNER), jnp.float32) * 0.02, 'q_scale': jnp.ones((DEPTH, DIM_HEAD), jnp.float32), 'k_scale': jnp.ones((DEPTH, DIM_HEAD), jnp.float32), 'wo': jax.random.normal(ks[2], (DEPTH, INNER, DIM), jnp.float32) * 0.02, 'ln_g': jnp.ones((DEPTH, DIM), jnp.float32), 'ln_b': jnp.zeros((DEPTH, DIM), jnp.float32), 'w1': jax.random.normal(ks[3], (DEPTH, DIM, 2 * HID), jnp.float32) * 0.02, 'b1': jnp.zeros((DEPTH, 2 * HID), jnp.float32), 'w2': jax.random.normal(ks[4], (DEPTH, HID, DIM), jnp.float32) * 0.02, 'b2': jnp.zeros((DEPTH, DIM), jnp.float32)}
    _L0_ffn_in = _L0_ffn_setup()

    def _L1_attn_setup():
        import jax, jax.numpy as jnp
        import numpy as np
        H = 8
        LN_EPS = 1e-05
        key = jax.random.key(seed)
        ks = jax.random.split(key, 4)
        B, S, D = (4, 256, 128)
        x = jax.random.normal(ks[0], (B, S, D), dtype=jnp.float32)
        sc = 1.0 / np.sqrt(D)
        Wq = jax.random.normal(ks[1], (D, D), dtype=jnp.float32) * sc
        Wk = jax.random.normal(ks[2], (D, D), dtype=jnp.float32) * sc
        Wv = jax.random.normal(ks[3], (D, D * H), dtype=jnp.float32) * sc
        return {'x': x, 'Wq': Wq, 'bq': jnp.zeros((D,), jnp.float32), 'Wk': Wk, 'bk': jnp.zeros((D,), jnp.float32), 'Wv': Wv, 'bv': jnp.zeros((D * H,), jnp.float32), 'gamma': jnp.ones((D,), jnp.float32), 'beta': jnp.zeros((D,), jnp.float32)}
    _L1_attn_in = _L1_attn_setup()

    def _L1_ffn_setup():
        import jax, jax.numpy as jnp
        import numpy as np
        H = 128
        I = 256
        E = 32
        B, S = (4, 256)

        def _grouped_mm(a, w, group_sizes):
            return jax.lax.ragged_dot(a, w, group_sizes)

        def _swiglu(x, gw, uw, dw):
            return jax.nn.silu(x @ gw) * (x @ uw) @ dw
        key = jax.random.key(seed)
        ks = jax.random.split(key, 8)
        scale = 0.02
        inp = {'hidden_states': jax.random.normal(ks[0], (B, S, H), dtype=jnp.float32), 'gate_w': jax.random.normal(ks[1], (H, E), dtype=jnp.float32) * scale, 'shared_gate_w': jax.random.normal(ks[2], (H, I), dtype=jnp.float32) * scale, 'shared_up_w': jax.random.normal(ks[3], (H, I), dtype=jnp.float32) * scale, 'shared_down_w': jax.random.normal(ks[4], (I, H), dtype=jnp.float32) * scale, 'routed_gate_w': jax.random.normal(ks[5], (E, H, I), dtype=jnp.float32) * scale, 'routed_up_w': jax.random.normal(ks[6], (E, H, I), dtype=jnp.float32) * scale, 'routed_down_w': jax.random.normal(ks[7], (E, I, H), dtype=jnp.float32) * scale}
        return inp
    _L1_ffn_in = _L1_ffn_setup()
    _d = {'L0_attn_inputs': _L0_attn_in['inputs'], 'L0_attn_A': _L0_attn_in['A'], 'L0_attn_BC': _L0_attn_in['BC'], 'L0_ffn_wqkv': _L0_ffn_in['wqkv'], 'L0_ffn_q_scale': _L0_ffn_in['q_scale'], 'L0_ffn_k_scale': _L0_ffn_in['k_scale'], 'L0_ffn_wo': _L0_ffn_in['wo'], 'L0_ffn_ln_g': _L0_ffn_in['ln_g'], 'L0_ffn_ln_b': _L0_ffn_in['ln_b'], 'L0_ffn_w1': _L0_ffn_in['w1'], 'L0_ffn_b1': _L0_ffn_in['b1'], 'L0_ffn_w2': _L0_ffn_in['w2'], 'L0_ffn_b2': _L0_ffn_in['b2'], 'L1_attn_Wq': _L1_attn_in['Wq'], 'L1_attn_bq': _L1_attn_in['bq'], 'L1_attn_Wk': _L1_attn_in['Wk'], 'L1_attn_bk': _L1_attn_in['bk'], 'L1_attn_Wv': _L1_attn_in['Wv'], 'L1_attn_bv': _L1_attn_in['bv'], 'L1_attn_gamma': _L1_attn_in['gamma'], 'L1_attn_beta': _L1_attn_in['beta'], 'L1_ffn_gate_w': _L1_ffn_in['gate_w'], 'L1_ffn_shared_gate_w': _L1_ffn_in['shared_gate_w'], 'L1_ffn_shared_up_w': _L1_ffn_in['shared_up_w'], 'L1_ffn_shared_down_w': _L1_ffn_in['shared_down_w'], 'L1_ffn_routed_gate_w': _L1_ffn_in['routed_gate_w'], 'L1_ffn_routed_up_w': _L1_ffn_in['routed_up_w'], 'L1_ffn_routed_down_w': _L1_ffn_in['routed_down_w']}
    _x0 = _d['L0_attn_inputs']
    _d['L0_attn_inputs'] = jax.random.normal(jax.random.fold_in(jax.random.key(seed), 1), (4, 512, 128), dtype=_x0.dtype)
    del _x0
    return _d

def reference(L0_attn_inputs, L0_attn_A, L0_attn_BC, L0_ffn_wqkv, L0_ffn_q_scale, L0_ffn_k_scale, L0_ffn_wo, L0_ffn_ln_g, L0_ffn_ln_b, L0_ffn_w1, L0_ffn_b1, L0_ffn_w2, L0_ffn_b2, L1_attn_Wq, L1_attn_bq, L1_attn_Wk, L1_attn_bk, L1_attn_Wv, L1_attn_bv, L1_attn_gamma, L1_attn_beta, L1_ffn_gate_w, L1_ffn_shared_gate_w, L1_ffn_shared_up_w, L1_ffn_shared_down_w, L1_ffn_routed_gate_w, L1_ffn_routed_up_w, L1_ffn_routed_down_w):

    def _L0_attn_ref(inputs, A, BC):
        import jax, jax.numpy as jnp
        import numpy as np
        B, S, D, O = (8, 256, 128, 128)
        x_tfirst = jnp.swapaxes(inputs, 0, 1)

        def step(h, x_t):
            h = h * A + x_t
            return (h, h)
        h0 = jnp.zeros((inputs.shape[0], A.shape[0]), dtype=inputs.dtype)
        _, hs = jax.lax.scan(step, h0, x_tfirst)
        out = jnp.einsum('sbd,do->bso', hs, BC)
        return out

    def _L0_ffn_ref(x, wqkv, q_scale, k_scale, wo, ln_g, ln_b, w1, b1, w2, b2):
        import jax, jax.numpy as jnp
        import numpy as np
        DIM = 128
        DEPTH = 2
        HEADS = 8
        DIM_HEAD = 64
        WINDOW = 64
        INNER = HEADS * DIM_HEAD
        HID = int(DIM * 4 * 2 / 3)
        B, N = (2, 1024)
        QK_SCALE = 8.0

        def shift_token(t):
            t1, t2 = jnp.split(t, 2, axis=-1)
            t2 = jnp.pad(t2, ((0, 0), (1, 0), (0, 0)))[:, :-1]
            return jnp.concatenate([t1, t2], axis=-1)

        def l2norm(t):
            return t / jnp.clip(jnp.linalg.norm(t, axis=-1, keepdims=True), 1e-12)

        def rotate_half(x):
            x1, x2 = jnp.split(x, 2, axis=-1)
            return jnp.concatenate([-x2, x1], axis=-1)

        def rotary_xpos(q, k):
            n = q.shape[-2]
            half_idx = jnp.arange(0, DIM_HEAD, 2, dtype=jnp.float32)
            inv_freq = 1.0 / 10000.0 ** (half_idx / DIM_HEAD)
            t = jnp.arange(n, dtype=jnp.float32)
            freqs = t[:, None] * inv_freq[None, :]
            freqs = jnp.concatenate([freqs, freqs], axis=-1)
            base = (half_idx + 0.4 * DIM_HEAD) / (1.4 * DIM_HEAD)
            power = (t - n // 2) / float(WINDOW // 2)
            scale = base[None, :] ** power[:, None]
            scale = jnp.concatenate([scale, scale], axis=-1)
            cos, sin = (jnp.cos(freqs), jnp.sin(freqs))
            q = q * cos * scale + rotate_half(q) * sin * scale
            k = k * cos / scale + rotate_half(k) * sin / scale
            return (q, k)

        def local_attention(q, k, v):
            b, h, n, d = q.shape
            w = n // WINDOW
            bq = q.reshape(b, h, w, WINDOW, d) * QK_SCALE
            bk = k.reshape(b, h, w, WINDOW, d)
            bv = v.reshape(b, h, w, WINDOW, d)

            def look_around(t):
                p = jnp.pad(t, ((0, 0), (0, 0), (1, 0), (0, 0), (0, 0)))
                return jnp.concatenate([p[:, :, :w], p[:, :, 1:]], axis=3)
            bk, bv = (look_around(bk), look_around(bv))
            bt = jnp.arange(n).reshape(w, WINDOW)
            btp = jnp.pad(bt, ((1, 0), (0, 0)), constant_values=-1)
            btk = jnp.concatenate([btp[:w], btp[1:]], axis=1)
            sim = jnp.einsum('bhwid,bhwjd->bhwij', bq, bk)
            i = bt[:, :, None]
            j = btk[:, None, :]
            mask = (i < j) | (i > j + WINDOW) | (j == -1)
            sim = jnp.where(mask, -jnp.finfo(sim.dtype).max, sim)
            attn = jax.nn.softmax(sim, axis=-1)
            out = jnp.einsum('bhwij,bhwjd->bhwid', attn, bv)
            return out.reshape(b, h, n, d)

        def _layer(x, wqkv, qs, ksc, wo, lg, lb, w1, b1, w2, b2):
            b, n, _ = x.shape
            h = shift_token(x)
            qkv = h @ wqkv
            q, k, v = jnp.split(qkv, 3, axis=-1)
            to_heads = lambda t: t.reshape(b, n, HEADS, DIM_HEAD).transpose(0, 2, 1, 3)
            q, k, v = (to_heads(q), to_heads(k), to_heads(v))
            q = l2norm(q) * qs
            k = l2norm(k) * ksc
            q, k = rotary_xpos(q, k)
            o = local_attention(q, k, v)
            o = o.transpose(0, 2, 1, 3).reshape(b, n, INNER)
            x = x + o @ wo
            h = shift_token(x)
            mu = h.mean(-1, keepdims=True)
            var = h.var(-1, keepdims=True)
            h = (h - mu) / jnp.sqrt(var + 1e-05) * lg + lb
            h = h @ w1 + b1
            a, g = jnp.split(h, 2, axis=-1)
            h = a * jax.nn.gelu(g, approximate=False)
            x = x + h @ w2 + b2
            return x
        for l in range(DEPTH):
            x = _layer(x, wqkv[l], q_scale[l], k_scale[l], wo[l], ln_g[l], ln_b[l], w1[l], b1[l], w2[l], b2[l])
        return x

    def _L1_attn_ref(x, Wq, bq, Wk, bk, Wv, bv, gamma, beta):
        import jax, jax.numpy as jnp
        import numpy as np
        H = 8
        LN_EPS = 1e-05
        B, S, D = x.shape
        dk = D // H
        mu = jnp.mean(x, axis=-1, keepdims=True)
        var = jnp.mean(jnp.square(x - mu), axis=-1, keepdims=True)
        xn = (x - mu) * jax.lax.rsqrt(var + LN_EPS) * gamma + beta
        q = (xn @ Wq + bq).reshape(B, S, H, dk).transpose(0, 2, 1, 3)
        k = (xn @ Wk + bk).reshape(B, S, H, dk).transpose(0, 2, 1, 3)
        v = (xn @ Wv + bv).reshape(B, S, H, D).transpose(0, 2, 1, 3)
        scores = jnp.einsum('bhsd,bhtd->bhst', q, k) / jnp.sqrt(jnp.asarray(dk, x.dtype))
        p = jax.nn.softmax(scores, axis=-1)
        att = jnp.einsum('bhst,bhtd->bhsd', p, v)
        out = att.reshape(S, B, D, H).sum(axis=-1).reshape(B, S, D)
        return out

    def _L1_ffn_ref(hidden_states, gate_w, shared_gate_w, shared_up_w, shared_down_w, routed_gate_w, routed_up_w, routed_down_w):
        import jax, jax.numpy as jnp
        import numpy as np
        H = 128
        I = 256
        E = 32
        B, S = (4, 256)

        def _grouped_mm(a, w, group_sizes):
            return jax.lax.ragged_dot(a, w, group_sizes)

        def _swiglu(x, gw, uw, dw):
            return jax.nn.silu(x @ gw) * (x @ uw) @ dw
        b, s, h = hidden_states.shape
        x = hidden_states.reshape(-1, h)
        shared_out = _swiglu(x, shared_gate_w, shared_up_w, shared_down_w)
        logits = x @ gate_w
        topk_ids = jnp.argmax(logits, axis=-1)
        topk_val = jnp.max(logits, axis=-1)
        scores = jax.nn.sigmoid(topk_val)[:, None]
        xs = x * scores
        tokens_per_expert = jnp.zeros((E,), jnp.int32).at[topk_ids].add(1)
        order = jnp.argsort(topk_ids)
        sorted_x = xs[order]
        g = _grouped_mm(sorted_x, routed_gate_w, tokens_per_expert)
        u = _grouped_mm(sorted_x, routed_up_w, tokens_per_expert)
        d = _grouped_mm(jax.nn.silu(g) * u, routed_down_w, tokens_per_expert)
        inv = jnp.argsort(order)
        routed_out = d[inv]
        return (shared_out + routed_out).reshape(b, s, h)
    x = L0_attn_inputs
    x = x + _L0_attn_ref(_layernorm(x, axis=-1), L0_attn_A, L0_attn_BC)
    x = x + _L0_ffn_ref(_layernorm(x, axis=-1), L0_ffn_wqkv, L0_ffn_q_scale, L0_ffn_k_scale, L0_ffn_wo, L0_ffn_ln_g, L0_ffn_ln_b, L0_ffn_w1, L0_ffn_b1, L0_ffn_w2, L0_ffn_b2)
    x = x + _L1_attn_ref(_layernorm(x, axis=-1), L1_attn_Wq, L1_attn_bq, L1_attn_Wk, L1_attn_bk, L1_attn_Wv, L1_attn_bv, L1_attn_gamma, L1_attn_beta)
    x = x + _L1_ffn_ref(_layernorm(x, axis=-1), L1_ffn_gate_w, L1_ffn_shared_gate_w, L1_ffn_shared_up_w, L1_ffn_shared_down_w, L1_ffn_routed_gate_w, L1_ffn_routed_up_w, L1_ffn_routed_down_w)
    return x

_drawn_inputs = setup_inputs


def setup_inputs(seed=0):
    import zlib

    import numpy as np

    out = dict(_drawn_inputs(seed))
    spreads = {'L0_ffn_q_scale': (1.0, 0.6),
     'L0_ffn_k_scale': (1.0, 0.6),
     'L0_ffn_ln_g': (1.0, 0.6),
     'L0_ffn_ln_b': (0.0, 0.8),
     'L0_ffn_b1': (0.0, 0.8),
     'L0_ffn_b2': (0.0, 0.1),
     'L1_attn_bq': (0.0, 0.393),
     'L1_attn_bk': (0.0, 0.8),
     'L1_attn_bv': (0.0, 0.1),
     'L1_attn_gamma': (1.0, 0.2),
     'L1_attn_beta': (0.0, 0.1)}
    factors = {'L0_ffn_wqkv': 3.402,
     'L0_ffn_wo': 3.337,
     'L0_ffn_w1': 6.159,
     'L0_ffn_w2': 5.924,
     'L1_ffn_gate_w': 8.0,
     'L1_ffn_shared_gate_w': 8.0,
     'L1_ffn_shared_up_w': 8.0,
     'L1_ffn_shared_down_w': 8.0,
     'L1_ffn_routed_gate_w': 8.0,
     'L1_ffn_routed_up_w': 8.0,
     'L1_ffn_routed_down_w': 8.0}
    for name, (base, spread) in spreads.items():
        noise = np.random.default_rng([zlib.crc32(name.encode()), seed]).standard_normal(out[name].shape)
        drawn = base * np.exp(spread * noise) if base else spread * noise
        out[name] = jnp.asarray(drawn.astype(out[name].dtype))
    for name, factor in factors.items():
        out[name] = (out[name] * factor).astype(out[name].dtype)
    return out
```

```python
import concourse.bass as bass
from concourse import mybir
from contextlib import ExitStack

FP = mybir.dt.float32
BF = mybir.dt.bfloat16
I32 = mybir.dt.int32
U32 = mybir.dt.uint32
ALU = mybir.AluOpType
ACT = mybir.ActivationFunctionType
AX = mybir.AxisListType

P = 128
BATCH, SEQ = 4, 512
TOK = BATCH * SEQ
NT = SEQ // P
TILES = TOK // P
PAIRS = BATCH // 2
EPS = 1e-5
BANK = 512

LAYERS, HEADS, DH, WIN = 2, 8, 64, 64
INNER = HEADS * DH
HP = HEADS // 2
HID, HC = 341, 3
HW = -(-HID // HC)
VW = DH + 1

H1, DK = 8, 16
GRP = 8
VG = P // GRP
PARTS = 6
Q_PART = (0, 0, 0, 1, 1, 2)
K_PART = (0, 1, 2, 0, 1, 0)
KS = PARTS * DK
NSH = 3

EXP, INTER = 32, 256
IC = INTER // P
SLOT_TILES = TILES + EXP - 1
AHEAD = 4
LOOP_TILES = -(-SLOT_TILES // AHEAD) * AHEAD
PASSES = LOOP_TILES // AHEAD
UP, XT, BACK = 2, 3, 1
SLOT_ROWS = (LOOP_TILES + AHEAD) * P
NEG = -1e30


def after(it, per_pair, n):
    return it * per_pair + max(n, 0) + 1


COUNTED = {
    "DVE": ("ln_stats", "ln_mv", "ln_out", "scanned", "x1", "hT_hi", "ssq", "normed", "rot_a", "smax", "diffed", "o_rec",
            "o_norm", "y_att", "hs_top", "acted", "y_out"),
    "Pool": ("ln_eps", "ln_rstd", "ssq_c", "rnormed", "rot_bb", "rotated", "based_y", "based"),
    "ACT": ("hT_lo", "squared", "v_sb", "qkT_sb", "exped", "oT_sb", "hnT_sb", "gelued"),
    "PE": ("xnT_mm", "bc_mm", "yT_mm", "qk_mm", "v_mm", "qkT_mm", "s_mm", "pT_mm", "o_mm", "oT_mm", "wo_mm", "hnT_mm",
           "up_mm", "down_mm"),
}


def build(nc, A, out):
    with ExitStack() as ctx:
        def sb(name, shape, dt=FP):
            return ctx.enter_context(nc.sbuf_tensor(name, shape, dt))

        def sem(name):
            return ctx.enter_context(nc.semaphore(name))

        region_a = sb("region_a", [P, EXP * 2 * INTER])
        region_d = sb("region_d", [P, EXP * IC * P + 88])
        region_b = sb("region_b", [P, 10400])
        region_r = sb("region_r", [P, 2 * 4096])
        used = {}

        def part(region, width, dt=FP):
            at = used.get(region.name, 0)
            used[region.name] = at + width
            assert used[region.name] <= region.shape[1], (region.name, used[region.name])
            return region[:, at:at + width]

        KZW = WIN + SEQ
        kz = [part(region_a, HP * 2 * KZW).rearrange("p (h z t) -> p h z t", h=HP, z=2) for _ in range(2)]
        v_al = [part(region_a, NT * HEADS * VW).rearrange("p (t h d) -> p t h d", t=NT, h=HEADS) for _ in range(2)]
        qn = part(region_a, 2 * INNER)
        sq = part(region_a, 2 * INNER)
        hnT = part(region_a, SEQ)

        wqkv = [part(region_d, 3 * INNER) for _ in range(LAYERS)]
        wo = [part(region_d, 4 * P).rearrange("p (c n) -> p c n", c=4) for _ in range(LAYERS)]
        w1 = [part(region_d, 2 * HC * HW).rearrange("p (g c n) -> p g c n", g=2, c=HC) for _ in range(LAYERS)]
        w2 = [part(region_d, HC * P).rearrange("p (c n) -> p c n", c=HC) for _ in range(LAYERS)]
        tab_c, tab_s = (part(region_d, LAYERS * NT * 2 * DH).rearrange("p (l t z d) -> p l t z d", l=LAYERS, t=NT, z=2)
                        for _ in range(2))

        qT = [part(region_b, HP * SEQ).rearrange("p (h t) -> p h t", h=HP) for _ in range(2)]
        v_off = [part(region_b, NT * HEADS * VW).rearrange("p (t h d) -> p t h d", t=NT, h=HEADS) for _ in range(2)]
        sdiff = [part(region_b, HEADS * P).rearrange("p (h k) -> p h k", h=HEADS) for _ in range(2)]

        rot = [region_r[:, s * 4096:(s + 1) * 4096].rearrange("p (t n) -> p t n", t=NT) for s in range(2)]
        o_sb = [region_r[:, s * 4096:s * 4096 + 2048].rearrange("p (t n) -> p t n", t=NT) for s in range(2)]
        act = [region_r[0:HW, s * 4096 + 2048:s * 4096 + 3584].rearrange("p (c t) -> p c t", c=HC) for s in range(2)]
        hs = [region_r[:, s * 4096 + 3584:(s + 1) * 4096].rearrange("p (t n) -> p t n", t=NT) for s in range(2)]

        xr = sb("xr", [P, TILES, P])
        y = [sb(f"y{s}", [P, NT, P]) for s in range(2)]
        hT = [sb(f"hT{s}", [P, SEQ]) for s in range(2)]
        pts = [sb(f"pts{i}", [P, HEADS, P]) for i in range(2)]
        hT_scan = [pts[s][:, 0:4, :].rearrange("p h q -> p (h q)") for s in range(2)]
        rot_b = sb("rot_b", [P, 2 * INNER])
        oT = [sb(f"oT{i}", [P, 4, P]) for i in range(2)]
        ybase = rot_b[:, 0:SEQ].rearrange("p (t c) -> p t c", t=NT)
        gel = rot_b[0:HW, SEQ:2 * SEQ]
        ident = sb("ident", [P, P])
        ident_b = sb("ident_b", [P, P], BF)
        mask_b = sb("mask_b", [P, 2, 4, P], BF)
        a_col = sb("a_col", [P, 1])
        bc_w = sb("bc_w", [P, P])
        ln_gb = sb("ln_gb", [P, LAYERS, 2])
        b1 = sb("b1", [HW, LAYERS, 2, HC])
        b2 = sb("b2", [P, LAYERS, P])
        stats = sb("stats", [P, NT, 6])
        mv = sb("mv", [P, NT, 2])
        rstd = sb("rstd", [P, NT])
        ssum = sb("ssum", [P, 2 * HEADS])
        ssum_c = sb("ssum_c", [P, 2 * HEADS])
        var_eps = sb("var_eps", [P, NT])
        eps = sb("eps", [P, NT])
        neg_half = sb("neg_half", [P, 2 * HEADS])
        rnorm = sb("rnorm", [P, 2 * HEADS])
        smx = [sb(f"smx{i}", [P, HEADS]) for i in range(2)]
        orec = [sb(f"orec{i}", [P, 2, 4]) for i in range(2)]

        def stack(region, at):
            return region[:, at:at + H1 * SEQ // 2].bitcast(BF).rearrange("p (h t) -> p h t", h=H1)

        half_st = H1 * SEQ // 2
        qst = [stack(region_b, 0), stack(region_b, half_st), stack(region_r, 0)]
        kst = [stack(region_b, 2 * half_st), stack(region_b, 3 * half_st), stack(region_r, half_st)]
        pt = [region_r[:, 4096 + i * 2048:4096 + (i + 1) * 2048].rearrange("p (h t) -> p h t", h=4) for i in range(2)]
        qk_parts = [region_b[:, 4 * half_st + i * 768:4 * half_st + (i + 1) * 768].bitcast(BF)
                    .rearrange("p (r t) -> p r t", r=3) for i in range(2)]
        wq, wk, wvg = (region_b[:, 4 * half_st + 1536 + i * P:4 * half_st + 1536 + (i + 1) * P] for i in range(3))
        z1, xn1 = y[0], hT[0]
        qk_f = [pts[0][:, i * 4:(i + 1) * 4, :].rearrange("p h q -> p (h q)") for i in range(2)]
        v1 = [pts[1][:, :, :].rearrange("p h q -> p (h q)").rearrange("p (t h g) -> p t h g", t=NT, h=H1),
              rot_b[:, :].rearrange("p (t h g) -> p t h g", t=NT, h=H1)]
        at_sb = [oT[i][:, :, :].rearrange("p c t -> p (c t)") for i in range(2)]
        att = y[1]
        wv_raw = pts[0][:, :, :].rearrange("p h q -> p (h q)")
        bv_raw = rot_b[:, :]
        ones_f = sb("ones_f", [P, EXP])
        sel = sb("sel", [P, 2, 2 * (VG + 1)])
        bvg = hT[1][:, 384:512]
        gb1 = sb("gb1", [P, 2])
        bqk = sb("bqk", [P, 2])
        mneg = [sb(f"mneg{i}", [P, H1 * NT]) for i in range(2)]
        shift_r = hT[1][0:H1 * NT, 0:P]
        shift_p = hT[1][0:H1 * NT, P:P + NSH * P // 2].bitcast(BF).rearrange("p (r t) -> p r t", r=NSH)
        arec = sb("arec", [P, 2, 16])
        parts_dram = nc.dram_tensor("parts_dram", (2, 3, P, SEQ), BF).ap()

        wgu = region_a[:, :].rearrange("p (e n) -> p e n", e=EXP)
        wd = region_d[:, 0:EXP * IC * P].rearrange("p (e c n) -> p e c n", e=EXP, c=IC)
        h_m = region_b[:, 0:2048].rearrange("p (t c) -> p t c", t=TILES)
        hT_m = region_b[:, 2048:4096]
        sg, su = region_b[:, 4096:4352], region_b[:, 4352:4608]
        sd = region_b[:, 4608:4864].rearrange("p (c n) -> p c n", c=IC)
        gate_w = region_b[:, 4864:4896]
        consts = region_b[:, 4896:5024]
        tri_f = region_b[:, 5024:5152]
        tri = region_b[:, 5152:5216].bitcast(BF)
        ones_b = region_b[:, 5216:5280].bitcast(BF)
        hot = region_b[:, 5280:5536].bitcast(BF).rearrange("p (t e) -> p t e", t=TILES)
        silu_s = [region_b[:, 5536 + i * 512:6048 + i * 512] for i in range(2)]
        act_s = [region_b[:, 6560 + i * 1024:7584 + i * 1024].rearrange("p (c t) -> p c t", c=IC) for i in range(2)]
        y_g = region_r[:, 0:2048].rearrange("p (t c) -> p t c", t=TILES)
        m1, m2 = region_r[:, 2048:2560], region_r[:, 2560:3072]
        m3 = region_r[0:1, 3072:3072 + (LOOP_TILES + AHEAD) * EXP]
        xs_in_sb = [region_r[:, 5120 + i * P:5120 + (i + 1) * P] for i in range(AHEAD)]
        xsT = [region_r[:, 5632 + i * P:5632 + (i + 1) * P] for i in range(2)]
        silu_r = [region_r[:, 5888 + i * INTER:5888 + (i + 1) * INTER] for i in range(2)]
        act_r = [region_r[:, 6400 + i * INTER:6400 + (i + 1) * INTER] for i in range(2)]
        actT = [region_r[:, 6912 + i * INTER:6912 + (i + 1) * INTER] for i in range(2)]
        ys = [region_r[:, 7424 + i * P:7424 + (i + 1) * P] for i in range(AHEAD)]
        zeros = region_r[:, 4096:4096 + SLOT_ROWS // 2]
        rmax, rev2, esc, score, slot_f = (region_b[:, 8608 + i * TILES:8608 + (i + 1) * TILES] for i in range(5))
        slot_i = region_b[:, 8688:8704].bitcast(U32)
        ntile, incl, base_e = (region_b[:, 8704 + i * EXP:8704 + (i + 1) * EXP] for i in range(3))
        exp_of_f = region_b[0:1, 8800:8800 + LOOP_TILES + AHEAD]
        exp_of = region_b[0:1, 8864:8864 + LOOP_TILES + AHEAD].bitcast(I32)
        xs_dram = nc.dram_tensor("xs_dram", (SLOT_ROWS, P), FP).ap()
        ys_dram = nc.dram_tensor("ys_dram", (LOOP_TILES * P, P), FP).ap()

        base_c = region_r[:, 0:NT * 2 * DH].rearrange("p (t z d) -> p t z d", t=NT, z=2)
        base_s = region_r[:, 512:1024].rearrange("p (t z d) -> p t z d", t=NT, z=2)
        scales = region_r[:, 1024:1024 + LAYERS * 4 * DH].rearrange("p (l c z d) -> p l c z d", l=LAYERS, c=2, z=2)
        mask_f = region_r[:, 2048:2048 + 2 * P].rearrange("p (m k) -> p m k", m=2)

        ps = ctx.enter_context(nc.psum_tensor("ps", [P, 8 * BANK], FP))

        def bank(n, width=BANK, of=1):
            return ps[:, n * BANK:n * BANK + width * of]

        S = {n: sem(n) for n in (
            "x_in", "small_in", "w_in", "tabs", "idn", "zero_p", "masks",
            "ln_turn", "norm_turn", "v_turn", "ln_stats", "ln_mv", "ln_eps", "ln_rstd", "ln_out",
            "xnT_mm", "scanned", "bc_mm", "x1", "y_in", "yT_mm", "hT_lo", "hT_hi",
            "qk_mm", "v_mm", "squared", "ssq", "ssq_c", "rnormed", "normed", "rot_a", "rot_bb", "rotated",
            "v_sb", "qkT_mm", "qkT_sb", "s_mm", "smax", "diffed", "pT_mm", "exped", "o_mm",
            "o_rec", "o_norm", "oT_mm", "oT_sb", "wo_mm", "y_att", "hs_top", "based_y", "based", "hnT_mm", "hnT_sb",
            "up_mm", "gelued", "acted", "down_mm", "y_out", "stored")}
        v_off_in = [sem(f"v_off_in{s}") for s in range(2)]
        hs_in = [sem(f"hs_in{s}") for s in range(2)]
        T = {n: sem("l1_" + n) for n in (
            "w_in", "wv", "zero", "ones", "xn_mm", "xn_sb", "qk_mm", "qk_sb", "v_mm", "v_sb", "part", "parts", "stored",
            "d_mm", "mx", "ms_mm", "ms_part", "ms_sb", "f_mm", "ex", "pv", "at_sb", "sel_mm", "rec", "att", "x3")}
        st_in = [sem(f"l1_st_in{i}") for i in range(3)]
        sh_in = [sem(f"l1_sh_in{i}") for i in range(3)]
        M = {n: sem("moe_" + n) for n in (
            "zeros", "zeroed", "w_gu", "w_d", "w_in", "tri", "hT_mm", "hT_sb", "logits", "step", "rmax", "esc", "hot",
            "rank_mm", "slots", "scaled", "up_mm", "silu", "acted", "down_mm", "x4s", "scattered",
            "sp_turn", "xT_mm", "xT_sb", "gu_mm", "r_silu", "r_act", "actT_mm", "actT_sb", "y_mm", "y_sb", "x4")}
        xs_in = [sem(f"moe_xs_in{i}") for i in range(AHEAD)]
        gathered = [sem(f"moe_gathered{i}") for i in range(BATCH)]
        ys_out = [sem(f"moe_ys_out{i}") for i in range(AHEAD)]
        block = ctx.enter_context(nc.Block())

        def experts(engine, step):
            with engine.Fori(0, PASSES - 1) as i:
                for r in range(AHEAD):
                    step(i, r, False)
            for r in range(AHEAD):
                step(PASSES - 1, r, True)

        def l1_steps():
            for b in range(2):
                yield "pre", b, 0
                yield "qk", b, 0
                yield "val", b, 0
            for i in range(16):
                yield "max", 0, i
            yield "shift", 0, 0
            for b in range(BATCH):
                for i in range(16):
                    yield "probs", b, i
                    if b + 1 < BATCH:
                        yield "max", b + 1, i
                    if b + 2 < BATCH and i == 4:
                        yield "pre", b + 2, 0
                    if b + 2 < BATCH and i == 8:
                        yield "qk", b + 2, 0
                if b + 1 < BATCH:
                    yield "shift", b + 1, 0
                yield "end", b, 0
                if b + 2 < BATCH:
                    yield "val", b + 2, 0

        l1_bank, turn = {}, 0
        for what, b, i in l1_steps():
            if what != "end":
                l1_bank[what, b, i] = 2 * (turn % 3)
                turn += 1

        def unit(l, s):
            return 2 * l + s

        def ut(l, s, t):
            return 4 * unit(l, s) + t

        NU, NUT = 2 * LAYERS, 4 * 2 * LAYERS
        ln_front = lambda k, s: 2 * k + s
        ln_ffn = lambda l, s: 4 + 2 * l + s
        NLN = 8

        def z_pad(v):
            return v[:, :, :, :].rearrange("p t h g -> p (t h g)")

        def xr_tiles(it, s):
            return xr[:, bass.ds(it * (2 * NT) + s * NT, NT), :]

        @block.sync
        def _(sp):
            sp.dma_start(xr[:, :, :], A["x"].rearrange("(t p) c -> p t c", p=P)).then_inc(S["x_in"], 16)
            loads = [(a_col[:, :], A["a"]), (bc_w[:, :], A["bc"]), (base_c, A["tab_c"]), (base_s, A["tab_s"]),
                     (mask_f, A["mask"]), (ln_gb[:, :, :], A["ln_gb"]), (b1[:, :, :, :], A["b1"])]
            for dst, src in loads:
                sp.dma_start(dst, src).then_inc(S["small_in"], 16)
            sp.dma_start(scales, A["scales"].partition_broadcast(P)).then_inc(S["small_in"], 16)
            sp.dma_start(b2[:, :, :], A["b2"].partition_broadcast(P)).then_inc(S["small_in"], 16)
            for l in range(LAYERS):
                sp.dma_start(wqkv[l], A["wqkv"][l, :, :]).then_inc(S["w_in"], 16)
                sp.dma_start(wo[l], A["wo"][l, :, :].rearrange("(c p) n -> p c n", p=P)).then_inc(S["w_in"], 16)
                sp.dma_start(w1[l], A["w1"][l, :, :, :, :]).then_inc(S["w_in"], 16)
                sp.dma_start(w2[l][0:HW], A["w2"][l, :, :, :].rearrange("c p n -> p c n")).then_inc(S["w_in"], 16)
            sp.wait_ge(M["zeros"], 1)
            half = SLOT_ROWS // 2
            for i in range(2):
                sp.dma_start(xs_dram[i * half:(i + 1) * half, :].rearrange("(p r) c -> p (r c)", p=P), zeros)\
                  .then_inc(M["zeroed"], 16)
            with sp.Fori(0, PAIRS) as it:
                for l in range(LAYERS):
                    for s in range(2):
                        sp.wait_ge(S["v_sb"], after(it, NUT, ut(l, s, 3) + 1))
                        sp.sem_inc(S["v_turn"], 1)
                        sp.wait_ge(S["o_mm"], after(it, NUT, ut(l, s, 3) + 1 - 2 * NT))
                        sp.dma_start(v_off[s][0:WIN, 1:NT], v_al[s][WIN:P, 0:NT - 1]).then_inc(v_off_in[s], 16)
                        sp.dma_start(v_off[s][WIN:P, :], v_al[s][0:WIN, :]).then_inc(v_off_in[s], 16)
                    for s in range(2):
                        sp.wait_ge(S["y_att"], after(it, NU, unit(l, s) + 1))
                        h = P // 2
                        sp.dma_start(hs[s][1:P, :, h:P], y[s][0:P - 1, :, h:P]).then_inc(hs_in[s], 16)
                        sp.dma_start(hs[s][0:1, 1:NT, h:P], y[s][P - 1:P, 0:NT - 1, h:P]).then_inc(hs_in[s], 16)
            sp.wait_ge(S["y_out"], after(PAIRS, NU, 0))
            sp.dma_start(wv_raw, A["wv"]).then_inc(T["w_in"], 16)
            sp.dma_start(bv_raw, A["bv"].partition_broadcast(P)).then_inc(T["w_in"], 16)
            for dst, src in ((wq, A["wq"]), (wk, A["wk"]), (gb1[:, :], A["gb1"]), (bqk[:, :], A["bqk"]),
                             (sel[:, :, :], A["sel"])):
                sp.dma_start(dst, src).then_inc(T["w_in"], 16)
            chunk = 0
            for what, b, i in l1_steps():
                k = b % 3
                if what == "probs" and i % 3 == 1 and chunk < 20:
                    sp.wait_ge(T["ex"], 16 * b + i)
                    if chunk < 16:
                        e0 = 2 * chunk
                        sp.dma_start(wgu[:, e0:e0 + 2, :], A["wgu"][:, e0:e0 + 2, :]).then_inc(M["w_gu"], 16)
                    else:
                        e0 = 8 * (chunk - 16)
                        sp.dma_start(wd[:, e0:e0 + 8, :, :], A["wd"][:, e0:e0 + 8, :, :]).then_inc(M["w_d"], 16)
                    chunk += 1
                if what == "qk":
                    sp.wait_ge(T["parts"], 2 * (b + 1))
                    for z in range(2):
                        sp.dma_start(parts_dram[z, :, :, :].rearrange("r p t -> p r t"), qk_parts[z]).then_inc(T["stored"], 16)
                    sp.wait_ge(T["stored"], 32 * (b + 1))
                    if b >= 3:
                        sp.wait_ge(T["f_mm"], 16 * (b - 2))
                    for z, (st, which) in enumerate(((qst, Q_PART), (kst, K_PART))):
                        for g in range(PARTS):
                            sp.dma_start(st[k][g * DK:(g + 1) * DK, :, :],
                                         parts_dram[z, which[g], :, :].rearrange("(h d) t -> d h t", h=H1))\
                              .then_inc(st_in[k], 16)
                    sp.wait_ge(st_in[k], 16 * 2 * PARTS * (b // 3 + 1))
                if what == "shift":
                    sp.wait_ge(T["ms_sb"], b + 1)
                    for j in range(NSH):
                        sp.dma_start(qst[k][KS + j:KS + j + 1, :, :].rearrange("p h (q t) -> p (h q) t", q=NT),
                                     shift_p[:, j, :]).then_inc(sh_in[k], 16)
            sp.wait_ge(T["x3"], BATCH)
            sp.wait_ge(T["pv"], 8 * BATCH)
            for dst, src in ((sg, A["sg"]), (su, A["su"]), (sd, A["sd"].rearrange("(c p) n -> p c n", p=P)),
                             (gate_w, A["gate"]), (consts, A["consts"]), (tri_f, A["tri"])):
                sp.dma_start(dst, src).then_inc(M["w_in"], 16)
            sp.wait_ge(M["scattered"], 16 * TILES)
            for r in range(AHEAD):
                sp.dma_start(xs_in_sb[r], xs_dram[r * P:(r + 1) * P, :]).then_inc(xs_in[r], 16)
            for r in range(AHEAD):
                sp.sem_inc(ys_out[r], 16)
            for t in range(XT):
                sp.wait_ge(M["xT_mm"], t + 1)
                sp.dma_start(xs_in_sb[t], xs_dram[(t + AHEAD) * P:(t + AHEAD + 1) * P, :]).then_inc(xs_in[t], 16)

            def sp_step(i, r, last):
                row = (i * AHEAD + r) * P
                if not last:
                    sp.wait_ge(M["xT_mm"], i * AHEAD + r + XT + 1)
                    sp.sem_inc(M["sp_turn"], 1)
                    t = (r + XT) % AHEAD
                    sp.dma_start(xs_in_sb[t], xs_dram[bass.ds(row + (XT + AHEAD) * P, P), :]).then_inc(xs_in[t], 16)
                sp.wait_ge(M["y_sb"], i * AHEAD + r + 3)
                sp.sem_inc(M["sp_turn"], 1)
                sp.dma_start(ys_dram[bass.ds(row, P), :], ys[r]).then_inc(ys_out[r], 16)

            experts(sp, sp_step)
            for b in range(BATCH):
                sp.wait_ge(M["x4"], b + 1)
                rows = out[b * SEQ:(b + 1) * SEQ, :].rearrange("(t p) c -> p t c", p=P)
                sp.dma_start(rows, xr[:, b * NT:(b + 1) * NT, :]).then_inc(S["stored"], 16)
            for r in range(AHEAD):
                sp.wait_ge(xs_in[r], 16 * (PASSES + (r < XT)))
            sp.wait_ge(S["stored"], 16 * BATCH)

        @block.gpsimd
        def _(pool):
            g = nc.gpsimd
            for name in COUNTED["Pool"]:
                pool.sem_inc(S[name], 1)
            g.memset(zeros, 0.0).then_inc(M["zeros"], 1)
            g.memset(ident[:, :], 0.0).then_inc(S["idn"], 1)
            pool.wait_ge(S["idn"], 1)
            g.affine_select(out=ident[:, :], in_=ident[:, :], compare_op=ALU.not_equal, fill=1.0,
                            base=0, pattern=[[-1, P]], channel_multiplier=1).then_inc(S["idn"], 1)
            g.memset(eps[:, :], EPS)
            g.memset(neg_half[:, :], -0.5).then_inc(S["idn"], 1)
            pool.wait_ge(S["idn"], 3)
            for s in range(2):
                g.memset(kz[s].rearrange("p h z t -> p (h z t)"), 0.0).then_inc(S["zero_p"], 1)
                g.memset(v_off[s].rearrange("p t h d -> p (t h d)"), 0.0).then_inc(S["zero_p"], 1)
                g.memset(v_al[s][:, :, :, DH:VW], 1.0).then_inc(S["zero_p"], 1)
            with pool.Fori(0, PAIRS) as it:
                def power(n):
                    pool.wait_ge(S["ln_mv"], after(it, NLN, n + 1))
                    g.tensor_tensor(var_eps[:, 0:NT], mv[:, :, 1], eps[:, 0:NT], ALU.add).then_inc(S["ln_eps"], 1)
                    pool.wait_ge(S["ln_eps"], after(it, NLN, n + 1))
                    g.tensor_tensor(rstd[:, :], var_eps[:, 0:NT], neg_half[:, 0:NT], ALU.pow)\
                     .then_inc(S["ln_rstd"], 1)

                for k in range(2):
                    for s in range(2):
                        power(ln_front(k, s))
                for l in range(LAYERS):
                    for s in range(2):
                        for t in range(NT):
                            n = ut(l, s, t)
                            pool.wait_ge(S["ssq"], after(it, NUT, n + 1))
                            pool.sem_inc(S["norm_turn"], 1)
                            g.tensor_scalar(ssum_c[:, :], ssum[:, :], 1e-24, None, ALU.max).then_inc(S["ssq_c"], 1)
                            pool.wait_ge(S["ssq_c"], after(it, NUT, n + 1))
                            g.tensor_tensor(rnorm[:, :], ssum_c[:, :], neg_half[:, :], ALU.pow)\
                             .then_inc(S["rnormed"], 1)
                            pool.wait_ge(S["normed"], after(it, NUT, n + 1))
                            for half in range(2):
                                src = qn.rearrange("p (z h j d) -> p z h j d", z=2, h=HEADS, j=2)[:, :, :, 1 - half, :]
                                dst = rot_b[:, :].rearrange("p (z h j d) -> p z h j d", z=2, h=HEADS, j=2)[:, :, :, half, :]
                                tab = tab_s[:, l, t, :, half * 32:half * 32 + 32].unsqueeze(2)\
                                    .to_broadcast([P, 2, HEADS, 32])
                                g.tensor_tensor(dst, src, tab, ALU.mult).then_inc(S["rot_bb"], 1)
                            pool.wait_ge(S["rot_a"], after(it, NUT, n + 1))
                            pool.wait_ge(S["rot_bb"], after(it, 2 * NUT, 2 * n + 2))
                            g.tensor_tensor(rot[s][:, t, :], rot[s][:, t, :], rot_b[:, :], ALU.add)\
                             .then_inc(S["rotated"], 1)
                    for s in range(2):
                        power(ln_ffn(l, s))
                        pool.wait_ge(S["y_out"], after(it, NU, unit(l, s)))
                        pool.wait_ge(S["y_att"], after(it, NU, unit(l, s) + 1))
                        bb = b2[:, l, :].unsqueeze(1).to_broadcast([P, NT, P])
                        last = g.tensor_tensor(ybase[:, :, :], y[s][:, :, :], bb, ALU.add)
                        if l == LAYERS - 1:
                            last.then_inc(S["based_y"], 1)
                            pool.wait_ge(S["based_y"], after(it, 2, s + 1))
                            last = g.tensor_tensor(ybase[:, :, :], ybase[:, :, :], xr_tiles(it, s), ALU.add)
                        last.then_inc(S["based"], 1)

            pool.wait_ge(S["y_out"], after(PAIRS, NU, 0))
            for k in range(3):
                g.memset(kst[k][KS:KS + NSH, :, :], 1.0).then_inc(T["ones"], 1)
                pool.wait_ge(T["ones"], k + 1)
            g.memset(z_pad(v1[0]), 0.0).then_inc(T["zero"], 1)
            pool.wait_ge(T["wv"], 1)
            g.memset(z_pad(v1[1]), 0.0).then_inc(T["zero"], 1)
            pool.wait_ge(T["zero"], 2)
            for i in range(2):
                g.memset(v1[i][:, :, :, VG:VG + 1], 1.0).then_inc(T["zero"], 1)
            for what, b, i in l1_steps():
                if what == "pre":
                    for r in range(2):
                        n = 2 * b + r
                        pool.wait_ge(S["ln_mv"], after(PAIRS, NLN, n + 1))
                        g.tensor_tensor(var_eps[:, 0:NT], mv[:, :, 1], eps[:, 0:NT], ALU.add).then_inc(S["ln_eps"], 1)
                        pool.wait_ge(S["ln_eps"], after(PAIRS, NLN, n + 1))
                        g.tensor_tensor(rstd[:, :], var_eps[:, 0:NT], neg_half[:, 0:NT], ALU.pow)\
                         .then_inc(S["ln_rstd"], 1)
                if what == "qk":
                    pool.wait_ge(T["qk_sb"], b + 1)
                    if b:
                        pool.wait_ge(T["stored"], 32 * b)
                    for z in range(2):
                        f, p3 = qk_f[z], qk_parts[z]
                        g.tensor_copy(p3[:, 0, :], f).then_inc(T["part"], 1)
                    pool.wait_ge(T["part"], 6 * b + 2)
                    for z in range(2):
                        f, p3 = qk_f[z], qk_parts[z]
                        g.tensor_tensor(f, f, p3[:, 0, :], ALU.subtract).then_inc(T["part"], 1)
                    pool.wait_ge(T["part"], 6 * b + 4)
                    for z in range(2):
                        f, p3 = qk_f[z], qk_parts[z]
                        g.tensor_copy(p3[:, 1, :], f).then_inc(T["part"], 1)
                    pool.wait_ge(T["part"], 6 * b + 6)
                    for z in range(2):
                        f, p3 = qk_f[z], qk_parts[z]
                        g.tensor_tensor(p3[:, 2, :], f, p3[:, 1, :], ALU.subtract).then_inc(T["parts"], 1)

            for b in range(BATCH):
                n = 2 * BATCH + b
                pool.wait_ge(S["ln_mv"], after(PAIRS, NLN, n + 1))
                g.tensor_tensor(var_eps[:, 0:NT], mv[:, :, 1], eps[:, 0:NT], ALU.add).then_inc(S["ln_eps"], 1)
                pool.wait_ge(S["ln_eps"], after(PAIRS, NLN, n + 1))
                g.tensor_tensor(rstd[:, :], var_eps[:, 0:NT], neg_half[:, 0:NT], ALU.pow).then_inc(S["ln_rstd"], 1)
            pool.wait_ge(M["slots"], 1)
            pool.wait_ge(M["scaled"], 1)
            pool.wait_ge(M["zeroed"], 32)
            for t in range(TILES):
                g.indirect_dma_start(out=xs_dram[:, :], out_offset=bass.IndirectOffsetOnAxis(ap=slot_i[:, t:t + 1], axis=0),
                                     in_=h_m[:, t, :], in_offset=None).then_inc(M["scattered"], 16)
            for r in range(AHEAD):
                pool.wait_ge(ys_out[r], 16 * (PASSES + 1))
            for t in range(TILES):
                g.indirect_dma_start(out=y_g[:, t, :], out_offset=None, in_=ys_dram[:, :],
                                     in_offset=bass.IndirectOffsetOnAxis(ap=slot_i[:, t:t + 1], axis=0))\
                 .then_inc(gathered[t // NT], 16)

        @block.scalar
        def _(a):
            act_ = nc.scalar.activation
            for name in COUNTED["ACT"]:
                a.sem_inc(S[name], 1)
            a.wait_ge(S["small_in"], 9 * 16)
            with a.Fori(0, PAIRS) as it:
                for l in range(LAYERS):
                    for s in range(2):
                        a.wait_ge(S["yT_mm"], after(it, NU, unit(l, s) + 1))
                        act_(hT[s][0:64, :], ps[0:64, (6 + s) * BANK:(7 + s) * BANK], ACT.Copy).then_inc(S["hT_lo"], 1)
                        for t in range(NT):
                            n = ut(l, s, t)
                            a.wait_ge(S["qk_mm"], after(it, NUT, n + 1))
                            a.wait_ge(S["ssq"], after(it, NUT, n))
                            act_(sq, bank((n % 2) * 2, of=2), ACT.Square).then_inc(S["squared"], 1)
                            a.wait_ge(S["v_mm"], after(it, NUT, n + 1))
                            act_(v_al[s][:, t, :, 0:DH], bank(4 + n % 2).rearrange("p (h d) -> p h d", h=HEADS),
                                 ACT.Copy).then_inc(S["v_sb"], 1)
                    for s in range(2):
                        for t in range(NT):
                            a.wait_ge(S["qkT_mm"], after(it, NUT, ut(l, s, t) + 1))
                            b0 = 6 if t % 2 == 0 else 4
                            cols = slice(t * P, (t + 1) * P)
                            kcols = slice(WIN + t * P, WIN + (t + 1) * P)
                            act_(qT[s][:, :, cols], bank(b0).rearrange("p (h t) -> p h t", h=HP), ACT.Copy)
                            kp = bank(b0 + 1).rearrange("p (h t) -> p h t", h=HP)
                            act_(kz[s][0:64, :, 0, kcols], kp[0:64], ACT.Copy)
                            act_(kz[s][64:P, :, 1, kcols], kp[64:P], ACT.Copy).then_inc(S["qkT_sb"], 1)
                        for t in range(NT):
                            n = ut(l, s, t)
                            a.wait_ge(S["pT_mm"], after(it, NUT, n + 1))
                            a.wait_ge(S["o_mm"], after(it, NUT, n - 1))
                            act_(pts[n % 2].rearrange("p h q -> p (h q)"), bank(4, of=2), ACT.Exp).then_inc(S["exped"], 1)
                    for s in range(2):
                        for t in range(NT):
                            n = ut(l, s, t)
                            a.wait_ge(S["oT_mm"], after(it, NUT, n + 1))
                            act_(oT[n % 2].rearrange("p c t -> p (c t)"), bank(n % 2), ACT.Copy).then_inc(S["oT_sb"], 1)
                    for s in range(2):
                        a.wait_ge(S["hnT_mm"], after(it, NU, unit(l, s) + 1))
                        act_(hnT, bank(6 + s), ACT.Identity, scale=ln_gb[:, l, 0:1],
                             bias=ln_gb[:, l, 1:2]).then_inc(S["hnT_sb"], 1)
                        for c in range(HC):
                            n = HC * unit(l, s) + c
                            m = HC * s + c
                            a.wait_ge(S["up_mm"], after(it, HC * NU, n + 1))
                            a.wait_ge(S["acted"], after(it, HC * NU, n))
                            act_(gel[:, :], ps[0:HW, ((5, 1)[m % 2]) * BANK:((5, 1)[m % 2] + 1) * BANK], ACT.Gelu,
                                 bias=b1[:, l, 1, c:c + 1]).then_inc(S["gelued"], 1)

            a.wait_ge(T["w_in"], 7 * 16)
            for what, b, i in l1_steps():
                if what == "pre":
                    a.wait_ge(T["xn_mm"], b + 1)
                    if b:
                        a.wait_ge(T["v_mm"], b)
                    act_(xn1[:, :], bank(l1_bank[what, b, i]), ACT.Identity, scale=gb1[:, 0:1], bias=gb1[:, 1:2])\
                        .then_inc(T["xn_sb"], 1)
                if what == "qk":
                    a.wait_ge(T["qk_mm"], b + 1)
                    a.wait_ge(T["wv"], 2)
                    if b:
                        a.wait_ge(T["parts"], 2 * b)
                    act_(qk_f[0], bank(l1_bank[what, b, i]), ACT.Identity, scale=DK ** -0.5, bias=bqk[:, 0:1])
                    act_(qk_f[1], bank(l1_bank[what, b, i] + 1), ACT.Identity, bias=bqk[:, 1:2]).then_inc(T["qk_sb"], 1)
                if what == "probs":
                    a.wait_ge(T["f_mm"], 16 * b + i + 1)
                    if 8 * b + i // 2 - 1 > 0:
                        a.wait_ge(T["pv"], 8 * b + i // 2 - 1)
                    dst = pt[(i // 2) % 2][:, (i % 2) * 2:(i % 2) * 2 + 2, :].rearrange("p h t -> p (h t)")
                    act_(dst, bank(l1_bank[what, b, i], of=2), ACT.Exp).then_inc(T["ex"], 1)
                if (what, i) == ("probs", 10) or what == "end":
                    hg = int(what == "end")
                    a.wait_ge(T["pv"], 8 * b + 4 * (hg + 1))
                    if b:
                        a.wait_ge(T["sel_mm"], b)
                    act_(at_sb[hg], bank(6 + hg), ACT.Copy).then_inc(T["at_sb"], 1)

            for b in range(BATCH):
                a.wait_ge(M["hT_mm"], b + 1)
                act_(hT_m[:, b * SEQ:(b + 1) * SEQ], bank(b % 2), ACT.Copy).then_inc(M["hT_sb"], 1)
            a.wait_ge(M["rmax"], 1)
            act_(esc, rmax, ACT.Exp, scale=-1.0).then_inc(M["esc"], 1)
            for n in range(BATCH * IC):
                a.wait_ge(M["up_mm"], n + 1)
                if n >= 2:
                    a.wait_ge(M["acted"], n - 1)
                act_(silu_s[n % 2], bank(2 + 2 * (n % 2)), ACT.Silu).then_inc(M["silu"], 1)

            def tokens_sb(t, j):
                a.wait_ge(M["xT_mm"], j + 1)
                if not (isinstance(j, int) and j < 2):
                    a.wait_ge(M["gu_mm"], j - 1)
                act_(xsT[t % 2], bank(t % 2)[:, 0:P], ACT.Copy).then_inc(M["xT_sb"], 1)

            def gate_sb(t, j):
                a.wait_ge(M["gu_mm"], j + 1)
                if not (isinstance(j, int) and j < 2):
                    a.wait_ge(M["r_act"], j - 1)
                act_(silu_r[t % 2], bank(2 + t % 2)[:, 0:INTER], ACT.Silu).then_inc(M["r_silu"], 1)

            def back_sb(t, j):
                a.wait_ge(M["actT_mm"], j + 1)
                if not (isinstance(j, int) and j < 2):
                    a.wait_ge(M["y_mm"], j - 1)
                act_(actT[t % 2], bank(4 + t % 2)[:, 0:INTER], ACT.Copy).then_inc(M["actT_sb"], 1)

            def act_step(i, r, last):
                for lag, do in ((XT, tokens_sb), (UP, gate_sb), (BACK, back_sb)):
                    if not last or r + lag < AHEAD:
                        do(r + lag, i * AHEAD + r + lag)

            for t in range(XT):
                tokens_sb(t, t)
            for t in range(UP):
                gate_sb(t, t)
            back_sb(0, 0)
            experts(a, act_step)

        @block.vector
        def _(v):
            d = nc.vector
            for name in COUNTED["DVE"]:
                v.sem_inc(S[name], 1)

            def norm(it, n, src, dst):
                v.sem_inc(S["ln_turn"], 1)
                for t in range(NT):
                    last = d.bn_stats(stats[:, t, :], src[:, t, :])
                last.then_inc(S["ln_stats"], 1)
                v.wait_ge(S["ln_stats"], after(it, NLN, n + 1))
                v.sem_inc(S["ln_turn"], 1)
                for t in range(NT):
                    last = d.bn_aggr(mv[:, t, :], stats[:, t, :])
                last.then_inc(S["ln_mv"], 1)
                v.wait_ge(S["ln_mv"], after(it, NLN, n + 1))
                v.wait_ge(S["ln_rstd"], after(it, NLN, n + 1))
                for t in range(NT):
                    last = d.tensor_scalar(dst[:, t, :], src[:, t, :], mv[:, t, 0:1], rstd[:, t:t + 1],
                                           ALU.subtract, ALU.mult)
                last.then_inc(S["ln_out"], 1)

            d.memset(ones_f[:, :], 1.0)
            for s in range(2):
                d.memset(hT[s][64:P, 0:1], 0.0)
            v.wait_ge(S["small_in"], 9 * 16)
            for m in range(2):
                d.tensor_copy(mask_b[:, m, :, :], mask_f[:, m, :].unsqueeze(1).to_broadcast([P, 4, P]))
            for l in range(LAYERS):
                for z in range(2):
                    d.tensor_tensor(tab_c[:, l, :, z, :], base_c[:, :, z, :],
                                    scales[:, l, 0, z, :].unsqueeze(1).to_broadcast([P, NT, DH]), ALU.mult)
                    last = d.tensor_tensor(tab_s[:, l, :, z, :], base_s[:, :, z, :],
                                           scales[:, l, 1, z, :].unsqueeze(1).to_broadcast([P, NT, DH]), ALU.mult)
            v.wait_ge(S["idn"], 2)
            last = d.tensor_copy(ident_b[:, :], ident[:, :]).then_inc(S["tabs"], 1)
            v.wait_ge(S["tabs"], 1)
            v.wait_ge(S["x_in"], 16)
            v.wait_ge(M["zeroed"], 32)
            with v.Fori(0, PAIRS) as it:
                for s in range(2):
                    norm(it, ln_front(0, s), xr_tiles(it, s), y[s])
                for s in range(2):
                    v.wait_ge(S["xnT_mm"], after(it, 2, s + 1))
                    d.tensor_tensor_scan(hT_scan[s], a_col[:, 0:1].to_broadcast([P, SEQ]), bank(6 + s), 0.0,
                                         ALU.mult, ALU.add).then_inc(S["scanned"], 1)
                for s in range(2):
                    v.wait_ge(S["bc_mm"], after(it, 2, s + 1))
                    d.tensor_tensor(xr_tiles(it, s), xr_tiles(it, s), bank(2 + s).rearrange("p (t c) -> p t c", t=NT),
                                    ALU.add).then_inc(S["x1"], 1)
                    v.wait_ge(S["x1"], after(it, 2, s + 1))
                    norm(it, ln_front(1, s), xr_tiles(it, s), y[s])
                for l in range(LAYERS):
                    for s in range(2):
                        v.wait_ge(S["yT_mm"], after(it, NU, unit(l, s) + 1))
                        d.tensor_copy(hT[s][64:P, 1:SEQ], ps[64:P, (6 + s) * BANK:(7 + s) * BANK - 1])\
                         .then_inc(S["hT_hi"], 1)
                        for t in range(NT):
                            n = ut(l, s, t)
                            qk = bank((n % 2) * 2, of=2)
                            v.wait_ge(S["squared"], after(it, NUT, n + 1))
                            d.tensor_reduce(ssum[:, :], sq.rearrange("p (h d) -> p h d", d=DH), AX.X, ALU.add)\
                             .then_inc(S["ssq"], 1)
                            v.wait_ge(S["rnormed"], after(it, NUT, n + 1))
                            v.wait_ge(S["rot_bb"], after(it, 2 * NUT, 2 * n))
                            v.wait_ge(S["rot_a"], after(it, NUT, n))
                            d.tensor_tensor(qn.rearrange("p (h d) -> p h d", d=DH), qk.rearrange("p (h d) -> p h d", d=DH),
                                            rnorm[:, :].unsqueeze(2).to_broadcast([P, 2 * HEADS, DH]), ALU.mult)\
                             .then_inc(S["normed"], 1)
                            v.wait_ge(S["normed"], after(it, NUT, n + 1))
                            d.tensor_tensor(rot[s][:, t, :].rearrange("p (z h d) -> p z h d", z=2, h=HEADS),
                                            qn.rearrange("p (z h d) -> p z h d", z=2, h=HEADS),
                                            tab_c[:, l, t, :, :].unsqueeze(2).to_broadcast([P, 2, HEADS, DH]), ALU.mult)\
                             .then_inc(S["rot_a"], 1)
                    for s in range(2):
                        def scores_out(t):
                            n = ut(l, s, t)
                            sc = bank((t % 2) * 2, of=2).rearrange("p (h k) -> p h k", h=HEADS)
                            v.wait_ge(S["s_mm"], after(it, NUT, n + 1))
                            d.tensor_reduce(smx[t % 2][:, :], sc, AX.X, ALU.max).then_inc(S["smax"], 1)
                            v.wait_ge(S["smax"], after(it, NUT, n + 1))
                            v.wait_ge(S["pT_mm"], after(it, NUT, n - 1))
                            d.tensor_tensor(sdiff[t % 2], sc, smx[t % 2][:, :].unsqueeze(2).to_broadcast([P, HEADS, P]),
                                            ALU.subtract).then_inc(S["diffed"], 1)

                        def o_out(t):
                            n = ut(l, s, t)
                            ob = bank(6, of=2).rearrange("p (b n) -> p b n", b=2)[:, :, 0:4 * VW]\
                                .rearrange("p b (h d) -> p b h d", h=4)
                            v.wait_ge(S["o_mm"], after(it, NUT, n + 1))
                            d.reciprocal(orec[t % 2][:, :, :], ob[:, :, :, DH]).then_inc(S["o_rec"], 1)
                            v.wait_ge(S["o_rec"], after(it, NUT, n + 1))
                            d.tensor_tensor(o_sb[s][:, t, :].rearrange("p (b h d) -> p b h d", b=2, h=4),
                                            ob[:, :, :, 0:DH],
                                            orec[t % 2][:, :, :].unsqueeze(3).to_broadcast([P, 2, 4, DH]), ALU.mult)\
                             .then_inc(S["o_norm"], 1)

                        scores_out(0)
                        scores_out(1)
                        scores_out(2)
                        o_out(0)
                        scores_out(3)
                        o_out(1)
                        o_out(2)
                        o_out(3)
                    for s in range(2):
                        v.wait_ge(S["wo_mm"], after(it, NU, unit(l, s) + 1))
                        d.tensor_tensor(y[s][:, :, :], y[s][:, :, :], bank(2 + s).rearrange("p (t c) -> p t c", t=NT),
                                        ALU.add).then_inc(S["y_att"], 1)
                    for s in range(2):
                        v.wait_ge(S["y_att"], after(it, NU, unit(l, s) + 1))
                        d.tensor_copy(hs[s][:, :, 0:64], y[s][:, :, 0:64])
                        d.memset(hs[s][0:1, 0:1, 64:P], 0.0).then_inc(S["hs_top"], 1)
                        v.wait_ge(S["hs_top"], after(it, NU, unit(l, s) + 1))
                        v.wait_ge(hs_in[s], it * (LAYERS * 32) + 32 * (l + 1))
                        norm(it, ln_ffn(l, s), hs[s], hs[s])
                    for s in range(2):
                        for c in range(HC):
                            n = HC * unit(l, s) + c
                            m = HC * s + c
                            v.wait_ge(S["gelued"], after(it, HC * NU, n + 1))
                            b0 = (4, 0)[m % 2]
                            d.scalar_tensor_tensor(out=act[s][:, c, :], in0=ps[0:HW, b0 * BANK:(b0 + 1) * BANK],
                                                   scalar=b1[:, l, 0, c:c + 1], in1=gel[:, :], op0=ALU.add,
                                                   op1=ALU.mult).then_inc(S["acted"], 1)
                        v.wait_ge(S["down_mm"], after(it, NU, unit(l, s) + 1))
                        v.wait_ge(S["based"], after(it, NU, unit(l, s) + 1))
                        dst = y[s][:, :, :] if l < LAYERS - 1 else xr_tiles(it, s)
                        d.tensor_tensor(dst, ybase[:, :, :], bank(2 + s).rearrange("p (t c) -> p t c", t=NT),
                                        ALU.add).then_inc(S["y_out"], 1)

            v.wait_ge(T["w_in"], 7 * 16)
            d.tensor_reduce(wvg, wv_raw.rearrange("p (c j) -> p c j", j=GRP), AX.X, ALU.add)
            d.tensor_reduce(bvg[:, :], bv_raw.rearrange("p (c j) -> p c j", j=GRP), AX.X, ALU.add).then_inc(T["wv"], 1)
            d.tensor_scalar(bqk[:, 0:1], bqk[:, 0:1], DK ** -0.5, None, ALU.mult).then_inc(T["wv"], 1)
            for what, b, i in l1_steps():
                if what == "pre":
                    if b:
                        v.wait_ge(T["xn_mm"], b)
                    xb = xr[:, b * NT:(b + 1) * NT, :]
                    norm(PAIRS, 2 * b, xb, z1)
                    v.wait_ge(S["ln_out"], after(PAIRS, NLN, 2 * b + 1))
                    norm(PAIRS, 2 * b + 1, z1, z1)
                if what == "val":
                    v.wait_ge(T["v_mm"], b + 1)
                    v.wait_ge(T["zero"], 4)
                    if b >= 2:
                        v.wait_ge(T["pv"], 8 * (b - 1))
                    d.tensor_tensor(v1[b % 2][:, :, :, 0:VG], bank(l1_bank[what, b, i]).rearrange("p (t h g) -> p t h g", t=NT, h=H1),
                                    bvg[:, :].rearrange("p (h g) -> p h g", h=H1).unsqueeze(1).to_broadcast([P, NT, H1, VG]),
                                    ALU.add).then_inc(T["v_sb"], 1)
                if what == "max":
                    v.wait_ge(T["d_mm"], 16 * b + i + 1)
                    if b >= 2 and i == 0:
                        v.wait_ge(T["ms_mm"], b - 1)
                    d.tensor_reduce(mneg[b % 2][:, 2 * i:2 * i + 2], bank(l1_bank[what, b, i], of=2)
                                    .rearrange("p (q t) -> p q t", q=2), AX.X, ALU.max, negate=True).then_inc(T["mx"], 1)
                if what == "shift":
                    v.wait_ge(T["ms_mm"], b + 1)
                    if b:
                        v.wait_ge(sh_in[(b - 1) % 3], 16 * NSH * ((b - 1) // 3 + 1))
                    src = ps[0:H1 * NT, l1_bank[what, b, i] * BANK:l1_bank[what, b, i] * BANK + P]
                    d.tensor_copy(shift_p[:, 0, :], src).then_inc(T["ms_part"], 1)
                    v.wait_ge(T["ms_part"], 3 * b + 1)
                    d.tensor_tensor(shift_r[:, :], src, shift_p[:, 0, :], ALU.subtract).then_inc(T["ms_part"], 1)
                    v.wait_ge(T["ms_part"], 3 * b + 2)
                    d.tensor_copy(shift_p[:, 1, :], shift_r[:, :]).then_inc(T["ms_part"], 1)
                    v.wait_ge(T["ms_part"], 3 * b + 3)
                    d.tensor_tensor(shift_p[:, 2, :], shift_r[:, :], shift_p[:, 1, :], ALU.subtract).then_inc(T["ms_sb"], 1)
                if what == "end":
                    o = bank(6, of=2).rearrange("p (b n) -> p b n", b=2)[:, :, 0:16 * (VG + 1)]\
                        .rearrange("p b (j g) -> p b j g", j=16)
                    v.wait_ge(T["sel_mm"], b + 1)
                    d.reciprocal(arec[:, :, :], o[:, :, :, VG]).then_inc(T["rec"], 1)
                    v.wait_ge(T["rec"], b + 1)
                    d.tensor_tensor(att[:, :, :].rearrange("p t c -> p (t c)").rearrange("p (b j g) -> p b j g", b=2, j=16),
                                    o[:, :, :, 0:VG], arec[:, :, :].unsqueeze(3).to_broadcast([P, 2, 16, VG]), ALU.mult)\
                     .then_inc(T["att"], 1)
                    v.wait_ge(T["att"], b + 1)
                    xb = xr[:, b * NT:(b + 1) * NT, :]
                    d.tensor_tensor(xb, xb, att[:, :, :], ALU.add).then_inc(T["x3"], 1)

            for b in range(BATCH):
                norm(PAIRS, 2 * BATCH + b, xr[:, b * NT:(b + 1) * NT, :], h_m[:, b * NT:(b + 1) * NT, :])
            v.wait_ge(M["w_in"], 6 * 16)
            d.memset(ones_b, 1.0)
            d.tensor_copy(tri, tri_f).then_inc(M["tri"], 1)
            steps = [0]

            def link(ins):
                steps[0] += 1
                ins.then_inc(M["step"], 1)
                v.wait_ge(M["step"], steps[0])

            def te(x):
                return x.rearrange("p (t e) -> p t e", t=TILES)

            v.wait_ge(M["logits"], BATCH)
            lg = te(bank(7))
            d.tensor_reduce(rmax, lg, AX.X, ALU.max).then_inc(M["rmax"], 1)
            v.wait_ge(M["rmax"], 1)
            link(d.tensor_tensor(te(m1), lg, rmax.unsqueeze(2).to_broadcast([P, TILES, EXP]), ALU.is_equal))
            link(d.tensor_tensor(te(m2), te(m1), consts[:, 0:EXP].unsqueeze(1).to_broadcast([P, TILES, EXP]), ALU.mult))
            link(d.tensor_reduce(rev2, te(m2), AX.X, ALU.max))
            d.tensor_tensor(hot, te(m2), rev2.unsqueeze(2).to_broadcast([P, TILES, EXP]), ALU.is_equal).then_inc(M["hot"], 1)
            v.wait_ge(M["esc"], 1)
            link(d.tensor_scalar(score, esc, 1.0, None, ALU.add))
            link(d.reciprocal(score, score))
            d.tensor_tensor(h_m, h_m, score.unsqueeze(2).to_broadcast([P, TILES, P]), ALU.mult).then_inc(M["scaled"], 1)
            v.wait_ge(M["rank_mm"], 1)
            cnt = bank(1)[:, 0:EXP]
            link(d.tensor_tensor(m1.rearrange("p (e k) -> p e k", e=EXP), cnt.unsqueeze(2).to_broadcast([P, EXP, TILES]),
                                 consts[:, EXP:EXP + TILES].unsqueeze(1).to_broadcast([P, EXP, TILES]), ALU.is_gt))
            link(d.tensor_reduce(ntile, m1.rearrange("p (e k) -> p e k", e=EXP), AX.X, ALU.add))
            link(d.tensor_tensor_scan(incl, ones_f[:, :], ntile, 0.0, ALU.mult, ALU.add))
            link(d.tensor_tensor(base_e, incl, ntile, ALU.subtract))
            link(d.scalar_tensor_tensor(out=te(m1), in0=base_e.unsqueeze(1).to_broadcast([P, TILES, EXP]), scalar=float(P),
                                        in1=te(bank(0)), op0=ALU.mult, op1=ALU.add))
            link(d.tensor_tensor(te(m2), te(m1), hot, ALU.mult))
            link(d.tensor_reduce(slot_f, te(m2), AX.X, ALU.add))
            d.tensor_copy(slot_i, slot_f).then_inc(M["slots"], 1)
            nst = LOOP_TILES + AHEAD
            m3v = m3.rearrange("p (j e) -> p j e", e=EXP)
            link(d.tensor_tensor(m3v, consts[0:1, EXP + TILES:EXP + TILES + nst].unsqueeze(2).to_broadcast([1, nst, EXP]),
                                 incl[0:1, :].unsqueeze(1).to_broadcast([1, nst, EXP]), ALU.is_ge))
            link(d.tensor_reduce(exp_of_f, m3v, AX.X, ALU.add))
            d.tensor_scalar(exp_of, exp_of_f, float(EXP - 1), None, ALU.min).then_inc(M["slots"], 1)
            for b in range(BATCH):
                for c in range(IC):
                    n = IC * b + c
                    v.wait_ge(M["silu"], n + 1)
                    if b >= 2 and c == 0:
                        v.wait_ge(M["down_mm"], b - 1)
                    d.tensor_tensor(act_s[b % 2][:, c, :], silu_s[n % 2], bank(3 + 2 * (n % 2)), ALU.mult)\
                     .then_inc(M["acted"], 1)
                v.wait_ge(M["down_mm"], b + 1)
                xb = xr[:, b * NT:(b + 1) * NT, :]
                d.tensor_tensor(xb, xb, bank(6).rearrange("p (t c) -> p t c", t=NT), ALU.add).then_inc(M["x4s"], 1)

            def gated(t, j):
                v.wait_ge(M["r_silu"], j + 1)
                if not (isinstance(j, int) and j < 2):
                    v.wait_ge(M["actT_mm"], j - 1)
                d.tensor_tensor(act_r[t % 2], silu_r[t % 2], bank(2 + t % 2)[:, INTER:2 * INTER], ALU.mult)\
                 .then_inc(M["r_act"], 1)

            def dve_step(i, r, last):
                if not last or r + UP < AHEAD:
                    gated(r + UP, i * AHEAD + r + UP)
                v.wait_ge(M["y_mm"], i * AHEAD + r + 1)
                v.wait_ge(ys_out[r], i * 16 + 16)
                d.tensor_copy(ys[r], bank(6 + r % 2)[:, 0:P]).then_inc(M["y_sb"], 1)

            v.sem_inc(M["y_sb"], 2)
            for t in range(UP):
                gated(t, t)
            experts(v, dve_step)
            for b in range(BATCH):
                v.wait_ge(gathered[b], 16 * NT)
                xb = xr[:, b * NT:(b + 1) * NT, :]
                d.tensor_tensor(xb, xb, y_g[:, b * NT:(b + 1) * NT, :], ALU.add).then_inc(M["x4"], 1)

        @block.tensor
        def _(pe):
            mm, tr = nc.tensor.matmul, nc.tensor.transpose
            for name in COUNTED["PE"]:
                pe.sem_inc(S[name], 1)
            pe.wait_ge(S["tabs"], 1)
            pe.wait_ge(S["zero_p"], 6)
            pe.wait_ge(S["small_in"], 9 * 16)
            pe.wait_ge(S["w_in"], 8 * 16)
            with pe.Fori(0, PAIRS) as it:
                for s in range(2):
                    pe.wait_ge(S["ln_out"], after(it, NLN, ln_front(0, s) + 1))
                    for t in range(NT):
                        last = tr(bank(6 + s)[:, t * P:(t + 1) * P], y[s][:, t, :], ident[:, :])
                    last.then_inc(S["xnT_mm"], 1)
                for s in range(2):
                    pe.wait_ge(S["scanned"], after(it, 2, s + 1))
                    pe.wait_ge(S["y_out"], after(it, NU, 0))
                    for t in range(NT):
                        last = mm(bank(2 + s)[:, t * P:(t + 1) * P], hT_scan[s][:, t * P:(t + 1) * P], bc_w[:, :],
                                  start=True, stop=True)
                    last.then_inc(S["bc_mm"], 1)
                for l in range(LAYERS):
                    for s in range(2):
                        if l == 0:
                            pe.wait_ge(S["ln_out"], after(it, NLN, ln_front(1, s) + 1))
                        else:
                            pe.wait_ge(S["y_out"], after(it, NU, unit(l - 1, s) + 1))
                        for t in range(NT):
                            last = tr(bank(6 + s)[:, t * P:(t + 1) * P], y[s][:, t, :], ident[:, :])
                        last.then_inc(S["yT_mm"], 1)
                        pe.wait_ge(S["hT_lo"], after(it, NU, unit(l, s) + 1))
                        pe.wait_ge(S["hT_hi"], after(it, NU, unit(l, s) + 1))
                        for t in range(NT):
                            n = ut(l, s, t)
                            if s == 0 and t == 0:
                                pe.wait_ge(S["acted"], after(it, HC * NU, HC * unit(l, 0)))
                            if s == 0 and t == 1:
                                pe.wait_ge(S["y_out"], after(it, NU, unit(l, 0)))
                                if l == 0:
                                    pe.wait_ge(S["x1"], after(it, 2, 2))
                            pe.wait_ge(S["normed"], after(it, NUT, n - 1))
                            lhs = hT[s][:, t * P:(t + 1) * P]
                            mm(bank((n % 2) * 2), lhs, wqkv[l][:, 0:INNER], start=True, stop=True)
                            mm(bank((n % 2) * 2 + 1), lhs, wqkv[l][:, INNER:2 * INNER], start=True, stop=True)\
                                .then_inc(S["qk_mm"], 1)
                            pe.wait_ge(S["v_sb"], after(it, NUT, n - 1))
                            mm(bank(4 + n % 2), lhs, wqkv[l][:, 2 * INNER:3 * INNER], start=True, stop=True)\
                                .then_inc(S["v_mm"], 1)
                    for s in range(2):
                        def heads_T(t):
                            n = ut(l, s, t)
                            pe.wait_ge(S["rotated"], after(it, NUT, n + 1))
                            if t == 0 and s == 1:
                                pe.wait_ge(S["o_norm"], after(it, NUT, ut(l, 0, 3) + 1))
                            if t == 1 and s == 0:
                                pe.wait_ge(S["v_sb"], after(it, NUT, ut(l, 1, 3) + 1))
                            if t >= 2:
                                pe.wait_ge(S["qkT_sb"], after(it, NUT, n - 1))
                            b0 = 6 if t % 2 == 0 else 4
                            for z in range(2):
                                for h in range(HP):
                                    last = tr(bank(b0 + z)[:, h * P:(h + 1) * P],
                                              rot[s][:, t, (z * HP + h) * P:(z * HP + h + 1) * P], ident[:, :])
                            last.then_inc(S["qkT_mm"], 1)

                        def scores(t):
                            n = ut(l, s, t)
                            pe.wait_ge(S["qkT_sb"], after(it, NUT, n + 1))
                            if t < 2 and s == 0:
                                pe.wait_ge(S["normed"], after(it, NUT, ut(l, 1, t + 2) + 1))
                            if t >= 2 or s == 1:
                                pe.wait_ge(S["diffed"], after(it, NUT, n - 1))
                            for b in range(2):
                                bk = (t % 2) * 2 + b
                                mm(bank(bk), ident_b[:, :], mask_b[:, 0 if t else 1, :, :].rearrange("p h k -> p (h k)"),
                                   start=True, stop=True, skip_group_check=True)
                                for w in range(2):
                                    for h in range(2):
                                        q0 = t * P + w * WIN
                                        last = mm(ps[w * WIN:(w + 1) * WIN, bk * BANK + h * 256:bk * BANK + (h + 1) * 256],
                                                  qT[s][:, 2 * b + h, q0:q0 + WIN], kz[s][:, 2 * b + h, :, q0:q0 + P],
                                                  start=False, stop=True, skip_group_check=True)
                            last.then_inc(S["s_mm"], 1)

                        def probs_T(t):
                            n = ut(l, s, t)
                            pe.wait_ge(S["diffed"], after(it, NUT, n + 1))
                            if t == 0:
                                pe.wait_ge(S["qkT_sb"], after(it, NUT, ut(l, s, 3) + 1))
                            pe.wait_ge(S["exped"], after(it, NUT, n))
                            for h in range(HEADS):
                                last = tr(bank(4 + h // 4)[:, (h % 4) * P:(h % 4 + 1) * P], sdiff[t % 2][:, h, :], ident[:, :])
                            last.then_inc(S["pT_mm"], 1)

                        def values(t):
                            n = ut(l, s, t)
                            pe.wait_ge(S["exped"], after(it, NUT, n + 1))
                            if t == 0:
                                pe.wait_ge(v_off_in[s], it * (LAYERS * 32) + 32 * (l + 1))
                            pe.wait_ge(S["o_norm"], after(it, NUT, n))
                            for w in range(2):
                                vals = (v_off if w == 0 else v_al)[s]
                                for h in range(HEADS):
                                    c0 = (6 + h // 4) * BANK + (h % 4) * VW
                                    last = mm(ps[w * WIN:(w + 1) * WIN, c0:c0 + VW], pts[n % 2][:, h, w * WIN:(w + 1) * WIN],
                                              vals[:, t, h, :], start=True, stop=True)
                            last.then_inc(S["o_mm"], 1)

                        heads_T(0)
                        heads_T(1)
                        scores(0)
                        heads_T(2)
                        scores(1)
                        heads_T(3)
                        probs_T(0)
                        scores(2)
                        values(0)
                        probs_T(1)
                        scores(3)
                        values(1)
                        probs_T(2)
                        values(2)
                        probs_T(3)
                        values(3)
                    for s in range(2):
                        def o_T(t):
                            n = ut(l, s, t)
                            pe.wait_ge(S["o_norm"], after(it, NUT, n + 1))
                            if not (t < 2 and s == 0):
                                pe.wait_ge(S["oT_sb"], after(it, NUT, n - 1))
                            for c in range(4):
                                last = tr(bank(n % 2)[:, c * P:(c + 1) * P], o_sb[s][:, t, c * P:(c + 1) * P], ident[:, :])
                            last.then_inc(S["oT_mm"], 1)

                        def project(t):
                            n = ut(l, s, t)
                            pe.wait_ge(S["oT_sb"], after(it, NUT, n + 1))
                            for c in range(4):
                                last = mm(bank(2 + s)[:, t * P:(t + 1) * P], oT[n % 2][:, c, :], wo[l][:, c, :],
                                          start=(c == 0), stop=(c == 3))
                            if t == 3:
                                last.then_inc(S["wo_mm"], 1)

                        o_T(0)
                        o_T(1)
                        project(0)
                        o_T(2)
                        project(1)
                        o_T(3)
                        project(2)
                        project(3)
                    for s in range(2):
                        pe.wait_ge(S["ln_out"], after(it, NLN, ln_ffn(l, s) + 1))
                        for t in range(NT):
                            last = tr(bank(6 + s)[:, t * P:(t + 1) * P], hs[s][:, t, :], ident[:, :])
                        last.then_inc(S["hnT_mm"], 1)
                        pe.wait_ge(S["hnT_sb"], after(it, NU, unit(l, s) + 1))
                        for c in range(HC):
                            n = HC * unit(l, s) + c
                            m = HC * s + c
                            if m >= 2:
                                pe.wait_ge(S["acted"], after(it, HC * NU, n - 1))
                            b0 = (4, 0)[m % 2]
                            for g in range(2):
                                last = mm(ps[0:HW, (b0 + g) * BANK:(b0 + g + 1) * BANK], w1[l][:, g, c, :], hnT,
                                          start=True, stop=True)
                            last.then_inc(S["up_mm"], 1)
                        pe.wait_ge(S["acted"], after(it, HC * NU, HC * (unit(l, s) + 1)))
                        for t in range(NT):
                            for c in range(HC):
                                last = mm(bank(2 + s)[:, t * P:(t + 1) * P], act[s][:, c, t * P:(t + 1) * P],
                                          w2[l][0:HW, c, :], start=(c == 0), stop=(c == HC - 1))
                        last.then_inc(S["down_mm"], 1)
            pe.wait_ge(T["wv"], 1)
            pe.wait_ge(T["ones"], 3)
            ring = [(S["y_out"], after(PAIRS, NU, 0))] * 3

            def pair_of_banks(what, b, i, reader):
                at = l1_bank[what, b, i] // 2
                pe.wait_ge(*ring[at])
                ring[at] = reader
                return 2 * at

            def values1(b, i):
                hg, kt = i // 4, i % 4
                pe.wait_ge(T["ex"], 16 * b + 2 * i + 2)
                if kt == 0:
                    if b:
                        pe.wait_ge(T["att"], b)
                    if i == 0:
                        pe.wait_ge(T["v_sb"], b + 1)
                for h in range(4):
                    last = mm(ps[32 * h:32 * (h + 1), (6 + hg) * BANK:(7 + hg) * BANK],
                              v1[b % 2][:, kt, 4 * hg + h, :], pt[i % 2][:, h, :], start=(kt == 0), stop=(kt == NT - 1),
                              skip_group_check=True)
                last.then_inc(T["pv"], 1)

            for what, b, i in l1_steps():
                k = b % 3
                if what == "pre":
                    n0 = pair_of_banks(what, b, i, (T["xn_sb"], b + 1))
                    pe.wait_ge(S["ln_out"], after(PAIRS, NLN, 2 * b + 2))
                    for t in range(NT):
                        last = tr(bank(n0)[:, t * P:(t + 1) * P], z1[:, t, :], ident[:, :])
                    last.then_inc(T["xn_mm"], 1)
                if what == "qk":
                    n0 = pair_of_banks(what, b, i, (T["qk_sb"], b + 1))
                    pe.wait_ge(T["xn_sb"], b + 1)
                    mm(bank(n0), wq, xn1[:, :], start=True, stop=True)
                    mm(bank(n0 + 1), wk, xn1[:, :], start=True, stop=True).then_inc(T["qk_mm"], 1)
                if what == "val":
                    n0 = pair_of_banks(what, b, i, (T["v_sb"], b + 1))
                    for t in range(NT):
                        last = mm(bank(n0)[:, t * P:(t + 1) * P], xn1[:, t * P:(t + 1) * P], wvg, start=True, stop=True)
                    last.then_inc(T["v_mm"], 1)
                if what == "max":
                    n0 = pair_of_banks(what, b, i, (T["mx"], 16 * b + i + 1))
                    if i == 0:
                        pe.wait_ge(st_in[k], 16 * 2 * PARTS * (b // 3 + 1))
                    h = i // 2
                    for j in range(2):
                        q0 = ((i % 2) * 2 + j) * P
                        last = mm(bank(n0 + j), qst[k][0:KS, h, q0:q0 + P], kst[k][0:KS, h, :], start=True, stop=True)
                    last.then_inc(T["d_mm"], 1)
                if what == "shift":
                    n0 = pair_of_banks(what, b, i, (T["ms_sb"], b + 1))
                    pe.wait_ge(T["mx"], 16 * (b + 1))
                    tr(ps[0:H1 * NT, n0 * BANK:n0 * BANK + P], mneg[b % 2][:, :], ident[:, :]).then_inc(T["ms_mm"], 1)
                if what == "probs":
                    n0 = pair_of_banks(what, b, i, (T["ex"], 16 * b + i + 1))
                    if i == 0:
                        pe.wait_ge(sh_in[k], 16 * NSH * (b // 3 + 1))
                    kt, h0 = (i % 8) // 2, 4 * (i // 8) + 2 * (i % 2)
                    for j in range(2):
                        last = mm(bank(n0 + j), kst[k][0:KS + NSH, h0 + j, kt * P:(kt + 1) * P],
                                  qst[k][0:KS + NSH, h0 + j, :], start=True, stop=True)
                    last.then_inc(T["f_mm"], 1)
                    if i % 2 == 0 and i >= 2:
                        values1(b, i // 2 - 1)
                if what == "end":
                    values1(b, 7)
                    for hg in range(2):
                        pe.wait_ge(T["at_sb"], 2 * b + hg + 1)
                        cols = at_sb[hg].rearrange("p (r l) -> p r l", l=GRP)
                        for par in range(2):
                            for l in range(GRP):
                                dst = ps[64 * par:64 * par + 64, (6 + hg) * BANK:(6 + hg) * BANK + 16 * (VG + 1)]\
                                    .rearrange("p (j l g) -> p j l g", j=2, l=GRP)[:, :, l, :]
                                last = mm(dst, cols[:, :, l], sel[:, par, :].rearrange("p (j g) -> p j g", j=2),
                                          start=True, stop=True)
                    last.then_inc(T["sel_mm"], 1)
            pe.wait_ge(T["x3"], BATCH)
            pe.wait_ge(M["w_in"], 6 * 16)
            for b in range(BATCH):
                pe.wait_ge(S["ln_out"], after(PAIRS, NLN, 2 * BATCH + b + 1))
                if b >= 2:
                    pe.wait_ge(M["hT_sb"], b - 1)
                for t in range(NT):
                    last = tr(bank(b % 2)[:, t * P:(t + 1) * P], h_m[:, b * NT + t, :], ident[:, :])
                last.then_inc(M["hT_mm"], 1)
                pe.wait_ge(M["hT_sb"], b + 1)
                for t in range(b * NT, (b + 1) * NT):
                    last = mm(bank(7)[:, t * EXP:(t + 1) * EXP], hT_m[:, t * P:(t + 1) * P], gate_w, start=True, stop=True)
                last.then_inc(M["logits"], 1)

            def shared(b):
                for c in range(IC):
                    n = IC * b + c
                    if n >= 2:
                        pe.wait_ge(M["acted"], n - 1)
                    for z, w in enumerate((sg, su)):
                        last = mm(bank(2 + 2 * (n % 2) + z), w[:, c * P:(c + 1) * P], hT_m[:, b * SEQ:(b + 1) * SEQ],
                                  start=True, stop=True)
                    last.then_inc(M["up_mm"], 1)
                pe.wait_ge(M["acted"], IC * (b + 1))
                if b:
                    pe.wait_ge(M["x4s"], b)
                for t in range(NT):
                    for c in range(IC):
                        last = mm(bank(6)[:, t * P:(t + 1) * P], act_s[b % 2][:, c, t * P:(t + 1) * P], sd[:, c, :],
                                  start=(c == 0), stop=(c == IC - 1))
                last.then_inc(M["down_mm"], 1)

            pe.wait_ge(M["tri"], 1)
            pe.wait_ge(M["hot"], 1)
            hot_all = hot.rearrange("p t e -> p (t e)")
            mm(bank(0), tri, hot_all, start=True, stop=True, skip_group_check=True)
            for t in range(TILES - 1):
                rest = TILES - 1 - t
                mm(bank(0)[:, (t + 1) * EXP:].rearrange("p (t e) -> p t e", e=EXP), ones_b,
                   hot[:, t, :].unsqueeze(1).to_broadcast([P, rest, EXP]), start=False, stop=True,
                   skip_group_check=True)
            for t in range(TILES):
                last = mm(bank(1)[:, 0:EXP], ones_b, hot[:, t, :], start=(t == 0), stop=(t == TILES - 1))
            last.then_inc(M["rank_mm"], 1)
            for b in range(BATCH):
                shared(b)

            def tokens_T(t, i):
                pe.wait_ge(xs_in[t % AHEAD], i * 16 + 16 * (t // AHEAD + 1))
                tr(bank(t % 2)[:, 0:P], xs_in_sb[t % AHEAD], ident[:, :]).then_inc(M["xT_mm"], 1)

            def expert_of(t, i):
                return pe.value_load(exp_of[0:1, bass.ds(i * AHEAD + t, 1)], min_val=0, max_val=EXP - 1)

            def gate_up(t, i, e):
                pe.wait_ge(M["xT_sb"], i * AHEAD + t + 1)
                mm(bank(2 + t % 2), xsT[t % 2], wgu[:, bass.ds(e, 1), :].rearrange("p a n -> p (a n)"),
                   start=True, stop=True).then_inc(M["gu_mm"], 1)

            def gated_T(t, i):
                pe.wait_ge(M["r_act"], i * AHEAD + t + 1)
                for c in range(IC):
                    last = tr(bank(4 + t % 2)[:, c * P:(c + 1) * P], act_r[t % 2][:, c * P:(c + 1) * P], ident[:, :])
                last.then_inc(M["actT_mm"], 1)

            def down(t, i, e):
                pe.wait_ge(M["actT_sb"], i * AHEAD + t + 1)
                pe.wait_ge(M["y_sb"], i * AHEAD + t + 1)
                for c in range(IC):
                    last = mm(bank(6 + t % 2)[:, 0:P], actT[t % 2][:, c * P:(c + 1) * P],
                              wd[:, bass.ds(e, 1), c, :].rearrange("p a n -> p (a n)"), start=(c == 0), stop=(c == IC - 1))
                last.then_inc(M["y_mm"], 1)

            def pe_step(i, r, last):
                if not last or r + UP < AHEAD:
                    gate_up(r + UP, i, expert_of(r + UP, i))
                if not last or r + XT < AHEAD:
                    tokens_T(r + XT, i)
                if not last or r + BACK < AHEAD:
                    gated_T(r + BACK, i)
                down(r, i, expert_of(r, i))

            pe.wait_ge(M["slots"], 2)
            pe.wait_ge(M["x4s"], BATCH)
            pe.wait_ge(M["w_gu"], 16 * 16)
            pe.wait_ge(M["w_d"], 4 * 16)
            tokens_T(0, 0)
            tokens_T(1, 0)
            gate_up(0, 0, expert_of(0, 0))
            tokens_T(2, 0)
            gate_up(1, 0, expert_of(1, 0))
            gated_T(0, 0)
            experts(pe, pe_step)


def rotary_tables(np):
    f = np.float32
    half = np.arange(0, DH, 2, dtype=f)
    inv = (f(1.0) / np.power(f(10000.0), half / f(DH))).astype(f)
    t = np.arange(SEQ, dtype=f)
    fr = t[:, None] * inv[None, :]
    fr = np.concatenate([fr, fr], -1)
    base = (half + f(0.4 * DH)) / f(1.4 * DH)
    power = (t - SEQ // 2) / f(WIN // 2)
    sc = np.power(base[None, :], power[:, None]).astype(f)
    sc = np.concatenate([sc, sc], -1)
    cos, sin = np.cos(fr), np.sin(fr)
    sin = sin * np.concatenate([-np.ones(DH // 2, f), np.ones(DH // 2, f)])
    c = np.stack([cos * sc * f(8.0), cos / sc], 1)
    s = np.stack([sin * sc * f(8.0), sin / sc], 1)

    def lay(x):
        return np.ascontiguousarray(x.reshape(NT, P, 2, DH).transpose(1, 0, 2, 3).astype(f))

    return lay(c), lay(s)


def routing_constants(np):
    row = np.concatenate([EXP - np.arange(EXP), P * np.arange(TILES), np.arange(P - EXP - TILES)])
    return np.ascontiguousarray(np.broadcast_to(row.astype(np.float32), (P, P)))


def selector(np):
    sel = np.zeros((P, 2, 2, VG + 1), np.float32)
    for par in range(2):
        for j in range(2):
            for g in range(VG + 1):
                sel[32 * (2 * j + par) + g, par, j, g] = 1.0
    return sel.reshape(P, 2, 2 * (VG + 1))


def arrays_of(np, i):
    def c(a):
        return np.ascontiguousarray(a)

    tab_c, tab_s = rotary_tables(np)
    q = np.arange(P)[:, None] % WIN
    k = np.arange(P)[None, :]
    inside = (q <= k) & (k <= q + WIN)
    first = inside & ~((np.arange(P)[:, None] < WIN) & (k < WIN))
    f = np.float32
    mask = np.stack([np.where(inside, f(0), f(NEG)), np.where(first, f(0), f(NEG))], 1)
    qs, ks = np.asarray(i["L0_ffn_q_scale"]), np.asarray(i["L0_ffn_k_scale"])

    def swap(a):
        return np.concatenate([a[:, DH // 2:], a[:, :DH // 2]], -1)

    scales = np.stack([np.stack([qs, ks], 1), np.stack([swap(qs), swap(ks)], 1)], 1)
    w1, b1, w2 = (np.asarray(i["L0_ffn_" + n]) for n in ("w1", "b1", "w2"))
    w1 = np.pad(w1.reshape(LAYERS, P, 2, HID), ((0, 0),) * 3 + ((0, HC * HW - HID),)).reshape(LAYERS, P, 2, HC, HW)
    b1 = np.pad(b1.reshape(LAYERS, 2, HID), ((0, 0),) * 2 + ((0, HC * HW - HID),)).reshape(LAYERS, 2, HC, HW)
    w2 = np.pad(w2, ((0, 0), (0, HC * HW - HID), (0, 0))).reshape(LAYERS, HC, HW, P)
    return {
        "x": c(np.asarray(i["L0_attn_inputs"]).reshape(TOK, P)),
        "a": c(np.asarray(i["L0_attn_A"]).reshape(P, 1)),
        "bc": c(i["L0_attn_BC"]),
        "tab_c": tab_c, "tab_s": tab_s, "mask": c(mask.astype(f)),
        "scales": c(scales.reshape(LAYERS, 2, 2, DH)),
        "wqkv": c(i["L0_ffn_wqkv"]), "wo": c(i["L0_ffn_wo"]), "w1": c(w1), "w2": c(w2),
        "b1": c(b1.transpose(3, 0, 1, 2)), "b2": c(i["L0_ffn_b2"]),
        "wq": c(i["L1_attn_Wq"]), "wk": c(i["L1_attn_Wk"]), "wv": c(i["L1_attn_Wv"]), "bv": c(i["L1_attn_bv"]),
        "bqk": c(np.stack([np.asarray(i["L1_attn_bq"]), np.asarray(i["L1_attn_bk"])], 1)),
        "gb1": c(np.stack([np.asarray(i["L1_attn_gamma"]), np.asarray(i["L1_attn_beta"])], 1)),
        "sel": selector(np),
        "sg": c(i["L1_ffn_shared_gate_w"]), "su": c(i["L1_ffn_shared_up_w"]), "sd": c(i["L1_ffn_shared_down_w"]),
        "gate": c(i["L1_ffn_gate_w"]),
        "wgu": c(np.concatenate([np.asarray(i["L1_ffn_routed_gate_w"]), np.asarray(i["L1_ffn_routed_up_w"])], -1)
                 .transpose(1, 0, 2)),
        "wd": c(np.asarray(i["L1_ffn_routed_down_w"]).reshape(EXP, IC, P, P).transpose(2, 0, 1, 3)),
        "consts": routing_constants(np),
        "tri": c(np.triu(np.ones((P, P), np.float32), 1)),
        "ln_gb": c(np.stack([np.asarray(i["L0_ffn_ln_g"]), np.asarray(i["L0_ffn_ln_b"])], 1).transpose(2, 0, 1)),
    }


def kernel(**inputs):
    import numpy as _np
    import concourse.bacc as _bacc
    from concourse import mybir as _mybir
    from concourse.bass_utils import run_bass_kernel_spmd as _run

    nc = _bacc.Bacc("TRN2", target_bir_lowering=False, num_devices=1)
    arrays = arrays_of(_np, inputs)
    args = {n: nc.dram_tensor(f"in_{n}", a.shape, _mybir.dt.from_np(a.dtype), kind="ExternalInput").ap()
            for n, a in arrays.items()}
    out = nc.dram_tensor("out_0", (TOK, P), _mybir.dt.float32, kind="ExternalOutput").ap()
    build(nc, args, out)
    r = _run(nc, [{f"in_{n}": a for n, a in arrays.items()}], core_ids=[0])
    return r.results[0]["out_0"].reshape(BATCH, SEQ, P)
```

```python
import concourse.bass as bass
from concourse import mybir
from contextlib import ExitStack

FP = mybir.dt.float32
BF = mybir.dt.bfloat16
I32 = mybir.dt.int32
U32 = mybir.dt.uint32
ALU = mybir.AluOpType
ACT = mybir.ActivationFunctionType
AX = mybir.AxisListType

P = 128
BATCH, SEQ = 4, 512
TOK = BATCH * SEQ
NT = SEQ // P
TILES = TOK // P
PAIRS = BATCH // 2
EPS = 1e-5
BANK = 512

LAYERS, HEADS, DH, WIN = 2, 8, 64, 64
INNER = HEADS * DH
HEADS_LAG = 3
HP = HEADS // 2
HID, HC = 341, 3
HW = -(-HID // HC)
VW = DH + 1

H1, DK = 8, 16
GRP = 8
VG = P // GRP
PARTS = 6
Q_PART = (0, 0, 0, 1, 1, 2)
K_PART = (0, 1, 2, 0, 1, 0)
KS = PARTS * DK
NSH = 3

EXP, INTER = 32, 256
IC = INTER // P
SLOT_TILES = TILES + EXP - 1
AHEAD = 4
LOOP_TILES = -(-SLOT_TILES // AHEAD) * AHEAD
PASSES = LOOP_TILES // AHEAD
UP, XT, BACK = 2, 3, 1
SLOT_ROWS = (LOOP_TILES + AHEAD) * P
NEG = -1e30


def after(it, per_pair, n):
    return it * per_pair + max(n, 0) + 1


COUNTED = {
    "DVE": ("ln_stats", "ln_mv", "ln_out", "scanned", "x1", "hT_hi", "ssq", "root", "normed", "rot_a", "rotated", "smax", "diffed", "o_rec",
            "o_norm", "y_att", "hs_top", "acted", "y_out"),
    "Pool": ("ln_eps", "ln_rstd", "ssq_c", "newton", "rnormed", "rot_bb", "based_y", "based"),
    "ACT": ("hT_lo", "squared", "length", "v_sb", "qkT_sb", "exped", "oT_sb", "hnT_sb", "gelued"),
    "PE": ("xnT_mm", "bc_mm", "yT_mm", "qk_mm", "v_mm", "qkT_mm", "s_mm", "pT_mm", "o_mm", "oT_mm", "wo_mm", "hnT_mm",
           "up_mm", "down_mm"),
}


def build(nc, A, out):
    with ExitStack() as ctx:
        def sb(name, shape, dt=FP):
            return ctx.enter_context(nc.sbuf_tensor(name, shape, dt))

        def sem(name):
            return ctx.enter_context(nc.semaphore(name))

        region_a = sb("region_a", [P, EXP * 2 * INTER])
        region_d = sb("region_d", [P, EXP * IC * P + 88])
        region_b = sb("region_b", [P, 10400])
        region_r = sb("region_r", [P, 2 * 4096])
        used = {}

        def part(region, width, dt=FP):
            at = used.get(region.name, 0)
            used[region.name] = at + width
            assert used[region.name] <= region.shape[1], (region.name, used[region.name])
            return region[:, at:at + width]

        KZW = WIN + SEQ
        kz = [part(region_a, HP * 2 * KZW).rearrange("p (h z t) -> p h z t", h=HP, z=2) for _ in range(2)]
        v_al = [part(region_a, NT * HEADS * VW).rearrange("p (t h d) -> p t h d", t=NT, h=HEADS) for _ in range(2)]
        sq = part(region_a, 2 * INNER)
        hnT = [part(region_a, SEQ), sq[:, 0:SEQ]]
        ZEROS = 416
        zeros = part(region_a, ZEROS)

        wqkv = [part(region_d, 3 * INNER) for _ in range(LAYERS)]
        wo = [part(region_d, 4 * P).rearrange("p (c n) -> p c n", c=4) for _ in range(LAYERS)]
        w1 = [part(region_d, 2 * HC * HW).rearrange("p (g c n) -> p g c n", g=2, c=HC) for _ in range(LAYERS)]
        w2 = [part(region_d, HC * P).rearrange("p (c n) -> p c n", c=HC) for _ in range(LAYERS)]
        tab_c, tab_s = (part(region_d, LAYERS * NT * 2 * DH).rearrange("p (l t z d) -> p l t z d", l=LAYERS, t=NT, z=2)
                        for _ in range(2))

        qT = [part(region_b, HP * SEQ).rearrange("p (h t) -> p h t", h=HP) for _ in range(2)]
        v_off = [part(region_b, NT * HEADS * VW).rearrange("p (t h d) -> p t h d", t=NT, h=HEADS) for _ in range(2)]
        sdiff = [part(region_b, HEADS * P).rearrange("p (h k) -> p h k", h=HEADS) for _ in range(2)]

        rot = [region_r[:, i * 2 * INNER:(i + 1) * 2 * INNER] for i in range(HEADS_LAG)]
        qn = [region_r[:, (HEADS_LAG + i) * 2 * INNER:(HEADS_LAG + 1 + i) * 2 * INNER] for i in range(2)]
        o_sb = [region_r[:, s * 4096:s * 4096 + 2048].rearrange("p (t n) -> p t n", t=NT) for s in range(2)]
        act = [region_r[0:HW, s * 4096 + 2048:s * 4096 + 3584].rearrange("p (c t) -> p c t", c=HC) for s in range(2)]
        hs = [region_r[:, s * 4096 + 3584:(s + 1) * 4096].rearrange("p (t n) -> p t n", t=NT) for s in range(2)]

        xr = sb("xr", [P, TILES, P])
        y = [sb(f"y{s}", [P, NT, P]) for s in range(2)]
        hT = [sb(f"hT{s}", [P, SEQ]) for s in range(2)]
        pts = [sb(f"pts{i}", [P, HEADS, P]) for i in range(2)]
        hT_scan = [pts[s][:, 0:4, :].rearrange("p h q -> p (h q)") for s in range(2)]
        rot_b = sb("rot_b", [P, 2 * INNER])
        rotb = [rot_b[:, :], region_r[:, 5 * 2 * INNER:6 * 2 * INNER]]
        oT = [sb(f"oT{i}", [P, 4, P]) for i in range(2)]
        ybase = rot_b[:, 0:SEQ].rearrange("p (t c) -> p t c", t=NT)
        gel = rot_b[0:HW, SEQ:2 * SEQ]
        ident = sb("ident", [P, P])
        ident_b = sb("ident_b", [P, P], BF)
        mask_b = sb("mask_b", [P, 2, 4, P], BF)
        a_col = sb("a_col", [P, 1])
        bc_w = sb("bc_w", [P, P])
        ln_gb = sb("ln_gb", [P, LAYERS, 2])
        b1 = sb("b1", [HW, LAYERS, 2, HC])
        b2 = sb("b2", [P, LAYERS, P])
        stats = sb("stats", [P, NT, 6])
        mv = sb("mv", [P, NT, 2])
        rstd = sb("rstd", [P, NT])
        ssum = sb("ssum", [P, 2 * HEADS])
        ssum_c = sb("ssum_c", [P, 2 * HEADS])
        var_eps = sb("var_eps", [P, NT])
        eps = sb("eps", [P, NT])
        neg_half = sb("neg_half", [P, 2 * HEADS])
        rnorm = sb("rnorm", [P, 2 * HEADS])
        length = part(region_a, 2 * HEADS)
        root = part(region_a, 2 * HEADS)
        newton = part(region_a, 2 * HEADS)
        smx = [sb(f"smx{i}", [P, HEADS]) for i in range(2)]
        orec = [sb(f"orec{i}", [P, 2, 4]) for i in range(2)]

        def stack(region, at):
            return region[:, at:at + H1 * SEQ // 2].bitcast(BF).rearrange("p (h t) -> p h t", h=H1)

        half_st = H1 * SEQ // 2
        qst = [stack(region_b, 0), stack(region_b, half_st), stack(region_r, 0)]
        kst = [stack(region_b, 2 * half_st), stack(region_b, 3 * half_st), stack(region_r, half_st)]
        pt = [region_r[:, 4096 + i * 2048:4096 + (i + 1) * 2048].rearrange("p (h t) -> p h t", h=4) for i in range(2)]
        qk_parts = [region_b[:, 4 * half_st + i * 768:4 * half_st + (i + 1) * 768].bitcast(BF)
                    .rearrange("p (r t) -> p r t", r=3) for i in range(2)]
        wq, wk, wvg = (region_b[:, 4 * half_st + 1536 + i * P:4 * half_st + 1536 + (i + 1) * P] for i in range(3))
        z1, xn1 = y[0], hT[0]
        qk_f = [pts[0][:, i * 4:(i + 1) * 4, :].rearrange("p h q -> p (h q)") for i in range(2)]
        v1 = [pts[1][:, :, :].rearrange("p h q -> p (h q)").rearrange("p (t h g) -> p t h g", t=NT, h=H1),
              rot_b[:, :].rearrange("p (t h g) -> p t h g", t=NT, h=H1)]
        at_sb = [oT[i][:, :, :].rearrange("p c t -> p (c t)") for i in range(2)]
        att = y[1]
        wv_raw = pts[0][:, :, :].rearrange("p h q -> p (h q)")
        bv_raw = rot_b[:, :]
        ones_f = sb("ones_f", [P, EXP])
        sel = sb("sel", [P, 2, 2 * (VG + 1)])
        bvg = hT[1][:, 384:512]
        gb1 = sb("gb1", [P, 2])
        bqk = sb("bqk", [P, 2])
        mneg = [sb(f"mneg{i}", [P, H1 * NT]) for i in range(2)]
        shift_r = hT[1][0:H1 * NT, 0:P]
        shift_p = hT[1][0:H1 * NT, P:P + NSH * P // 2].bitcast(BF).rearrange("p (r t) -> p r t", r=NSH)
        arec = sb("arec", [P, 2, 16])
        parts_dram = nc.dram_tensor("parts_dram", (2, 3, P, SEQ), BF).ap()

        wgu = region_a[:, :].rearrange("p (e n) -> p e n", e=EXP)
        wd = region_d[:, 0:EXP * IC * P].rearrange("p (e c n) -> p e c n", e=EXP, c=IC)
        h_m = region_b[:, 0:2048].rearrange("p (t c) -> p t c", t=TILES)
        hT_m = region_b[:, 2048:4096]
        sg, su = region_b[:, 4096:4352], region_b[:, 4352:4608]
        sd = region_b[:, 4608:4864].rearrange("p (c n) -> p c n", c=IC)
        gate_w = region_b[:, 4864:4896]
        consts = region_b[:, 4896:5024]
        tri_f = region_b[:, 5024:5152]
        tri = region_b[:, 5152:5216].bitcast(BF)
        ones_b = region_b[:, 5216:5280].bitcast(BF)
        hot = region_b[:, 5280:5536].bitcast(BF).rearrange("p (t e) -> p t e", t=TILES)
        silu_s = [region_b[:, 5536 + i * 512:6048 + i * 512] for i in range(2)]
        act_s = [region_b[:, 6560 + i * 1024:7584 + i * 1024].rearrange("p (c t) -> p c t", c=IC) for i in range(2)]
        y_g = region_r[:, 0:2048].rearrange("p (t c) -> p t c", t=TILES)
        m1, m2 = region_r[:, 2048:2560], region_r[:, 2560:3072]
        m3 = region_r[0:1, 3072:3072 + (LOOP_TILES + AHEAD) * EXP]
        xs_in_sb = [region_r[:, 5120 + i * P:5120 + (i + 1) * P] for i in range(AHEAD)]
        xsT = [region_r[:, 5632 + i * P:5632 + (i + 1) * P] for i in range(2)]
        silu_r = [region_r[:, 5888 + i * INTER:5888 + (i + 1) * INTER] for i in range(2)]
        act_r = [region_r[:, 6400 + i * INTER:6400 + (i + 1) * INTER] for i in range(2)]
        actT = [region_r[:, 6912 + i * INTER:6912 + (i + 1) * INTER] for i in range(2)]
        ys = [region_r[:, 7424 + i * P:7424 + (i + 1) * P] for i in range(AHEAD)]
        rmax, rev2, esc, score, slot_f = (region_b[:, 8608 + i * TILES:8608 + (i + 1) * TILES] for i in range(5))
        slot_i = region_b[:, 8688:8704].bitcast(U32)
        ntile, incl, base_e = (region_b[:, 8704 + i * EXP:8704 + (i + 1) * EXP] for i in range(3))
        exp_of_f = region_b[0:1, 8800:8800 + LOOP_TILES + AHEAD]
        exp_of = region_b[0:1, 8864:8864 + LOOP_TILES + AHEAD].bitcast(I32)
        xs_dram = nc.dram_tensor("xs_dram", (SLOT_ROWS, P), FP).ap()
        ys_dram = nc.dram_tensor("ys_dram", (LOOP_TILES * P, P), FP).ap()

        base_c = region_r[:, 0:NT * 2 * DH].rearrange("p (t z d) -> p t z d", t=NT, z=2)
        base_s = region_r[:, 512:1024].rearrange("p (t z d) -> p t z d", t=NT, z=2)
        scales = region_r[:, 1024:1024 + LAYERS * 4 * DH].rearrange("p (l c z d) -> p l c z d", l=LAYERS, c=2, z=2)
        mask_f = region_r[:, 2048:2048 + 2 * P].rearrange("p (m k) -> p m k", m=2)

        ps = ctx.enter_context(nc.psum_tensor("ps", [P, 8 * BANK], FP))

        def bank(n, width=BANK, of=1):
            return ps[:, n * BANK:n * BANK + width * of]

        S = {n: sem(n) for n in (
            "x_in", "small_in", "w_in", "tabs", "idn", "zero_p", "masks",
            "ln_turn", "norm_turn", "v_turn", "ln_stats", "ln_mv", "ln_eps", "ln_rstd", "ln_out",
            "xnT_mm", "scanned", "bc_mm", "x1", "y_in", "yT_mm", "hT_lo", "hT_hi",
            "qk_mm", "v_mm", "squared", "ssq", "ssq_c", "length", "root", "newton", "rnormed", "normed", "rot_a", "rot_bb", "rotated",
            "v_sb", "qkT_mm", "qkT_sb", "s_mm", "smax", "diffed", "pT_mm", "exped", "o_mm",
            "o_rec", "o_norm", "oT_mm", "oT_sb", "wo_mm", "y_att", "hs_top", "based_y", "based", "hnT_mm", "hnT_sb",
            "up_mm", "gelued", "acted", "down_mm", "y_out", "stored")}
        v_off_in = [sem(f"v_off_in{s}") for s in range(2)]
        hs_in = [sem(f"hs_in{s}") for s in range(2)]
        T = {n: sem("l1_" + n) for n in (
            "w_in", "wv", "zero", "ones", "xn_mm", "xn_sb", "qk_mm", "qk_sb", "v_mm", "v_sb", "part", "parts", "stored",
            "d_mm", "mx", "ms_mm", "ms_part", "ms_sb", "f_mm", "ex", "pv", "at_sb", "sel_mm", "rec", "att", "x3")}
        st_in = [sem(f"l1_st_in{i}") for i in range(3)]
        sh_in = [sem(f"l1_sh_in{i}") for i in range(3)]
        M = {n: sem("moe_" + n) for n in (
            "zeros", "zeroed", "w_gu", "w_d", "w_in", "tri", "hT_mm", "hT_sb", "logits", "step", "rmax", "esc", "hot",
            "rank_mm", "slots", "scaled", "up_mm", "silu", "acted", "down_mm", "x4s", "scattered",
            "sp_turn", "xT_mm", "xT_sb", "gu_mm", "r_silu", "r_act", "actT_mm", "actT_sb", "y_mm", "y_sb", "x4")}
        xs_in = [sem(f"moe_xs_in{i}") for i in range(AHEAD)]
        gathered = [sem(f"moe_gathered{i}") for i in range(BATCH)]
        ys_out = [sem(f"moe_ys_out{i}") for i in range(AHEAD)]
        block = ctx.enter_context(nc.Block())

        def experts(engine, step):
            with engine.Fori(0, PASSES - 1) as i:
                for r in range(AHEAD):
                    step(i, r, False)
            for r in range(AHEAD):
                step(PASSES - 1, r, True)

        def l1_steps():
            for b in range(2):
                yield "pre", b, 0
                yield "qk", b, 0
                yield "val", b, 0
            for i in range(16):
                yield "max", 0, i
            yield "shift", 0, 0
            for b in range(BATCH):
                for i in range(16):
                    yield "probs", b, i
                    if b + 1 < BATCH:
                        yield "max", b + 1, i
                    if b + 2 < BATCH and i == 4:
                        yield "pre", b + 2, 0
                    if b + 2 < BATCH and i == 8:
                        yield "qk", b + 2, 0
                if b + 1 < BATCH:
                    yield "shift", b + 1, 0
                yield "end", b, 0
                if b + 2 < BATCH:
                    yield "val", b + 2, 0

        l1_bank, turn = {}, 0
        for what, b, i in l1_steps():
            if what != "end":
                l1_bank[what, b, i] = 2 * (turn % 3)
                turn += 1

        def unit(l, s):
            return 2 * l + s

        def ut(l, s, t):
            return 4 * unit(l, s) + t

        UT = 2 * NT
        NU, NUT = 2 * LAYERS, UT * LAYERS
        ln_front = lambda k, s: 2 * k + s
        ln_ffn = lambda l, s: 4 + 2 * l + s
        NLN = 8

        def z_pad(v):
            return v[:, :, :, :].rearrange("p t h g -> p (t h g)")

        def xr_tiles(it, s):
            return xr[:, bass.ds(it * (2 * NT) + s * NT, NT), :]

        @block.sync
        def _(sp):
            sp.dma_start(xr[:, :, :], A["x"].rearrange("(t p) c -> p t c", p=P)).then_inc(S["x_in"], 16)
            loads = [(a_col[:, :], A["a"]), (bc_w[:, :], A["bc"]), (base_c, A["tab_c"]), (base_s, A["tab_s"]),
                     (mask_f, A["mask"]), (ln_gb[:, :, :], A["ln_gb"]), (b1[:, :, :, :], A["b1"])]
            for dst, src in loads:
                sp.dma_start(dst, src).then_inc(S["small_in"], 16)
            sp.dma_start(scales, A["scales"].partition_broadcast(P)).then_inc(S["small_in"], 16)
            sp.dma_start(b2[:, :, :], A["b2"].partition_broadcast(P)).then_inc(S["small_in"], 16)
            for l in range(LAYERS):
                sp.dma_start(wqkv[l], A["wqkv"][l, :, :]).then_inc(S["w_in"], 16)
                sp.dma_start(wo[l], A["wo"][l, :, :].rearrange("(c p) n -> p c n", p=P)).then_inc(S["w_in"], 16)
                sp.dma_start(w1[l], A["w1"][l, :, :, :, :]).then_inc(S["w_in"], 16)
                sp.dma_start(w2[l][0:HW], A["w2"][l, :, :, :].rearrange("c p n -> p c n")).then_inc(S["w_in"], 16)
            sp.wait_ge(M["zeros"], 1)
            n_z = SLOT_ROWS // ZEROS
            sp.dma_start(xs_dram.rearrange("(p r) c -> p (r c)", p=P).rearrange("p (n z) -> p n z", z=ZEROS),
                         zeros.unsqueeze(1).to_broadcast([P, n_z, ZEROS])).then_inc(M["zeroed"], 16)
            with sp.Fori(0, PAIRS) as it:
                for l in range(LAYERS):
                    for s in range(2):
                        sp.wait_ge(S["v_sb"], after(it, NUT, ut(l, s, 3) + 1))
                        sp.sem_inc(S["v_turn"], 1)
                        sp.wait_ge(S["o_mm"], after(it, NUT, ut(l, s, 3) + 1 - 2 * NT))
                        sp.dma_start(v_off[s][0:WIN, 1:NT], v_al[s][WIN:P, 0:NT - 1]).then_inc(v_off_in[s], 16)
                        sp.dma_start(v_off[s][WIN:P, :], v_al[s][0:WIN, :]).then_inc(v_off_in[s], 16)
                    for s in range(2):
                        sp.wait_ge(S["y_att"], after(it, NU, unit(l, s) + 1))
                        h = P // 2
                        sp.dma_start(hs[s][1:P, :, h:P], y[s][0:P - 1, :, h:P]).then_inc(hs_in[s], 16)
                        sp.dma_start(hs[s][0:1, 1:NT, h:P], y[s][P - 1:P, 0:NT - 1, h:P]).then_inc(hs_in[s], 16)
            sp.wait_ge(S["y_out"], after(PAIRS, NU, 0))
            sp.dma_start(wv_raw, A["wv"]).then_inc(T["w_in"], 16)
            sp.dma_start(bv_raw, A["bv"].partition_broadcast(P)).then_inc(T["w_in"], 16)
            for dst, src in ((wq, A["wq"]), (wk, A["wk"]), (gb1[:, :], A["gb1"]), (bqk[:, :], A["bqk"]),
                             (sel[:, :, :], A["sel"])):
                sp.dma_start(dst, src).then_inc(T["w_in"], 16)
            sp.wait_ge(M["zeroed"], 16)
            chunk = 0
            for what, b, i in l1_steps():
                k = b % 3
                if what == "probs" and i % 3 == 1 and chunk < 20:
                    sp.wait_ge(T["ex"], 16 * b + i)
                    if chunk < 16:
                        e0 = 2 * chunk
                        sp.dma_start(wgu[:, e0:e0 + 2, :], A["wgu"][:, e0:e0 + 2, :]).then_inc(M["w_gu"], 16)
                    else:
                        e0 = 8 * (chunk - 16)
                        sp.dma_start(wd[:, e0:e0 + 8, :, :], A["wd"][:, e0:e0 + 8, :, :]).then_inc(M["w_d"], 16)
                    chunk += 1
                if what == "qk":
                    sp.wait_ge(T["parts"], 2 * (b + 1))
                    for z in range(2):
                        sp.dma_start(parts_dram[z, :, :, :].rearrange("r p t -> p r t"), qk_parts[z]).then_inc(T["stored"], 16)
                    sp.wait_ge(T["stored"], 32 * (b + 1))
                    if b >= 3:
                        sp.wait_ge(T["f_mm"], 16 * (b - 2))
                    for z, (st, which) in enumerate(((qst, Q_PART), (kst, K_PART))):
                        for g in range(PARTS):
                            sp.dma_start(st[k][g * DK:(g + 1) * DK, :, :],
                                         parts_dram[z, which[g], :, :].rearrange("(h d) t -> d h t", h=H1))\
                              .then_inc(st_in[k], 16)
                    sp.wait_ge(st_in[k], 16 * 2 * PARTS * (b // 3 + 1))
                if what == "shift":
                    sp.wait_ge(T["ms_sb"], b + 1)
                    for j in range(NSH):
                        sp.dma_start(qst[k][KS + j:KS + j + 1, :, :].rearrange("p h (q t) -> p (h q) t", q=NT),
                                     shift_p[:, j, :]).then_inc(sh_in[k], 16)
            sp.wait_ge(T["x3"], BATCH)
            sp.wait_ge(T["pv"], 8 * BATCH)
            for dst, src in ((sg, A["sg"]), (su, A["su"]), (sd, A["sd"].rearrange("(c p) n -> p c n", p=P)),
                             (gate_w, A["gate"]), (consts, A["consts"]), (tri_f, A["tri"])):
                sp.dma_start(dst, src).then_inc(M["w_in"], 16)
            sp.wait_ge(M["scattered"], 16 * TILES)
            for r in range(AHEAD):
                sp.dma_start(xs_in_sb[r], xs_dram[r * P:(r + 1) * P, :]).then_inc(xs_in[r], 16)
            for r in range(AHEAD):
                sp.sem_inc(ys_out[r], 16)
            for t in range(XT):
                sp.wait_ge(M["xT_mm"], t + 1)
                sp.dma_start(xs_in_sb[t], xs_dram[(t + AHEAD) * P:(t + AHEAD + 1) * P, :]).then_inc(xs_in[t], 16)

            def sp_step(i, r, last):
                row = (i * AHEAD + r) * P
                if not last:
                    sp.wait_ge(M["xT_mm"], i * AHEAD + r + XT + 1)
                    sp.sem_inc(M["sp_turn"], 1)
                    t = (r + XT) % AHEAD
                    sp.dma_start(xs_in_sb[t], xs_dram[bass.ds(row + (XT + AHEAD) * P, P), :]).then_inc(xs_in[t], 16)
                sp.wait_ge(M["y_sb"], i * AHEAD + r + 3)
                sp.sem_inc(M["sp_turn"], 1)
                sp.dma_start(ys_dram[bass.ds(row, P), :], ys[r]).then_inc(ys_out[r], 16)

            experts(sp, sp_step)
            for b in range(BATCH):
                sp.wait_ge(M["x4"], b + 1)
                rows = out[b * SEQ:(b + 1) * SEQ, :].rearrange("(t p) c -> p t c", p=P)
                sp.dma_start(rows, xr[:, b * NT:(b + 1) * NT, :]).then_inc(S["stored"], 16)
            for r in range(AHEAD):
                sp.wait_ge(xs_in[r], 16 * (PASSES + (r < XT)))
            sp.wait_ge(S["stored"], 16 * BATCH)

        @block.gpsimd
        def _(pool):
            g = nc.gpsimd
            for name in COUNTED["Pool"]:
                pool.sem_inc(S[name], 1)
            g.memset(zeros, 0.0).then_inc(M["zeros"], 1)
            g.memset(ident[:, :], 0.0).then_inc(S["idn"], 1)
            pool.wait_ge(S["idn"], 1)
            g.affine_select(out=ident[:, :], in_=ident[:, :], compare_op=ALU.not_equal, fill=1.0,
                            base=0, pattern=[[-1, P]], channel_multiplier=1).then_inc(S["idn"], 1)
            g.memset(eps[:, :], EPS)
            g.memset(neg_half[:, :], -0.5).then_inc(S["idn"], 1)
            pool.wait_ge(S["idn"], 3)
            for s in range(2):
                g.memset(kz[s].rearrange("p h z t -> p (h z t)"), 0.0).then_inc(S["zero_p"], 1)
                g.memset(v_off[s].rearrange("p t h d -> p (t h d)"), 0.0).then_inc(S["zero_p"], 1)
                g.memset(v_al[s][:, :, :, DH:VW], 1.0).then_inc(S["zero_p"], 1)
            with pool.Fori(0, PAIRS) as it:
                def power(n):
                    pool.wait_ge(S["ln_mv"], after(it, NLN, n + 1))
                    g.tensor_tensor(var_eps[:, 0:NT], mv[:, :, 1], eps[:, 0:NT], ALU.add).then_inc(S["ln_eps"], 1)
                    pool.wait_ge(S["ln_eps"], after(it, NLN, n + 1))
                    g.tensor_tensor(rstd[:, :], var_eps[:, 0:NT], neg_half[:, 0:NT], ALU.pow)\
                     .then_inc(S["ln_rstd"], 1)

                for k in range(2):
                    for s in range(2):
                        power(ln_front(k, s))
                for l in range(LAYERS):
                    def clamp(u):
                        n = UT * l + u
                        pool.wait_ge(S["ssq"], after(it, NUT, n + 1))
                        pool.sem_inc(S["norm_turn"], 1)
                        g.tensor_scalar(ssum_c[:, :], ssum[:, :], 1e-24, None, ALU.max).then_inc(S["ssq_c"], 1)

                    def refine(u):
                        n = UT * l + u
                        pool.wait_ge(S["root"], after(it, NUT, n + 1))
                        g.tensor_tensor(newton, root, root, ALU.mult).then_inc(S["newton"], 1)
                        pool.wait_ge(S["newton"], after(it, 3 * NUT, 3 * n + 1))
                        g.tensor_tensor(newton, newton, ssum_c[:, :], ALU.mult).then_inc(S["newton"], 1)
                        pool.wait_ge(S["newton"], after(it, 3 * NUT, 3 * n + 2))
                        pool.sem_inc(S["norm_turn"], 1)
                        g.tensor_scalar(newton, newton, -0.5, 1.5, ALU.mult, ALU.add).then_inc(S["newton"], 1)
                        pool.wait_ge(S["newton"], after(it, 3 * NUT, 3 * n + 3))
                        g.tensor_tensor(rnorm[:, :], newton, root, ALU.mult).then_inc(S["rnormed"], 1)

                    def rotate_half(u, half):
                        t, n = u % NT, UT * l + u
                        src = qn[n % 2].rearrange("p (z h j d) -> p z h j d", z=2, h=HEADS, j=2)[:, :, :, 1 - half, :]
                        dst = rotb[n % 2].rearrange("p (z h j d) -> p z h j d", z=2, h=HEADS, j=2)[:, :, :, half, :]
                        tab = tab_s[:, l, t, :, half * 32:half * 32 + 32].unsqueeze(2).to_broadcast([P, 2, HEADS, 32])
                        g.tensor_tensor(dst, src, tab, ALU.mult).then_inc(S["rot_bb"], 1)

                    clamp(0)
                    refine(0)
                    for u in range(UT):
                        n = UT * l + u
                        pool.wait_ge(S["normed"], after(it, NUT, n + 1))
                        pool.sem_inc(S["norm_turn"], 1)
                        pool.wait_ge(S["rotated"], after(it, NUT, n - 1))
                        rotate_half(u, 0)
                        if u + 1 < UT:
                            clamp(u + 1)
                        rotate_half(u, 1)
                        if u + 1 < UT:
                            refine(u + 1)
                    for s in range(2):
                        power(ln_ffn(l, s))
                        pool.wait_ge(S["y_out"], after(it, NU, unit(l, s)))
                        pool.wait_ge(S["y_att"], after(it, NU, unit(l, s) + 1))
                        bb = b2[:, l, :].unsqueeze(1).to_broadcast([P, NT, P])
                        last = g.tensor_tensor(ybase[:, :, :], y[s][:, :, :], bb, ALU.add)
                        if l == LAYERS - 1:
                            last.then_inc(S["based_y"], 1)
                            pool.wait_ge(S["based_y"], after(it, 2, s + 1))
                            last = g.tensor_tensor(ybase[:, :, :], ybase[:, :, :], xr_tiles(it, s), ALU.add)
                        last.then_inc(S["based"], 1)

            pool.wait_ge(S["y_out"], after(PAIRS, NU, 0))
            for k in range(3):
                g.memset(kst[k][KS:KS + NSH, :, :], 1.0).then_inc(T["ones"], 1)
                pool.wait_ge(T["ones"], k + 1)
            g.memset(z_pad(v1[0]), 0.0).then_inc(T["zero"], 1)
            pool.wait_ge(T["wv"], 1)
            g.memset(z_pad(v1[1]), 0.0).then_inc(T["zero"], 1)
            pool.wait_ge(T["zero"], 2)
            for i in range(2):
                g.memset(v1[i][:, :, :, VG:VG + 1], 1.0).then_inc(T["zero"], 1)
            for what, b, i in l1_steps():
                if what == "pre":
                    for r in range(2):
                        n = 2 * b + r
                        pool.wait_ge(S["ln_mv"], after(PAIRS, NLN, n + 1))
                        g.tensor_tensor(var_eps[:, 0:NT], mv[:, :, 1], eps[:, 0:NT], ALU.add).then_inc(S["ln_eps"], 1)
                        pool.wait_ge(S["ln_eps"], after(PAIRS, NLN, n + 1))
                        g.tensor_tensor(rstd[:, :], var_eps[:, 0:NT], neg_half[:, 0:NT], ALU.pow)\
                         .then_inc(S["ln_rstd"], 1)
                if what == "qk":
                    pool.wait_ge(T["qk_sb"], b + 1)
                    if b:
                        pool.wait_ge(T["stored"], 32 * b)
                    for z in range(2):
                        f, p3 = qk_f[z], qk_parts[z]
                        g.tensor_copy(p3[:, 0, :], f).then_inc(T["part"], 1)
                    pool.wait_ge(T["part"], 6 * b + 2)
                    for z in range(2):
                        f, p3 = qk_f[z], qk_parts[z]
                        g.tensor_tensor(f, f, p3[:, 0, :], ALU.subtract).then_inc(T["part"], 1)
                    pool.wait_ge(T["part"], 6 * b + 4)
                    for z in range(2):
                        f, p3 = qk_f[z], qk_parts[z]
                        g.tensor_copy(p3[:, 1, :], f).then_inc(T["part"], 1)
                    pool.wait_ge(T["part"], 6 * b + 6)
                    for z in range(2):
                        f, p3 = qk_f[z], qk_parts[z]
                        g.tensor_tensor(p3[:, 2, :], f, p3[:, 1, :], ALU.subtract).then_inc(T["parts"], 1)

            for b in range(BATCH):
                n = 2 * BATCH + b
                pool.wait_ge(S["ln_mv"], after(PAIRS, NLN, n + 1))
                g.tensor_tensor(var_eps[:, 0:NT], mv[:, :, 1], eps[:, 0:NT], ALU.add).then_inc(S["ln_eps"], 1)
                pool.wait_ge(S["ln_eps"], after(PAIRS, NLN, n + 1))
                g.tensor_tensor(rstd[:, :], var_eps[:, 0:NT], neg_half[:, 0:NT], ALU.pow).then_inc(S["ln_rstd"], 1)
            pool.wait_ge(M["slots"], 1)
            pool.wait_ge(M["scaled"], 1)
            pool.wait_ge(M["zeroed"], 16)
            for t in range(TILES):
                g.indirect_dma_start(out=xs_dram[:, :], out_offset=bass.IndirectOffsetOnAxis(ap=slot_i[:, t:t + 1], axis=0),
                                     in_=h_m[:, t, :], in_offset=None).then_inc(M["scattered"], 16)
            for r in range(AHEAD):
                pool.wait_ge(ys_out[r], 16 * (PASSES + 1))
            for t in range(TILES):
                g.indirect_dma_start(out=y_g[:, t, :], out_offset=None, in_=ys_dram[:, :],
                                     in_offset=bass.IndirectOffsetOnAxis(ap=slot_i[:, t:t + 1], axis=0))\
                 .then_inc(gathered[t // NT], 16)

        @block.scalar
        def _(a):
            act_ = nc.scalar.activation
            for name in COUNTED["ACT"]:
                a.sem_inc(S[name], 1)
            a.wait_ge(S["small_in"], 9 * 16)
            with a.Fori(0, PAIRS) as it:
                for l in range(LAYERS):
                    def lower_half(s):
                        a.wait_ge(S["yT_mm"], after(it, NU, unit(l, s) + 1))
                        act_(hT[s][0:64, :], ps[0:64, 5 * BANK:6 * BANK], ACT.Copy).then_inc(S["hT_lo"], 1)

                    def heads_sb(u):
                        s, t, n = u // NT, u % NT, UT * l + u
                        a.wait_ge(S["qkT_mm"], after(it, NUT, n + 1))
                        cols = slice(t * P, (t + 1) * P)
                        kcols = slice(WIN + t * P, WIN + (t + 1) * P)
                        act_(qT[s][:, :, cols], bank(6).rearrange("p (h t) -> p h t", h=HP), ACT.Copy)
                        kp = bank(7).rearrange("p (h t) -> p h t", h=HP)
                        act_(kz[s][0:64, :, 0, kcols], kp[0:64], ACT.Copy)
                        act_(kz[s][64:P, :, 1, kcols], kp[64:P], ACT.Copy).then_inc(S["qkT_sb"], 1)

                    lower_half(0)
                    for u in range(UT):
                        s, t, n = u // NT, u % NT, UT * l + u
                        a.wait_ge(S["qk_mm"], after(it, NUT, n + 1))
                        a.wait_ge(S["ssq"], after(it, NUT, n))
                        act_(sq, bank((n % 2) * 2, of=2), ACT.Square).then_inc(S["squared"], 1)
                        a.wait_ge(S["v_mm"], after(it, NUT, n + 1))
                        act_(v_al[s][:, t, :, 0:DH], bank(4).rearrange("p (h d) -> p h d", h=HEADS),
                             ACT.Copy).then_inc(S["v_sb"], 1)
                        if u == 1:
                            lower_half(1)
                        if u >= HEADS_LAG:
                            heads_sb(u - HEADS_LAG)
                        a.wait_ge(S["ssq_c"], after(it, NUT, n + 1))
                        act_(length, ssum_c[:, :], ACT.Sqrt).then_inc(S["length"], 1)
                    for u in range(UT - HEADS_LAG, UT):
                        heads_sb(u)
                    for u in range(UT):
                        n = UT * l + u
                        a.wait_ge(S["pT_mm"], after(it, NUT, n + 1))
                        a.wait_ge(S["o_mm"], after(it, NUT, n - 1))
                        act_(pts[n % 2].rearrange("p h q -> p (h q)"), bank(4, of=2), ACT.Exp).then_inc(S["exped"], 1)
                    for s in range(2):
                        for t in range(NT):
                            n = ut(l, s, t)
                            a.wait_ge(S["oT_mm"], after(it, NUT, n + 1))
                            act_(oT[n % 2].rearrange("p c t -> p (c t)"), bank(n % 2), ACT.Copy).then_inc(S["oT_sb"], 1)
                    def normed_sb(s):
                        a.wait_ge(S["hnT_mm"], after(it, NU, unit(l, s) + 1))
                        act_(hnT[s], bank(6 + s), ACT.Identity, scale=ln_gb[:, l, 0:1],
                             bias=ln_gb[:, l, 1:2]).then_inc(S["hnT_sb"], 1)

                    normed_sb(0)
                    for m in range(2 * HC):
                        n = HC * unit(l, 0) + m
                        a.wait_ge(S["up_mm"], after(it, HC * NU, n + 1))
                        a.wait_ge(S["acted"], after(it, HC * NU, n))
                        act_(gel[:, :], ps[0:HW, ((5, 1)[m % 2]) * BANK:((5, 1)[m % 2] + 1) * BANK], ACT.Gelu,
                             bias=b1[:, l, 1, m % HC:m % HC + 1]).then_inc(S["gelued"], 1)
                        if m == HC - 1:
                            normed_sb(1)

            a.wait_ge(T["w_in"], 7 * 16)
            for what, b, i in l1_steps():
                if what == "pre":
                    a.wait_ge(T["xn_mm"], b + 1)
                    if b:
                        a.wait_ge(T["v_mm"], b)
                    act_(xn1[:, :], bank(l1_bank[what, b, i]), ACT.Identity, scale=gb1[:, 0:1], bias=gb1[:, 1:2])\
                        .then_inc(T["xn_sb"], 1)
                if what == "qk":
                    a.wait_ge(T["qk_mm"], b + 1)
                    a.wait_ge(T["wv"], 2)
                    if b:
                        a.wait_ge(T["parts"], 2 * b)
                    act_(qk_f[0], bank(l1_bank[what, b, i]), ACT.Identity, scale=DK ** -0.5, bias=bqk[:, 0:1])
                    act_(qk_f[1], bank(l1_bank[what, b, i] + 1), ACT.Identity, bias=bqk[:, 1:2]).then_inc(T["qk_sb"], 1)
                if what == "probs":
                    a.wait_ge(T["f_mm"], 16 * b + i + 1)
                    if 8 * b + i // 2 - 1 > 0:
                        a.wait_ge(T["pv"], 8 * b + i // 2 - 1)
                    dst = pt[(i // 2) % 2][:, (i % 2) * 2:(i % 2) * 2 + 2, :].rearrange("p h t -> p (h t)")
                    act_(dst, bank(l1_bank[what, b, i], of=2), ACT.Exp).then_inc(T["ex"], 1)
                if (what, i) == ("probs", 10) or what == "end":
                    hg = int(what == "end")
                    a.wait_ge(T["pv"], 8 * b + 4 * (hg + 1))
                    if b:
                        a.wait_ge(T["sel_mm"], b)
                    act_(at_sb[hg], bank(6 + hg), ACT.Copy).then_inc(T["at_sb"], 1)

            for b in range(BATCH):
                a.wait_ge(M["hT_mm"], b + 1)
                act_(hT_m[:, b * SEQ:(b + 1) * SEQ], bank(b % 2), ACT.Copy).then_inc(M["hT_sb"], 1)
            a.wait_ge(M["rmax"], 1)
            act_(esc, rmax, ACT.Exp, scale=-1.0).then_inc(M["esc"], 1)
            for n in range(BATCH * IC):
                a.wait_ge(M["up_mm"], n + 1)
                if n >= 2:
                    a.wait_ge(M["acted"], n - 1)
                act_(silu_s[n % 2], bank(2 + 2 * (n % 2)), ACT.Silu).then_inc(M["silu"], 1)

            def tokens_sb(t, j):
                a.wait_ge(M["xT_mm"], j + 1)
                if not (isinstance(j, int) and j < 2):
                    a.wait_ge(M["gu_mm"], j - 1)
                act_(xsT[t % 2], bank(t % 2)[:, 0:P], ACT.Copy).then_inc(M["xT_sb"], 1)

            def gate_sb(t, j):
                a.wait_ge(M["gu_mm"], j + 1)
                if not (isinstance(j, int) and j < 2):
                    a.wait_ge(M["r_act"], j - 1)
                act_(silu_r[t % 2], bank(2 + t % 2)[:, 0:INTER], ACT.Silu).then_inc(M["r_silu"], 1)

            def back_sb(t, j):
                a.wait_ge(M["actT_mm"], j + 1)
                if not (isinstance(j, int) and j < 2):
                    a.wait_ge(M["y_mm"], j - 1)
                act_(actT[t % 2], bank(4 + t % 2)[:, 0:INTER], ACT.Copy).then_inc(M["actT_sb"], 1)

            def act_step(i, r, last):
                for lag, do in ((XT, tokens_sb), (UP, gate_sb), (BACK, back_sb)):
                    if not last or r + lag < AHEAD:
                        do(r + lag, i * AHEAD + r + lag)

            for t in range(XT):
                tokens_sb(t, t)
            for t in range(UP):
                gate_sb(t, t)
            back_sb(0, 0)
            experts(a, act_step)

        @block.vector
        def _(v):
            d = nc.vector
            for name in COUNTED["DVE"]:
                v.sem_inc(S[name], 1)

            def norm(it, n, src, dst):
                v.sem_inc(S["ln_turn"], 1)
                for t in range(NT):
                    last = d.bn_stats(stats[:, t, :], src[:, t, :])
                last.then_inc(S["ln_stats"], 1)
                v.wait_ge(S["ln_stats"], after(it, NLN, n + 1))
                v.sem_inc(S["ln_turn"], 1)
                for t in range(NT):
                    last = d.bn_aggr(mv[:, t, :], stats[:, t, :])
                last.then_inc(S["ln_mv"], 1)
                v.wait_ge(S["ln_mv"], after(it, NLN, n + 1))
                v.wait_ge(S["ln_rstd"], after(it, NLN, n + 1))
                for t in range(NT):
                    last = d.tensor_scalar(dst[:, t, :], src[:, t, :], mv[:, t, 0:1], rstd[:, t:t + 1],
                                           ALU.subtract, ALU.mult)
                last.then_inc(S["ln_out"], 1)

            d.memset(ones_f[:, :], 1.0)
            for s in range(2):
                d.memset(hT[s][64:P, 0:1], 0.0)
            v.wait_ge(S["small_in"], 9 * 16)
            for m in range(2):
                d.tensor_copy(mask_b[:, m, :, :], mask_f[:, m, :].unsqueeze(1).to_broadcast([P, 4, P]))
            for l in range(LAYERS):
                for z in range(2):
                    d.tensor_tensor(tab_c[:, l, :, z, :], base_c[:, :, z, :],
                                    scales[:, l, 0, z, :].unsqueeze(1).to_broadcast([P, NT, DH]), ALU.mult)
                    last = d.tensor_tensor(tab_s[:, l, :, z, :], base_s[:, :, z, :],
                                           scales[:, l, 1, z, :].unsqueeze(1).to_broadcast([P, NT, DH]), ALU.mult)
            v.wait_ge(S["idn"], 2)
            last = d.tensor_copy(ident_b[:, :], ident[:, :]).then_inc(S["tabs"], 1)
            v.wait_ge(S["tabs"], 1)
            v.wait_ge(S["x_in"], 16)
            with v.Fori(0, PAIRS) as it:
                for s in range(2):
                    norm(it, ln_front(0, s), xr_tiles(it, s), y[s])
                for s in range(2):
                    v.wait_ge(S["xnT_mm"], after(it, 2, s + 1))
                    d.tensor_tensor_scan(hT_scan[s], a_col[:, 0:1].to_broadcast([P, SEQ]), bank(6 + s), 0.0,
                                         ALU.mult, ALU.add).then_inc(S["scanned"], 1)
                for s in range(2):
                    v.wait_ge(S["bc_mm"], after(it, 2, s + 1))
                    d.tensor_tensor(xr_tiles(it, s), xr_tiles(it, s), bank(2 + s).rearrange("p (t c) -> p t c", t=NT),
                                    ALU.add).then_inc(S["x1"], 1)
                    v.wait_ge(S["x1"], after(it, 2, s + 1))
                    norm(it, ln_front(1, s), xr_tiles(it, s), y[s])
                for l in range(LAYERS):
                    def upper_half(s):
                        v.wait_ge(S["yT_mm"], after(it, NU, unit(l, s) + 1))
                        d.tensor_copy(hT[s][64:P, 1:SEQ], ps[64:P, 5 * BANK:6 * BANK - 1]).then_inc(S["hT_hi"], 1)

                    def squares_sum(u):
                        v.wait_ge(S["squared"], after(it, NUT, UT * l + u + 1))
                        d.tensor_reduce(ssum[:, :], sq.rearrange("p (h d) -> p h d", d=DH), AX.X, ALU.add)\
                         .then_inc(S["ssq"], 1)

                    def normalise(u):
                        t, n = u % NT, UT * l + u
                        qk = bank((n % 2) * 2, of=2)
                        v.wait_ge(S["rnormed"], after(it, NUT, n + 1))
                        v.wait_ge(S["rot_bb"], after(it, 2 * NUT, 2 * n - 2))
                        v.wait_ge(S["rot_a"], after(it, NUT, n - 1))
                        d.tensor_tensor(qn[n % 2].rearrange("p (h d) -> p h d", d=DH), qk.rearrange("p (h d) -> p h d", d=DH),
                                        rnorm[:, :].unsqueeze(2).to_broadcast([P, 2 * HEADS, DH]), ALU.mult)\
                         .then_inc(S["normed"], 1)

                    def inverse(u):
                        n = UT * l + u
                        v.wait_ge(S["length"], after(it, NUT, n + 1))
                        v.wait_ge(S["rnormed"], after(it, NUT, n))
                        d.reciprocal(root, length).then_inc(S["root"], 1)

                    def scale_cos(u):
                        t, n = u % NT, UT * l + u
                        v.wait_ge(S["normed"], after(it, NUT, n + 1))
                        v.wait_ge(S["qkT_mm"], after(it, NUT, n - 2))
                        d.tensor_tensor(rot[u % HEADS_LAG].rearrange("p (z h d) -> p z h d", z=2, h=HEADS),
                                        qn[n % 2].rearrange("p (z h d) -> p z h d", z=2, h=HEADS),
                                        tab_c[:, l, t, :, :].unsqueeze(2).to_broadcast([P, 2, HEADS, DH]), ALU.mult)\
                         .then_inc(S["rot_a"], 1)

                    def rotate(u):
                        n = UT * l + u
                        v.wait_ge(S["rot_a"], after(it, NUT, n + 1))
                        v.wait_ge(S["rot_bb"], after(it, 2 * NUT, 2 * n + 2))
                        d.tensor_tensor(rot[u % HEADS_LAG], rot[u % HEADS_LAG], rotb[n % 2], ALU.add).then_inc(S["rotated"], 1)

                    def scores_out(u):
                        n = UT * l + u
                        sc = bank((n % 2) * 2, of=2).rearrange("p (h k) -> p h k", h=HEADS)
                        v.wait_ge(S["s_mm"], after(it, NUT, n + 1))
                        d.tensor_reduce(smx[n % 2][:, :], sc, AX.X, ALU.max).then_inc(S["smax"], 1)
                        v.wait_ge(S["smax"], after(it, NUT, n + 1))
                        v.wait_ge(S["pT_mm"], after(it, NUT, n - 1))
                        d.tensor_tensor(sdiff[n % 2], sc, smx[n % 2][:, :].unsqueeze(2).to_broadcast([P, HEADS, P]),
                                        ALU.subtract).then_inc(S["diffed"], 1)

                    def o_out(u):
                        s, t, n = u // NT, u % NT, UT * l + u
                        ob = bank(6, of=2).rearrange("p (b n) -> p b n", b=2)[:, :, 0:4 * VW]\
                            .rearrange("p b (h d) -> p b h d", h=4)
                        v.wait_ge(S["o_mm"], after(it, NUT, n + 1))
                        d.reciprocal(orec[n % 2][:, :, :], ob[:, :, :, DH]).then_inc(S["o_rec"], 1)
                        v.wait_ge(S["o_rec"], after(it, NUT, n + 1))
                        d.tensor_tensor(o_sb[s][:, t, :].rearrange("p (b h d) -> p b h d", b=2, h=4), ob[:, :, :, 0:DH],
                                        orec[n % 2][:, :, :].unsqueeze(3).to_broadcast([P, 2, 4, DH]), ALU.mult)\
                         .then_inc(S["o_norm"], 1)

                    def y_att(s):
                        v.wait_ge(S["wo_mm"], after(it, NU, unit(l, s) + 1))
                        d.tensor_tensor(y[s][:, :, :], y[s][:, :, :], bank(2 + s).rearrange("p (t c) -> p t c", t=NT),
                                        ALU.add).then_inc(S["y_att"], 1)
                        v.wait_ge(S["y_att"], after(it, NU, unit(l, s) + 1))
                        d.tensor_copy(hs[s][:, :, 0:64], y[s][:, :, 0:64])
                        d.memset(hs[s][0:1, 0:1, 64:P], 0.0).then_inc(S["hs_top"], 1)

                    def norm_hs(s):
                        v.wait_ge(S["hs_top"], after(it, NU, unit(l, s) + 1))
                        v.wait_ge(hs_in[s], it * (LAYERS * 32) + 32 * (l + 1))
                        norm(it, ln_ffn(l, s), hs[s], hs[s])

                    def gated_l0(m):
                        n = HC * unit(l, 0) + m
                        v.wait_ge(S["gelued"], after(it, HC * NU, n + 1))
                        b0 = (4, 0)[m % 2]
                        d.scalar_tensor_tensor(out=act[m // HC][:, m % HC, :], in0=ps[0:HW, b0 * BANK:(b0 + 1) * BANK],
                                               scalar=b1[:, l, 0, m % HC:m % HC + 1], in1=gel[:, :], op0=ALU.add,
                                               op1=ALU.mult).then_inc(S["acted"], 1)

                    def y_out(s):
                        v.wait_ge(S["down_mm"], after(it, NU, unit(l, s) + 1))
                        v.wait_ge(S["based"], after(it, NU, unit(l, s) + 1))
                        dst = y[s][:, :, :] if l < LAYERS - 1 else xr_tiles(it, s)
                        d.tensor_tensor(dst, ybase[:, :, :], bank(2 + s).rearrange("p (t c) -> p t c", t=NT),
                                        ALU.add).then_inc(S["y_out"], 1)

                    upper_half(0)
                    squares_sum(0)
                    inverse(0)
                    normalise(0)
                    squares_sum(1)
                    scale_cos(0)
                    inverse(1)
                    upper_half(1)
                    for u in range(UT):
                        if u + 1 < UT:
                            normalise(u + 1)
                        if u + 2 < UT:
                            squares_sum(u + 2)
                        if u + 1 < UT:
                            scale_cos(u + 1)
                        else:
                            scores_out(0)
                        if u + 2 < UT:
                            inverse(u + 2)
                        rotate(u)
                    scores_out(1)
                    for u in range(UT):
                        if u + 2 < UT:
                            scores_out(u + 2)
                        o_out(u)
                    y_att(0)
                    norm_hs(0)
                    y_att(1)
                    gated_l0(0)
                    norm_hs(1)
                    for m in range(1, 2 * HC):
                        gated_l0(m)
                        if m == HC:
                            y_out(0)
                    y_out(1)

            v.wait_ge(T["w_in"], 7 * 16)
            d.tensor_reduce(wvg, wv_raw.rearrange("p (c j) -> p c j", j=GRP), AX.X, ALU.add)
            d.tensor_reduce(bvg[:, :], bv_raw.rearrange("p (c j) -> p c j", j=GRP), AX.X, ALU.add).then_inc(T["wv"], 1)
            d.tensor_scalar(bqk[:, 0:1], bqk[:, 0:1], DK ** -0.5, None, ALU.mult).then_inc(T["wv"], 1)
            for what, b, i in l1_steps():
                if what == "pre":
                    if b:
                        v.wait_ge(T["xn_mm"], b)
                    xb = xr[:, b * NT:(b + 1) * NT, :]
                    norm(PAIRS, 2 * b, xb, z1)
                    v.wait_ge(S["ln_out"], after(PAIRS, NLN, 2 * b + 1))
                    norm(PAIRS, 2 * b + 1, z1, z1)
                if what == "val":
                    v.wait_ge(T["v_mm"], b + 1)
                    v.wait_ge(T["zero"], 4)
                    if b >= 2:
                        v.wait_ge(T["pv"], 8 * (b - 1))
                    d.tensor_tensor(v1[b % 2][:, :, :, 0:VG], bank(l1_bank[what, b, i]).rearrange("p (t h g) -> p t h g", t=NT, h=H1),
                                    bvg[:, :].rearrange("p (h g) -> p h g", h=H1).unsqueeze(1).to_broadcast([P, NT, H1, VG]),
                                    ALU.add).then_inc(T["v_sb"], 1)
                if what == "max":
                    v.wait_ge(T["d_mm"], 16 * b + i + 1)
                    if b >= 2 and i == 0:
                        v.wait_ge(T["ms_mm"], b - 1)
                    d.tensor_reduce(mneg[b % 2][:, 2 * i:2 * i + 2], bank(l1_bank[what, b, i], of=2)
                                    .rearrange("p (q t) -> p q t", q=2), AX.X, ALU.max, negate=True).then_inc(T["mx"], 1)
                if what == "shift":
                    v.wait_ge(T["ms_mm"], b + 1)
                    if b:
                        v.wait_ge(sh_in[(b - 1) % 3], 16 * NSH * ((b - 1) // 3 + 1))
                    src = ps[0:H1 * NT, l1_bank[what, b, i] * BANK:l1_bank[what, b, i] * BANK + P]
                    d.tensor_copy(shift_p[:, 0, :], src).then_inc(T["ms_part"], 1)
                    v.wait_ge(T["ms_part"], 3 * b + 1)
                    d.tensor_tensor(shift_r[:, :], src, shift_p[:, 0, :], ALU.subtract).then_inc(T["ms_part"], 1)
                    v.wait_ge(T["ms_part"], 3 * b + 2)
                    d.tensor_copy(shift_p[:, 1, :], shift_r[:, :]).then_inc(T["ms_part"], 1)
                    v.wait_ge(T["ms_part"], 3 * b + 3)
                    d.tensor_tensor(shift_p[:, 2, :], shift_r[:, :], shift_p[:, 1, :], ALU.subtract).then_inc(T["ms_sb"], 1)
                if what == "end":
                    o = bank(6, of=2).rearrange("p (b n) -> p b n", b=2)[:, :, 0:16 * (VG + 1)]\
                        .rearrange("p b (j g) -> p b j g", j=16)
                    v.wait_ge(T["sel_mm"], b + 1)
                    d.reciprocal(arec[:, :, :], o[:, :, :, VG]).then_inc(T["rec"], 1)
                    v.wait_ge(T["rec"], b + 1)
                    d.tensor_tensor(att[:, :, :].rearrange("p t c -> p (t c)").rearrange("p (b j g) -> p b j g", b=2, j=16),
                                    o[:, :, :, 0:VG], arec[:, :, :].unsqueeze(3).to_broadcast([P, 2, 16, VG]), ALU.mult)\
                     .then_inc(T["att"], 1)
                    v.wait_ge(T["att"], b + 1)
                    xb = xr[:, b * NT:(b + 1) * NT, :]
                    d.tensor_tensor(xb, xb, att[:, :, :], ALU.add).then_inc(T["x3"], 1)

            for b in range(BATCH):
                norm(PAIRS, 2 * BATCH + b, xr[:, b * NT:(b + 1) * NT, :], h_m[:, b * NT:(b + 1) * NT, :])
            v.wait_ge(M["w_in"], 6 * 16)
            d.memset(ones_b, 1.0)
            d.tensor_copy(tri, tri_f).then_inc(M["tri"], 1)
            steps = [0]

            def link(ins):
                steps[0] += 1
                ins.then_inc(M["step"], 1)
                v.wait_ge(M["step"], steps[0])

            def te(x):
                return x.rearrange("p (t e) -> p t e", t=TILES)

            v.wait_ge(M["logits"], BATCH)
            lg = te(bank(7))
            d.tensor_reduce(rmax, lg, AX.X, ALU.max).then_inc(M["rmax"], 1)
            v.wait_ge(M["rmax"], 1)
            link(d.tensor_tensor(te(m1), lg, rmax.unsqueeze(2).to_broadcast([P, TILES, EXP]), ALU.is_equal))
            link(d.tensor_tensor(te(m2), te(m1), consts[:, 0:EXP].unsqueeze(1).to_broadcast([P, TILES, EXP]), ALU.mult))
            link(d.tensor_reduce(rev2, te(m2), AX.X, ALU.max))
            d.tensor_tensor(hot, te(m2), rev2.unsqueeze(2).to_broadcast([P, TILES, EXP]), ALU.is_equal).then_inc(M["hot"], 1)
            v.wait_ge(M["esc"], 1)
            link(d.tensor_scalar(score, esc, 1.0, None, ALU.add))
            link(d.reciprocal(score, score))
            d.tensor_tensor(h_m, h_m, score.unsqueeze(2).to_broadcast([P, TILES, P]), ALU.mult).then_inc(M["scaled"], 1)
            v.wait_ge(M["rank_mm"], 1)
            cnt = bank(1)[:, 0:EXP]
            link(d.tensor_tensor(m1.rearrange("p (e k) -> p e k", e=EXP), cnt.unsqueeze(2).to_broadcast([P, EXP, TILES]),
                                 consts[:, EXP:EXP + TILES].unsqueeze(1).to_broadcast([P, EXP, TILES]), ALU.is_gt))
            link(d.tensor_reduce(ntile, m1.rearrange("p (e k) -> p e k", e=EXP), AX.X, ALU.add))
            link(d.tensor_tensor_scan(incl, ones_f[:, :], ntile, 0.0, ALU.mult, ALU.add))
            link(d.tensor_tensor(base_e, incl, ntile, ALU.subtract))
            link(d.scalar_tensor_tensor(out=te(m1), in0=base_e.unsqueeze(1).to_broadcast([P, TILES, EXP]), scalar=float(P),
                                        in1=te(bank(0)), op0=ALU.mult, op1=ALU.add))
            link(d.tensor_tensor(te(m2), te(m1), hot, ALU.mult))
            link(d.tensor_reduce(slot_f, te(m2), AX.X, ALU.add))
            d.tensor_copy(slot_i, slot_f).then_inc(M["slots"], 1)
            nst = LOOP_TILES + AHEAD
            m3v = m3.rearrange("p (j e) -> p j e", e=EXP)
            link(d.tensor_tensor(m3v, consts[0:1, EXP + TILES:EXP + TILES + nst].unsqueeze(2).to_broadcast([1, nst, EXP]),
                                 incl[0:1, :].unsqueeze(1).to_broadcast([1, nst, EXP]), ALU.is_ge))
            link(d.tensor_reduce(exp_of_f, m3v, AX.X, ALU.add))
            d.tensor_scalar(exp_of, exp_of_f, float(EXP - 1), None, ALU.min).then_inc(M["slots"], 1)
            for b in range(BATCH):
                for c in range(IC):
                    n = IC * b + c
                    v.wait_ge(M["silu"], n + 1)
                    if b >= 2 and c == 0:
                        v.wait_ge(M["down_mm"], b - 1)
                    d.tensor_tensor(act_s[b % 2][:, c, :], silu_s[n % 2], bank(3 + 2 * (n % 2)), ALU.mult)\
                     .then_inc(M["acted"], 1)
                v.wait_ge(M["down_mm"], b + 1)
                xb = xr[:, b * NT:(b + 1) * NT, :]
                d.tensor_tensor(xb, xb, bank(6).rearrange("p (t c) -> p t c", t=NT), ALU.add).then_inc(M["x4s"], 1)

            def gated(t, j):
                v.wait_ge(M["r_silu"], j + 1)
                if not (isinstance(j, int) and j < 2):
                    v.wait_ge(M["actT_mm"], j - 1)
                d.tensor_tensor(act_r[t % 2], silu_r[t % 2], bank(2 + t % 2)[:, INTER:2 * INTER], ALU.mult)\
                 .then_inc(M["r_act"], 1)

            def dve_step(i, r, last):
                if not last or r + UP < AHEAD:
                    gated(r + UP, i * AHEAD + r + UP)
                v.wait_ge(M["y_mm"], i * AHEAD + r + 1)
                v.wait_ge(ys_out[r], i * 16 + 16)
                d.tensor_copy(ys[r], bank(6 + r % 2)[:, 0:P]).then_inc(M["y_sb"], 1)

            v.sem_inc(M["y_sb"], 2)
            for t in range(UP):
                gated(t, t)
            experts(v, dve_step)
            for b in range(BATCH):
                v.wait_ge(gathered[b], 16 * NT)
                xb = xr[:, b * NT:(b + 1) * NT, :]
                d.tensor_tensor(xb, xb, y_g[:, b * NT:(b + 1) * NT, :], ALU.add).then_inc(M["x4"], 1)

        @block.tensor
        def _(pe):
            mm, tr = nc.tensor.matmul, nc.tensor.transpose
            for name in COUNTED["PE"]:
                pe.sem_inc(S[name], 1)
            pe.wait_ge(S["tabs"], 1)
            pe.wait_ge(S["zero_p"], 6)
            pe.wait_ge(S["small_in"], 9 * 16)
            pe.wait_ge(S["w_in"], 8 * 16)
            with pe.Fori(0, PAIRS) as it:
                for s in range(2):
                    pe.wait_ge(S["ln_out"], after(it, NLN, ln_front(0, s) + 1))
                    for t in range(NT):
                        last = tr(bank(6 + s)[:, t * P:(t + 1) * P], y[s][:, t, :], ident[:, :])
                    last.then_inc(S["xnT_mm"], 1)
                for s in range(2):
                    pe.wait_ge(S["scanned"], after(it, 2, s + 1))
                    pe.wait_ge(S["y_out"], after(it, NU, 0))
                    for t in range(NT):
                        last = mm(bank(2 + s)[:, t * P:(t + 1) * P], hT_scan[s][:, t * P:(t + 1) * P], bc_w[:, :],
                                  start=True, stop=True)
                    last.then_inc(S["bc_mm"], 1)
                for l in range(LAYERS):
                    def stream_T(s):
                        if s == 0:
                            pe.wait_ge(S["acted"], after(it, HC * NU, HC * unit(l, 0)))
                        else:
                            pe.wait_ge(S["hT_lo"], after(it, NU, unit(l, 0) + 1))
                            pe.wait_ge(S["hT_hi"], after(it, NU, unit(l, 0) + 1))
                        if l == 0:
                            pe.wait_ge(S["ln_out"], after(it, NLN, ln_front(1, s) + 1))
                        else:
                            pe.wait_ge(S["y_out"], after(it, NU, unit(l - 1, s) + 1))
                        for t in range(NT):
                            last = tr(bank(5)[:, t * P:(t + 1) * P], y[s][:, t, :], ident[:, :])
                        last.then_inc(S["yT_mm"], 1)

                    def project_qkv(u):
                        s, t, n = u // NT, u % NT, UT * l + u
                        if t == 0:
                            pe.wait_ge(S["hT_lo"], after(it, NU, unit(l, s) + 1))
                            pe.wait_ge(S["hT_hi"], after(it, NU, unit(l, s) + 1))
                        if u == 1:
                            pe.wait_ge(S["y_out"], after(it, NU, unit(l, 0)))
                            if l == 0:
                                pe.wait_ge(S["x1"], after(it, 2, 2))
                        pe.wait_ge(S["normed"], after(it, NUT, n - 1))
                        lhs = hT[s][:, t * P:(t + 1) * P]
                        mm(bank((n % 2) * 2), lhs, wqkv[l][:, 0:INNER], start=True, stop=True)
                        mm(bank((n % 2) * 2 + 1), lhs, wqkv[l][:, INNER:2 * INNER], start=True, stop=True)\
                            .then_inc(S["qk_mm"], 1)
                        pe.wait_ge(S["v_sb"], after(it, NUT, n))
                        mm(bank(4), lhs, wqkv[l][:, 2 * INNER:3 * INNER], start=True, stop=True).then_inc(S["v_mm"], 1)

                    def heads_T(u):
                        n = UT * l + u
                        pe.wait_ge(S["rotated"], after(it, NUT, n + 1))
                        if u == 0:
                            pe.wait_ge(S["hnT_sb"], after(it, NU, unit(l, 0)))
                        pe.wait_ge(S["qkT_sb"], after(it, NUT, n))
                        for z in range(2):
                            for h in range(HP):
                                last = tr(bank(6 + z)[:, h * P:(h + 1) * P],
                                          rot[u % HEADS_LAG][:, (z * HP + h) * P:(z * HP + h + 1) * P], ident[:, :])
                        last.then_inc(S["qkT_mm"], 1)

                    def scores(u):
                        s, t, n = u // NT, u % NT, UT * l + u
                        if t == 0:
                            pe.wait_ge(S["qkT_sb"], after(it, NUT, n + NT))
                        if u < 2:
                            pe.wait_ge(S["normed"], after(it, NUT, n + UT - 2 + 1))
                        else:
                            pe.wait_ge(S["diffed"], after(it, NUT, n - 1))
                        for b in range(2):
                            bk = (n % 2) * 2 + b
                            mm(bank(bk), ident_b[:, :], mask_b[:, 0 if t else 1, :, :].rearrange("p h k -> p (h k)"),
                               start=True, stop=True, skip_group_check=True)
                            for w in range(2):
                                for h in range(2):
                                    q0 = t * P + w * WIN
                                    last = mm(ps[w * WIN:(w + 1) * WIN, bk * BANK + h * 256:bk * BANK + (h + 1) * 256],
                                              qT[s][:, 2 * b + h, q0:q0 + WIN], kz[s][:, 2 * b + h, :, q0:q0 + P],
                                              start=False, stop=True, skip_group_check=True)
                        last.then_inc(S["s_mm"], 1)

                    def probs_T(u):
                        n = UT * l + u
                        pe.wait_ge(S["diffed"], after(it, NUT, n + 1))
                        if u == 0:
                            pe.wait_ge(S["v_sb"], after(it, NUT, UT * (l + 1)))
                        pe.wait_ge(S["exped"], after(it, NUT, n))
                        for h in range(HEADS):
                            last = tr(bank(4 + h // 4)[:, (h % 4) * P:(h % 4 + 1) * P], sdiff[n % 2][:, h, :], ident[:, :])
                        last.then_inc(S["pT_mm"], 1)

                    def values(u):
                        s, t, n = u // NT, u % NT, UT * l + u
                        pe.wait_ge(S["exped"], after(it, NUT, n + 1))
                        if u == 0:
                            pe.wait_ge(S["qkT_sb"], after(it, NUT, UT * (l + 1)))
                        if t == 0:
                            pe.wait_ge(v_off_in[s], it * (LAYERS * 32) + 32 * (l + 1))
                        pe.wait_ge(S["o_norm"], after(it, NUT, n))
                        for w in range(2):
                            vals = (v_off if w == 0 else v_al)[s]
                            for h in range(HEADS):
                                c0 = (6 + h // 4) * BANK + (h % 4) * VW
                                last = mm(ps[w * WIN:(w + 1) * WIN, c0:c0 + VW], pts[n % 2][:, h, w * WIN:(w + 1) * WIN],
                                          vals[:, t, h, :], start=True, stop=True)
                        last.then_inc(S["o_mm"], 1)

                    def o_T(u):
                        s, t, n = u // NT, u % NT, UT * l + u
                        pe.wait_ge(S["o_norm"], after(it, NUT, n + 1))
                        if u >= 2:
                            pe.wait_ge(S["oT_sb"], after(it, NUT, n - 1))
                        for c in range(4):
                            last = tr(bank(n % 2)[:, c * P:(c + 1) * P], o_sb[s][:, t, c * P:(c + 1) * P], ident[:, :])
                        last.then_inc(S["oT_mm"], 1)

                    def project_o(u):
                        s, t, n = u // NT, u % NT, UT * l + u
                        pe.wait_ge(S["oT_sb"], after(it, NUT, n + 1))
                        for c in range(4):
                            last = mm(bank(2 + s)[:, t * P:(t + 1) * P], oT[n % 2][:, c, :], wo[l][:, c, :],
                                      start=(c == 0), stop=(c == 3))
                        if t == 3:
                            last.then_inc(S["wo_mm"], 1)

                    def normed_T(s):
                        pe.wait_ge(S["ln_out"], after(it, NLN, ln_ffn(l, s) + 1))
                        for t in range(NT):
                            last = tr(bank(6 + s)[:, t * P:(t + 1) * P], hs[s][:, t, :], ident[:, :])
                        last.then_inc(S["hnT_mm"], 1)

                    def up_l0(m):
                        s, c, n = m // HC, m % HC, HC * unit(l, 0) + m
                        if c == 0:
                            pe.wait_ge(S["hnT_sb"], after(it, NU, unit(l, s) + 1))
                        if m >= 2:
                            pe.wait_ge(S["acted"], after(it, HC * NU, n - 1))
                        b0 = (4, 0)[m % 2]
                        for g in range(2):
                            last = mm(ps[0:HW, (b0 + g) * BANK:(b0 + g + 1) * BANK], w1[l][:, g, c, :], hnT[s],
                                      start=True, stop=True)
                        last.then_inc(S["up_mm"], 1)

                    def down_l0(s):
                        pe.wait_ge(S["acted"], after(it, HC * NU, HC * (unit(l, s) + 1)))
                        for t in range(NT):
                            for c in range(HC):
                                last = mm(bank(2 + s)[:, t * P:(t + 1) * P], act[s][:, c, t * P:(t + 1) * P],
                                          w2[l][0:HW, c, :], start=(c == 0), stop=(c == HC - 1))
                        last.then_inc(S["down_mm"], 1)

                    stream_T(0)
                    for u in range(UT):
                        project_qkv(u)
                        if u == 1:
                            stream_T(1)
                        if u >= HEADS_LAG:
                            heads_T(u - HEADS_LAG)
                    heads_T(UT - 3)
                    scores(0)
                    heads_T(UT - 2)
                    scores(1)
                    heads_T(UT - 1)
                    probs_T(0)
                    for u in range(UT):
                        if u + 2 < UT:
                            scores(u + 2)
                        if u + 1 < UT:
                            probs_T(u + 1)
                        if u == UT - 1:
                            o_T(0)
                        values(u)
                    o_T(1)
                    for u in range(UT):
                        project_o(u)
                        if u + 2 < UT:
                            o_T(u + 2)
                    normed_T(0)
                    for m in range(2 * HC):
                        up_l0(m)
                        if m == HC - 1:
                            normed_T(1)
                        if m == HC:
                            down_l0(0)
                    down_l0(1)
            pe.wait_ge(T["wv"], 1)
            pe.wait_ge(T["ones"], 3)
            ring = [(S["y_out"], after(PAIRS, NU, 0))] * 3

            def pair_of_banks(what, b, i, reader):
                at = l1_bank[what, b, i] // 2
                pe.wait_ge(*ring[at])
                ring[at] = reader
                return 2 * at

            def values1(b, i):
                hg, kt = i // 4, i % 4
                pe.wait_ge(T["ex"], 16 * b + 2 * i + 2)
                if kt == 0:
                    if b:
                        pe.wait_ge(T["att"], b)
                    if i == 0:
                        pe.wait_ge(T["v_sb"], b + 1)
                for h in range(4):
                    last = mm(ps[32 * h:32 * (h + 1), (6 + hg) * BANK:(7 + hg) * BANK],
                              v1[b % 2][:, kt, 4 * hg + h, :], pt[i % 2][:, h, :], start=(kt == 0), stop=(kt == NT - 1),
                              skip_group_check=True)
                last.then_inc(T["pv"], 1)

            for what, b, i in l1_steps():
                k = b % 3
                if what == "pre":
                    n0 = pair_of_banks(what, b, i, (T["xn_sb"], b + 1))
                    pe.wait_ge(S["ln_out"], after(PAIRS, NLN, 2 * b + 2))
                    for t in range(NT):
                        last = tr(bank(n0)[:, t * P:(t + 1) * P], z1[:, t, :], ident[:, :])
                    last.then_inc(T["xn_mm"], 1)
                if what == "qk":
                    n0 = pair_of_banks(what, b, i, (T["qk_sb"], b + 1))
                    pe.wait_ge(T["xn_sb"], b + 1)
                    mm(bank(n0), wq, xn1[:, :], start=True, stop=True)
                    mm(bank(n0 + 1), wk, xn1[:, :], start=True, stop=True).then_inc(T["qk_mm"], 1)
                if what == "val":
                    n0 = pair_of_banks(what, b, i, (T["v_sb"], b + 1))
                    for t in range(NT):
                        last = mm(bank(n0)[:, t * P:(t + 1) * P], xn1[:, t * P:(t + 1) * P], wvg, start=True, stop=True)
                    last.then_inc(T["v_mm"], 1)
                if what == "max":
                    n0 = pair_of_banks(what, b, i, (T["mx"], 16 * b + i + 1))
                    if i == 0:
                        pe.wait_ge(st_in[k], 16 * 2 * PARTS * (b // 3 + 1))
                    h = i // 2
                    for j in range(2):
                        q0 = ((i % 2) * 2 + j) * P
                        last = mm(bank(n0 + j), qst[k][0:KS, h, q0:q0 + P], kst[k][0:KS, h, :], start=True, stop=True)
                    last.then_inc(T["d_mm"], 1)
                if what == "shift":
                    n0 = pair_of_banks(what, b, i, (T["ms_sb"], b + 1))
                    pe.wait_ge(T["mx"], 16 * (b + 1))
                    tr(ps[0:H1 * NT, n0 * BANK:n0 * BANK + P], mneg[b % 2][:, :], ident[:, :]).then_inc(T["ms_mm"], 1)
                if what == "probs":
                    n0 = pair_of_banks(what, b, i, (T["ex"], 16 * b + i + 1))
                    if i == 0:
                        pe.wait_ge(sh_in[k], 16 * NSH * (b // 3 + 1))
                    kt, h0 = (i % 8) // 2, 4 * (i // 8) + 2 * (i % 2)
                    for j in range(2):
                        last = mm(bank(n0 + j), kst[k][0:KS + NSH, h0 + j, kt * P:(kt + 1) * P],
                                  qst[k][0:KS + NSH, h0 + j, :], start=True, stop=True)
                    last.then_inc(T["f_mm"], 1)
                    if i % 2 == 0 and i >= 2:
                        values1(b, i // 2 - 1)
                if what == "end":
                    values1(b, 7)
                    for hg in range(2):
                        pe.wait_ge(T["at_sb"], 2 * b + hg + 1)
                        cols = at_sb[hg].rearrange("p (r l) -> p r l", l=GRP)
                        for par in range(2):
                            for l in range(GRP):
                                dst = ps[64 * par:64 * par + 64, (6 + hg) * BANK:(6 + hg) * BANK + 16 * (VG + 1)]\
                                    .rearrange("p (j l g) -> p j l g", j=2, l=GRP)[:, :, l, :]
                                last = mm(dst, cols[:, :, l], sel[:, par, :].rearrange("p (j g) -> p j g", j=2),
                                          start=True, stop=True)
                    last.then_inc(T["sel_mm"], 1)
            pe.wait_ge(T["x3"], BATCH)
            pe.wait_ge(M["w_in"], 6 * 16)
            for b in range(BATCH):
                pe.wait_ge(S["ln_out"], after(PAIRS, NLN, 2 * BATCH + b + 1))
                if b >= 2:
                    pe.wait_ge(M["hT_sb"], b - 1)
                for t in range(NT):
                    last = tr(bank(b % 2)[:, t * P:(t + 1) * P], h_m[:, b * NT + t, :], ident[:, :])
                last.then_inc(M["hT_mm"], 1)
                pe.wait_ge(M["hT_sb"], b + 1)
                for t in range(b * NT, (b + 1) * NT):
                    last = mm(bank(7)[:, t * EXP:(t + 1) * EXP], hT_m[:, t * P:(t + 1) * P], gate_w, start=True, stop=True)
                last.then_inc(M["logits"], 1)

            def shared(b):
                for c in range(IC):
                    n = IC * b + c
                    if n >= 2:
                        pe.wait_ge(M["acted"], n - 1)
                    for z, w in enumerate((sg, su)):
                        last = mm(bank(2 + 2 * (n % 2) + z), w[:, c * P:(c + 1) * P], hT_m[:, b * SEQ:(b + 1) * SEQ],
                                  start=True, stop=True)
                    last.then_inc(M["up_mm"], 1)
                pe.wait_ge(M["acted"], IC * (b + 1))
                if b:
                    pe.wait_ge(M["x4s"], b)
                for t in range(NT):
                    for c in range(IC):
                        last = mm(bank(6)[:, t * P:(t + 1) * P], act_s[b % 2][:, c, t * P:(t + 1) * P], sd[:, c, :],
                                  start=(c == 0), stop=(c == IC - 1))
                last.then_inc(M["down_mm"], 1)

            pe.wait_ge(M["tri"], 1)
            pe.wait_ge(M["hot"], 1)
            hot_all = hot.rearrange("p t e -> p (t e)")
            mm(bank(0), tri, hot_all, start=True, stop=True, skip_group_check=True)
            for t in range(TILES - 1):
                rest = TILES - 1 - t
                mm(bank(0)[:, (t + 1) * EXP:].rearrange("p (t e) -> p t e", e=EXP), ones_b,
                   hot[:, t, :].unsqueeze(1).to_broadcast([P, rest, EXP]), start=False, stop=True,
                   skip_group_check=True)
            for t in range(TILES):
                last = mm(bank(1)[:, 0:EXP], ones_b, hot[:, t, :], start=(t == 0), stop=(t == TILES - 1))
            last.then_inc(M["rank_mm"], 1)
            for b in range(BATCH):
                shared(b)

            def tokens_T(t, i):
                pe.wait_ge(xs_in[t % AHEAD], i * 16 + 16 * (t // AHEAD + 1))
                tr(bank(t % 2)[:, 0:P], xs_in_sb[t % AHEAD], ident[:, :]).then_inc(M["xT_mm"], 1)

            def expert_of(t, i):
                return pe.value_load(exp_of[0:1, bass.ds(i * AHEAD + t, 1)], min_val=0, max_val=EXP - 1)

            def gate_up(t, i, e):
                pe.wait_ge(M["xT_sb"], i * AHEAD + t + 1)
                mm(bank(2 + t % 2), xsT[t % 2], wgu[:, bass.ds(e, 1), :].rearrange("p a n -> p (a n)"),
                   start=True, stop=True).then_inc(M["gu_mm"], 1)

            def gated_T(t, i):
                pe.wait_ge(M["r_act"], i * AHEAD + t + 1)
                for c in range(IC):
                    last = tr(bank(4 + t % 2)[:, c * P:(c + 1) * P], act_r[t % 2][:, c * P:(c + 1) * P], ident[:, :])
                last.then_inc(M["actT_mm"], 1)

            def down(t, i, e):
                pe.wait_ge(M["actT_sb"], i * AHEAD + t + 1)
                pe.wait_ge(M["y_sb"], i * AHEAD + t + 1)
                for c in range(IC):
                    last = mm(bank(6 + t % 2)[:, 0:P], actT[t % 2][:, c * P:(c + 1) * P],
                              wd[:, bass.ds(e, 1), c, :].rearrange("p a n -> p (a n)"), start=(c == 0), stop=(c == IC - 1))
                last.then_inc(M["y_mm"], 1)

            def pe_step(i, r, last):
                if not last or r + UP < AHEAD:
                    gate_up(r + UP, i, expert_of(r + UP, i))
                if not last or r + XT < AHEAD:
                    tokens_T(r + XT, i)
                if not last or r + BACK < AHEAD:
                    gated_T(r + BACK, i)
                down(r, i, expert_of(r, i))

            pe.wait_ge(M["slots"], 2)
            pe.wait_ge(M["x4s"], BATCH)
            pe.wait_ge(M["w_gu"], 16 * 16)
            pe.wait_ge(M["w_d"], 4 * 16)
            tokens_T(0, 0)
            tokens_T(1, 0)
            gate_up(0, 0, expert_of(0, 0))
            tokens_T(2, 0)
            gate_up(1, 0, expert_of(1, 0))
            gated_T(0, 0)
            experts(pe, pe_step)


def rotary_tables(np):
    f = np.float32
    half = np.arange(0, DH, 2, dtype=f)
    inv = (f(1.0) / np.power(f(10000.0), half / f(DH))).astype(f)
    t = np.arange(SEQ, dtype=f)
    fr = t[:, None] * inv[None, :]
    fr = np.concatenate([fr, fr], -1)
    base = (half + f(0.4 * DH)) / f(1.4 * DH)
    power = (t - SEQ // 2) / f(WIN // 2)
    sc = np.power(base[None, :], power[:, None]).astype(f)
    sc = np.concatenate([sc, sc], -1)
    cos, sin = np.cos(fr), np.sin(fr)
    sin = sin * np.concatenate([-np.ones(DH // 2, f), np.ones(DH // 2, f)])
    c = np.stack([cos * sc * f(8.0), cos / sc], 1)
    s = np.stack([sin * sc * f(8.0), sin / sc], 1)

    def lay(x):
        return np.ascontiguousarray(x.reshape(NT, P, 2, DH).transpose(1, 0, 2, 3).astype(f))

    return lay(c), lay(s)


def routing_constants(np):
    row = np.concatenate([EXP - np.arange(EXP), P * np.arange(TILES), np.arange(P - EXP - TILES)])
    return np.ascontiguousarray(np.broadcast_to(row.astype(np.float32), (P, P)))


def selector(np):
    sel = np.zeros((P, 2, 2, VG + 1), np.float32)
    for par in range(2):
        for j in range(2):
            for g in range(VG + 1):
                sel[32 * (2 * j + par) + g, par, j, g] = 1.0
    return sel.reshape(P, 2, 2 * (VG + 1))


def arrays_of(np, i):
    def c(a):
        return np.ascontiguousarray(a)

    tab_c, tab_s = rotary_tables(np)
    q = np.arange(P)[:, None] % WIN
    k = np.arange(P)[None, :]
    inside = (q <= k) & (k <= q + WIN)
    first = inside & ~((np.arange(P)[:, None] < WIN) & (k < WIN))
    f = np.float32
    mask = np.stack([np.where(inside, f(0), f(NEG)), np.where(first, f(0), f(NEG))], 1)
    qs, ks = np.asarray(i["L0_ffn_q_scale"]), np.asarray(i["L0_ffn_k_scale"])

    def swap(a):
        return np.concatenate([a[:, DH // 2:], a[:, :DH // 2]], -1)

    scales = np.stack([np.stack([qs, ks], 1), np.stack([swap(qs), swap(ks)], 1)], 1)
    w1, b1, w2 = (np.asarray(i["L0_ffn_" + n]) for n in ("w1", "b1", "w2"))
    w1 = np.pad(w1.reshape(LAYERS, P, 2, HID), ((0, 0),) * 3 + ((0, HC * HW - HID),)).reshape(LAYERS, P, 2, HC, HW)
    b1 = np.pad(b1.reshape(LAYERS, 2, HID), ((0, 0),) * 2 + ((0, HC * HW - HID),)).reshape(LAYERS, 2, HC, HW)
    w2 = np.pad(w2, ((0, 0), (0, HC * HW - HID), (0, 0))).reshape(LAYERS, HC, HW, P)
    return {
        "x": c(np.asarray(i["L0_attn_inputs"]).reshape(TOK, P)),
        "a": c(np.asarray(i["L0_attn_A"]).reshape(P, 1)),
        "bc": c(i["L0_attn_BC"]),
        "tab_c": tab_c, "tab_s": tab_s, "mask": c(mask.astype(f)),
        "scales": c(scales.reshape(LAYERS, 2, 2, DH)),
        "wqkv": c(i["L0_ffn_wqkv"]), "wo": c(i["L0_ffn_wo"]), "w1": c(w1), "w2": c(w2),
        "b1": c(b1.transpose(3, 0, 1, 2)), "b2": c(i["L0_ffn_b2"]),
        "wq": c(i["L1_attn_Wq"]), "wk": c(i["L1_attn_Wk"]), "wv": c(i["L1_attn_Wv"]), "bv": c(i["L1_attn_bv"]),
        "bqk": c(np.stack([np.asarray(i["L1_attn_bq"]), np.asarray(i["L1_attn_bk"])], 1)),
        "gb1": c(np.stack([np.asarray(i["L1_attn_gamma"]), np.asarray(i["L1_attn_beta"])], 1)),
        "sel": selector(np),
        "sg": c(i["L1_ffn_shared_gate_w"]), "su": c(i["L1_ffn_shared_up_w"]), "sd": c(i["L1_ffn_shared_down_w"]),
        "gate": c(i["L1_ffn_gate_w"]),
        "wgu": c(np.concatenate([np.asarray(i["L1_ffn_routed_gate_w"]), np.asarray(i["L1_ffn_routed_up_w"])], -1)
                 .transpose(1, 0, 2)),
        "wd": c(np.asarray(i["L1_ffn_routed_down_w"]).reshape(EXP, IC, P, P).transpose(2, 0, 1, 3)),
        "consts": routing_constants(np),
        "tri": c(np.triu(np.ones((P, P), np.float32), 1)),
        "ln_gb": c(np.stack([np.asarray(i["L0_ffn_ln_g"]), np.asarray(i["L0_ffn_ln_b"])], 1).transpose(2, 0, 1)),
    }


def kernel(**inputs):
    import numpy as _np
    import concourse.bacc as _bacc
    from concourse import mybir as _mybir
    from concourse.bass_utils import run_bass_kernel_spmd as _run

    nc = _bacc.Bacc("TRN2", target_bir_lowering=False, num_devices=1)
    arrays = arrays_of(_np, inputs)
    args = {n: nc.dram_tensor(f"in_{n}", a.shape, _mybir.dt.from_np(a.dtype), kind="ExternalInput").ap()
            for n, a in arrays.items()}
    out = nc.dram_tensor("out_0", (TOK, P), _mybir.dt.float32, kind="ExternalOutput").ap()
    build(nc, args, out)
    r = _run(nc, [{f"in_{n}": a for n, a in arrays.items()}], core_ids=[0])
    return r.results[0]["out_0"].reshape(BATCH, SEQ, P)
```

```python
import concourse.bass as bass
from concourse import mybir
from contextlib import ExitStack

FP = mybir.dt.float32
BF = mybir.dt.bfloat16
I32 = mybir.dt.int32
U32 = mybir.dt.uint32
ALU = mybir.AluOpType
ACT = mybir.ActivationFunctionType
AX = mybir.AxisListType

P = 128
BATCH, SEQ = 4, 512
TOK = BATCH * SEQ
NT = SEQ // P
TILES = TOK // P
PAIRS = BATCH // 2
EPS = 1e-5
BANK = 512

LAYERS, HEADS, DH, WIN = 2, 8, 64, 64
INNER = HEADS * DH
HEADS_LAG = 3
HP = HEADS // 2
HID, HC = 341, 3
HW = -(-HID // HC)
VW = DH + 1

H1, DK = 8, 16
GRP = 8
VG = P // GRP
PARTS = 6
RUNS = ((0, 0, 0, 3), (3, 0, 1, 2), (5, 0, 2, 1))
LEAD = 22
KS = PARTS * DK
NSH = 3

EXP, INTER = 32, 256
IC = INTER // P
SLOT_TILES = TILES + EXP - 1
AHEAD = 4
LOOP_TILES = -(-SLOT_TILES // AHEAD) * AHEAD
PASSES = LOOP_TILES // AHEAD
UP, XT, BACK, NUM = 2, 3, 1, 2
SLOT_ROWS = (LOOP_TILES + AHEAD) * P
ROW = P + 1
NEG = -1e30


def after(it, per_pair, n):
    return it * per_pair + max(n, 0) + 1


COUNTED = {
    "DVE": ("ln_stats", "ln_mv", "ln_out", "scanned", "x1", "hT_hi", "ssq", "root", "normed", "rot_a", "rotated",
            "smax", "diffed", "o_rec", "o_norm", "y_att", "hs_top", "acted", "y_out"),
    "Pool": ("ln_eps", "ln_rstd", "ssq_c", "newton", "rnormed", "rot_bb", "based_y", "based"),
    "ACT": ("warm", "hT_lo", "squared", "length", "v_sb", "qkT_sb", "exped", "oT_sb", "hnT_sb", "gelued"),
    "PE": ("xnT_mm", "bc_mm", "yT_mm", "qk_mm", "v_mm", "qkT_mm", "s_mm", "pT_mm", "o_mm", "oT_mm", "wo_mm", "hnT_mm",
           "up_mm", "down_mm"),
}


def build(nc, A, out):
    with ExitStack() as ctx:
        def sb(name, shape, dt=FP):
            return ctx.enter_context(nc.sbuf_tensor(name, shape, dt))

        def sem(name):
            return ctx.enter_context(nc.semaphore(name))

        region_a = sb("region_a", [P, EXP * 2 * INTER])
        region_d = sb("region_d", [P, EXP * IC * P + 88])
        region_b = sb("region_b", [P, 10400])
        region_r = sb("region_r", [P, 2 * 4096])
        used = {}

        def part(region, width, dt=FP):
            at = used.get(region.name, 0)
            used[region.name] = at + width
            assert used[region.name] <= region.shape[1], (region.name, used[region.name])
            return region[:, at:at + width]

        KZW = WIN + SEQ
        kz = [part(region_a, HP * 2 * KZW).rearrange("p (h z t) -> p h z t", h=HP, z=2) for _ in range(2)]
        v_al = [part(region_a, NT * HEADS * VW).rearrange("p (t h d) -> p t h d", t=NT, h=HEADS) for _ in range(2)]
        sq = part(region_a, 2 * INNER)
        hnT = [part(region_a, SEQ), sq[:, 0:SEQ]]
        ZEROS = 4 * ROW
        zeros = part(region_a, ZEROS)

        wqkv = [part(region_d, 3 * INNER) for _ in range(LAYERS)]
        wo = [part(region_d, 4 * P).rearrange("p (c n) -> p c n", c=4) for _ in range(LAYERS)]
        w1 = [part(region_d, 2 * HC * HW).rearrange("p (g c n) -> p g c n", g=2, c=HC) for _ in range(LAYERS)]
        w2 = [part(region_d, HC * P).rearrange("p (c n) -> p c n", c=HC) for _ in range(LAYERS)]
        tab_c, tab_s = (part(region_d, LAYERS * NT * 2 * DH).rearrange("p (l t z d) -> p l t z d", l=LAYERS, t=NT, z=2)
                        for _ in range(2))

        qT = [part(region_b, HP * SEQ).rearrange("p (h t) -> p h t", h=HP) for _ in range(2)]
        v_off = [part(region_b, NT * HEADS * VW).rearrange("p (t h d) -> p t h d", t=NT, h=HEADS) for _ in range(2)]
        sdiff = [part(region_b, HEADS * P).rearrange("p (h k) -> p h k", h=HEADS) for _ in range(2)]

        rot = [region_r[:, i * 2 * INNER:(i + 1) * 2 * INNER] for i in range(HEADS_LAG)]
        qn = [region_r[:, (HEADS_LAG + i) * 2 * INNER:(HEADS_LAG + 1 + i) * 2 * INNER] for i in range(2)]
        o_sb = [region_r[:, s * 4096:s * 4096 + 2048].rearrange("p (t n) -> p t n", t=NT) for s in range(2)]
        act = [region_r[0:HW, s * 4096 + 2048:s * 4096 + 3584].rearrange("p (c t) -> p c t", c=HC) for s in range(2)]
        hs = [region_r[:, s * 4096 + 3584:(s + 1) * 4096].rearrange("p (t n) -> p t n", t=NT) for s in range(2)]

        xr = sb("xr", [P, TILES, P])
        y = [sb(f"y{s}", [P, NT, P]) for s in range(2)]
        hT = [sb(f"hT{s}", [P, SEQ]) for s in range(2)]
        pts = [sb(f"pts{i}", [P, HEADS, P]) for i in range(2)]
        hT_scan = [pts[s][:, 0:4, :].rearrange("p h q -> p (h q)") for s in range(2)]
        rot_b = sb("rot_b", [P, 2 * INNER])
        rotb = [rot_b[:, :], region_r[:, 5 * 2 * INNER:6 * 2 * INNER]]
        oT = [sb(f"oT{i}", [P, 4, P]) for i in range(2)]
        ybase = rot_b[:, 0:SEQ].rearrange("p (t c) -> p t c", t=NT)
        gel = rot_b[0:HW, SEQ:2 * SEQ]
        ident = sb("ident", [P, P])
        ident_b = sb("ident_b", [P, P], BF)
        mask_b = sb("mask_b", [P, 2, P], BF)
        a_col = sb("a_col", [P, 1])
        bc_w = sb("bc_w", [P, P])
        ln_gb = sb("ln_gb", [P, LAYERS, 2])
        b1 = sb("b1", [HW, LAYERS, 2, HC])
        b2 = sb("b2", [P, LAYERS, P])
        stats = [sb(f"stats{i}", [P, NT, 6]) for i in range(2)]
        mv = [sb(f"mv{i}", [P, NT, 2]) for i in range(2)]
        rstd = [sb(f"rstd{i}", [P, NT]) for i in range(2)]
        ssum = sb("ssum", [P, 2 * HEADS])
        ssum_c = sb("ssum_c", [P, 2 * HEADS])
        var_eps = [sb(f"var_eps{i}", [P, NT]) for i in range(2)]
        eps = sb("eps", [P, NT])
        neg_half = sb("neg_half", [P, 2 * HEADS])
        rnorm = sb("rnorm", [P, 2 * HEADS])
        length = part(region_a, 2 * HEADS)
        root = part(region_a, 2 * HEADS)
        newton = part(region_a, 2 * HEADS)
        warm = part(region_a, 1)
        smx = [sb(f"smx{i}", [P, HEADS]) for i in range(2)]
        orec = [sb(f"orec{i}", [P, 2, 4]) for i in range(2)]

        V1_AT = 28 * 2 * INTER
        def stack(region, at):
            return region[:, at:at + H1 * SEQ // 2].bitcast(BF).rearrange("p (h t) -> p h t", h=H1)

        half_st = H1 * SEQ // 2
        qst = [stack(region_b, 0), stack(region_b, half_st), stack(region_r, 0)]
        kst = [stack(region_b, 2 * half_st), stack(region_b, 3 * half_st), stack(region_r, half_st)]
        pt = [region_r[:, 4096 + i * 2048:4096 + (i + 1) * 2048].rearrange("p (h t) -> p h t", h=4) for i in range(2)]
        qk_parts = [region_b[:, 4 * half_st + i * 768:4 * half_st + (i + 1) * 768].bitcast(BF)
                    .rearrange("p (r t) -> p r t", r=3) for i in range(2)]
        wq, wk, wvg, bvg = (part(region_a, P) for _ in range(4))
        wv_raw, bv_raw = region_r[:, 2048:3072], region_r[:, 3072:4096]
        z1, xn1 = y[0], hT[0]
        qk_f = [pts[0][:, i * 4:(i + 1) * 4, :].rearrange("p h q -> p (h q)") for i in range(2)]
        v1 = [pts[1][:, :, :].rearrange("p h q -> p (h q)").rearrange("p (t h g) -> p t h g", t=NT, h=H1),
              rot_b[:, :].rearrange("p (t h g) -> p t h g", t=NT, h=H1),
              region_a[:, V1_AT:V1_AT + 1024].rearrange("p (t h g) -> p t h g", t=NT, h=H1)]
        at_sb = [oT[i][:, :, :].rearrange("p c t -> p (c t)") for i in range(2)]
        att = y[1]
        ones_f = sb("ones_f", [P, EXP])
        sel = sb("sel", [P, 2, 2 * (VG + 1)])
        ones_row = hT[1][0:NSH, 320:320 + P // 2].bitcast(BF)
        gate_w = hT[1][:, 384:384 + EXP]
        gb1 = sb("gb1", [P, 2])
        bqk = sb("bqk", [P, 2])
        mneg = [sb(f"mneg{i}", [P, H1 * NT]) for i in range(2)]
        shift_r = hT[1][0:H1 * NT, 0:P]
        shift_p = hT[1][0:H1 * NT, P:P + NSH * P // 2].bitcast(BF).rearrange("p (r t) -> p r t", r=NSH)
        arec = sb("arec", [P, 2, 16])

        def part_of(z, r):
            return qk_parts[z][:, 2 - r if z else r, :]

        parts_dram = nc.dram_tensor("parts_dram", (2, 3, P, SEQ), BF).ap()

        wgu = region_a[:, :].rearrange("p (e n) -> p e n", e=EXP)
        wd = region_d[:, 0:EXP * IC * P].rearrange("p (e c n) -> p e c n", e=EXP, c=IC)
        rows_m = region_b[:, half_st:half_st + TILES * ROW].rearrange("p (t c) -> p t c", t=TILES)
        h_m = rows_m[:, :, 0:P]
        hT_m = region_b[:, 3 * half_st:4 * half_st]
        sg, su = region_r[:, 0:256], region_r[:, 256:512]
        sd = region_r[:, 512:768].rearrange("p (c n) -> p c n", c=IC)
        consts, tri_f = region_r[:, 768:896 + TILES], region_r[:, 896 + TILES:1024 + TILES]
        tri = region_r[:, 1040:1104].bitcast(BF)
        ones_b = region_r[:, 1104:1168].bitcast(BF)
        slot_id = region_r[:, 1168:1168 + AHEAD].bitcast(U32)
        hot = region_r[:, 1184:1440].bitcast(BF).rearrange("p (t e) -> p t e", t=TILES)
        silu_s = qk_f
        act_s = [region_b[:, at:at + 1024].rearrange("p (c t) -> p c t", c=IC) for at in (5120, 9344)]
        y_g = region_b[:, 0:2048].rearrange("p (t c) -> p t c", t=TILES)
        m1, m2 = region_r[:, 2048:2560], region_r[:, 2560:3072]
        m3 = region_r[0:1, 3072:3072 + (LOOP_TILES + AHEAD) * EXP]
        rows_in = [pts[1][:, :, :].rearrange("p h q -> p (h q)")[:, i * ROW:(i + 1) * ROW] for i in range(AHEAD)]
        xs_in_sb = [rows_in[i][:, 0:P] for i in range(AHEAD)]
        xsT = [region_r[:, 5632 + i * P:5632 + (i + 1) * P] for i in range(2)]
        silu_r = [region_r[:, 5888 + i * INTER:5888 + (i + 1) * INTER] for i in range(2)]
        act_r = [region_r[:, 6400 + i * INTER:6400 + (i + 1) * INTER] for i in range(2)]
        actT = [region_r[:, 6912 + i * INTER:6912 + (i + 1) * INTER] for i in range(2)]
        ys = [region_r[:, 7424 + i * P:7424 + (i + 1) * P] for i in range(AHEAD)]
        warm2 = hT[1][:, 448:449]
        rmax, rev2, esc, score, slot_f = (region_b[:, 8608 + i * TILES:8608 + (i + 1) * TILES] for i in range(5))
        slot_i = region_b[:, 8688:8704].bitcast(U32)
        ntile, incl, base_e = (region_b[:, 8704 + i * EXP:8704 + (i + 1) * EXP] for i in range(3))
        exp_of_f = region_b[0:1, 8800:8800 + LOOP_TILES + AHEAD]
        exp_of = region_b[0:1, 8864:8864 + LOOP_TILES + AHEAD].bitcast(I32)
        xs_dram = nc.dram_tensor("xs_dram", (SLOT_ROWS, ROW), FP).ap()
        y_dram = nc.dram_tensor("y_dram", (AHEAD + TOK, P), FP).ap()

        base_c = region_r[:, 0:NT * 2 * DH].rearrange("p (t z d) -> p t z d", t=NT, z=2)
        base_s = region_r[:, 512:1024].rearrange("p (t z d) -> p t z d", t=NT, z=2)
        scales = region_r[:, 1024:1024 + LAYERS * 4 * DH].rearrange("p (l c z d) -> p l c z d", l=LAYERS, c=2, z=2)
        mask_f = region_r[:, 2048:2048 + 2 * P].rearrange("p (m k) -> p m k", m=2)

        ps = ctx.enter_context(nc.psum_tensor("ps", [P, 8 * BANK], FP))

        def bank(n, width=BANK, of=1):
            return ps[:, n * BANK:n * BANK + width * of]

        S = {n: sem(n) for n in (
            "x_in", "small_in", "warm", "ones_f", "w_in", "tabs", "idn", "zero_p",
            "ln_turn", "norm_turn", "v_turn", "ln_stats", "ln_mv", "ln_eps", "ln_rstd", "ln_out",
            "xnT_mm", "scanned", "bc_mm", "x1", "yT_mm", "hT_lo", "hT_hi",
            "qk_mm", "v_mm", "squared", "ssq", "ssq_c", "length", "root", "newton", "rnormed", "normed", "rot_a", "rot_bb", "rotated",
            "v_sb", "qkT_mm", "qkT_sb", "s_mm", "smax", "diffed", "pT_mm", "exped", "o_mm",
            "o_rec", "o_norm", "oT_mm", "oT_sb", "wo_mm", "y_att", "hs_top", "based_y", "based", "hnT_mm", "hnT_sb",
            "up_mm", "gelued", "acted", "down_mm", "y_out", "stored")}
        v_off_in = [sem(f"v_off_in{s}") for s in range(2)]
        hs_in = [sem(f"hs_in{s}") for s in range(2)]
        T = {n: sem("l1_" + n) for n in (
            "w_in", "wv_in", "wv", "q_bias", "vv", "ones_row", "zero", "ones", "xn_mm", "xn_sb", "qk_mm", "v_mm", "v_sb", "part", "rest", "parts", "stored",
            "d_mm", "mx", "ms_mm", "ms_part", "ms_sb", "f_mm", "ex", "pv", "at_sb", "sel_mm", "rec", "att", "x3")}
        st_in = [sem(f"l1_st_in{i}") for i in range(3)]
        sh_in = [sem(f"l1_sh_in{i}") for i in range(3)]
        M = {n: sem("moe_" + n) for n in (
            "zeros", "zeroed", "w_gu", "w_d", "w_in", "w_gate", "lg_used", "tri", "hT_mm", "hT_sb", "logits", "step", "rmax", "esc", "hot", "ranked",
            "rank_mm", "slots", "scaled", "up_mm", "silu", "acted", "down_mm", "x4s", "scattered",
            "sp_turn", "pool_turn", "ids", "xT_mm", "xT_sb", "gu_mm", "r_silu", "r_act", "actT_mm", "actT_sb", "y_mm", "y_sb", "x4")}
        xs_in = [sem(f"moe_xs_in{i}") for i in range(AHEAD)]
        gathered = [sem(f"moe_gathered{i}") for i in range(BATCH)]
        ys_out = [sem(f"moe_ys_out{i}") for i in range(AHEAD)]
        block = ctx.enter_context(nc.Block())

        def experts(engine, step):
            for r in range(AHEAD):
                step(0, r, False)
            with engine.Fori(1, PASSES - 1) as i:
                for r in range(AHEAD):
                    step(i, r, False)
            for r in range(AHEAD):
                step(PASSES - 1, r, True)

        def l1_steps():
            n = BATCH * 16
            for what, b in (("stat", 0), ("stat", 1), ("apply", 0), ("pre", 0), ("qk", 0), ("split", 0), ("load", 0),
                            ("apply", 1), ("sums", 0), ("val", 0), ("pre", 1), ("stat", 2), ("qk", 1), ("val", 1),
                            ("split", 1), ("load", 1), ("apply", 2), ("pre", 2)):
                yield what, b, 0
            early = {0: (("stat", 3),), 1: (("qk", 2),), 3: (("val", 2), ("apply", 3)), 4: (("split", 2),),
                     5: (("load", 2),), 8: (("pre", 3),), 10: (("qk", 3),), 12: (("split", 3),)}
            late = {17: (("load", 3), ("val", 3)), 50: (("rstat", 0),), 52: (("rapply", 0), ("rstat", 1)),
                    53: (("rpre", 0),), 54: (("rapply", 1), ("rstat", 2)), 55: (("rpre", 1), ("route", 0)),
                    57: (("rapply", 2), ("route", 1)), 58: (("rpre", 2), ("scale", 0)),
                    60: (("route", 2), ("scale", 1)), 62: (("scale", 2),)}
            for m in range(LEAD):
                yield "max", m // 16, m % 16
                if m == 16:
                    yield "shift", 0, 0
                for what, b in early.get(m, ()):
                    yield what, b, 0
            for g in range(n):
                yield "probs", g // 16, g % 16
                m = g + LEAD
                if m < n:
                    yield "max", m // 16, m % 16
                if m % 16 == 0 and 16 < m <= n:
                    yield "shift", m // 16 - 1, 0
                if g % 16 == 1 and g > 16:
                    yield "end", g // 16 - 1, 0
                for what, b in late.get(g, ()):
                    yield what, b, 0
            last = BATCH - 1
            for step in (("end", last, 0), ("s_up", 0, 0), ("rstat", last, 0), ("rank", 0, 0), ("rapply", last, 0),
                         ("rpre", last, 0), ("s_up", 0, 1), ("route", last, 0), ("s_down", 0, 0)):
                yield step

        SHARED_EARLY = IC

        def up_banks(n):
            return 2 + 2 * (n % 2) if n >= SHARED_EARLY else l1_bank["s_up", n // IC, n % IC]

        l1_bank, turn = {}, 0
        for what, b, i in l1_steps():
            if what in ("pre", "qk", "val", "max", "shift", "probs", "rpre", "route", "s_up"):
                l1_bank[what, b, i] = 2 * (turn % 3)
                turn += 1

        def unit(l, s):
            return 2 * l + s

        def ut(l, s, t):
            return 4 * unit(l, s) + t

        UT = 2 * NT
        NU, NUT = 2 * LAYERS, UT * LAYERS
        NLN = 2 + 2 * LAYERS

        def ln_ffn(l, s):
            return 2 + 2 * l + s

        def norms(it, n):
            return it * NLN + max(n + BATCH, 0) + 1

        def z_pad(v):
            return v[:, :, :, :].rearrange("p t h g -> p (t h g)")

        def xr_tiles(it, s):
            return xr[:, bass.ds(it * (2 * NT) + s * NT, NT), :]

        @block.sync
        def _(sp):
            sp.dma_start(xr[:, :, :], A["x"].rearrange("(t p) c -> p t c", p=P)).then_inc(S["x_in"], 16)
            loads = [(a_col[:, :], A["a"]), (bc_w[:, :], A["bc"]), (base_c, A["tab_c"]), (base_s, A["tab_s"]),
                     (mask_f, A["mask"]), (ln_gb[:, :, :], A["ln_gb"]), (b1[:, :, :, :], A["b1"])]
            for dst, src in loads:
                sp.dma_start(dst, src).then_inc(S["small_in"], 16)
            sp.dma_start(scales, A["scales"].partition_broadcast(P)).then_inc(S["small_in"], 16)
            sp.dma_start(b2[:, :, :], A["b2"].partition_broadcast(P)).then_inc(S["small_in"], 16)
            for l in range(LAYERS):
                sp.dma_start(wqkv[l], A["wqkv"][l, :, :]).then_inc(S["w_in"], 16)
                sp.dma_start(wo[l], A["wo"][l, :, :].rearrange("(c p) n -> p c n", p=P)).then_inc(S["w_in"], 16)
                sp.dma_start(w1[l], A["w1"][l, :, :, :, :]).then_inc(S["w_in"], 16)
                sp.dma_start(w2[l][0:HW], A["w2"][l, :, :, :].rearrange("c p n -> p c n")).then_inc(S["w_in"], 16)
            for dst, src in ((wq, A["wq"]), (wk, A["wk"]), (gb1[:, :], A["gb1"]), (bqk[:, :], A["bqk"]),
                             (sel[:, :, :], A["sel"])):
                sp.dma_start(dst, src).then_inc(T["w_in"], 16)
            sp.wait_ge(M["zeros"], 1)
            n_z = SLOT_ROWS // P * ROW // ZEROS
            sp.dma_start(xs_dram.rearrange("(p r) c -> p (r c)", p=P).rearrange("p (n z) -> p n z", z=ZEROS),
                         zeros.unsqueeze(1).to_broadcast([P, n_z, ZEROS])).then_inc(M["zeroed"], 16)
            with sp.Fori(0, PAIRS) as it:
                for l in range(LAYERS):
                    for s in range(2):
                        sp.wait_ge(S["v_sb"], after(it, NUT, ut(l, s, 3) + 1))
                        sp.sem_inc(S["v_turn"], 1)
                        sp.wait_ge(S["o_mm"], after(it, NUT, ut(l, s, 3) + 1 - 2 * NT))
                        sp.dma_start(v_off[s][0:WIN, 1:NT], v_al[s][WIN:P, 0:NT - 1]).then_inc(v_off_in[s], 16)
                        sp.dma_start(v_off[s][WIN:P, :], v_al[s][0:WIN, :]).then_inc(v_off_in[s], 16)
                    for s in range(2):
                        sp.wait_ge(S["y_att"], after(it, NU, unit(l, s) + 1))
                        h = P // 2
                        sp.dma_start(hs[s][1:P, :, h:P], y[s][0:P - 1, :, h:P]).then_inc(hs_in[s], 16)
                        sp.dma_start(hs[s][0:1, 1:NT, h:P], y[s][P - 1:P, 0:NT - 1, h:P]).then_inc(hs_in[s], 16)
            sp.wait_ge(S["y_out"], after(PAIRS, NU, 0))
            sp.dma_start(wv_raw, A["wv"]).then_inc(T["wv_in"], 16)
            sp.dma_start(bv_raw, A["bv"].partition_broadcast(P)).then_inc(T["wv_in"], 16)
            def ones_under(k):
                rows = kst[k][KS:KS + NSH, :, :].rearrange("p h (n t) -> p (h n) t", t=P)
                sp.dma_start(rows, ones_row.unsqueeze(1).to_broadcast([NSH, H1 * NT, P])).then_inc(T["ones"], 16)

            sp.wait_ge(T["ones_row"], 1)
            ones_under(0)
            ones_under(1)
            sp.dma_start(gate_w, A["gate"]).then_inc(M["w_gate"], 16)
            sp.wait_ge(M["zeroed"], 16)
            gu_chunks = [("gu", 2 * c) for c in range(EXP // 2)]
            chunks = gu_chunks[:14] + [("down", 8 * c) for c in range(4)] + gu_chunks[14:]
            for what, b, i in l1_steps():
                k, g = b % 3, 16 * b + i
                if what == "probs" and g % 3 == 1 and chunks:
                    kind, e0 = chunks.pop(0)
                    sp.wait_ge(T["ex"], g)
                    if (kind, e0) == ("gu", 28):
                        sp.wait_ge(T["pv"], 8 * (BATCH - 1))
                        sp.wait_ge(T["v_sb"], BATCH)
                    if kind == "gu":
                        sp.dma_start(wgu[:, e0:e0 + 2, :], A["wgu"][:, e0:e0 + 2, :]).then_inc(M["w_gu"], 16)
                    else:
                        sp.dma_start(wd[:, e0:e0 + 8, :, :], A["wd"][:, e0:e0 + 8, :, :]).then_inc(M["w_d"], 16)
                if what == "probs" and g == 48:
                    sp.wait_ge(T["f_mm"], 48)
                    for dst, src in ((consts, A["consts"]), (tri_f, A["tri"]), (sg, A["sg"]), (su, A["su"]),
                                     (sd, A["sd"].rearrange("(c p) n -> p c n", p=P))):
                        sp.dma_start(dst, src).then_inc(M["w_in"], 16)
                if what == "load" and b == 2:
                    sp.wait_ge(T["wv"], 1)
                    ones_under(2)
                if what == "split":
                    if b:
                        sp.wait_ge(st_in[(b - 1) % 3], 16 * 2 * len(RUNS) * ((b - 1) // 3 + 1))
                    for z in range(2):
                        sp.wait_ge(T["parts"], 2 * b + z + 1)
                        sp.dma_start(parts_dram[z, :, :, :].rearrange("r p t -> p r t"), qk_parts[z]).then_inc(T["stored"], 16)
                if what == "load":
                    sp.wait_ge(T["stored"], 32 * (b + 1))
                    if b >= 3:
                        sp.wait_ge(T["f_mm"], 16 * (b - 2))
                    for row, at_q, at_k, n in RUNS:
                        for z, (st, at) in enumerate(((qst, at_q), (kst, at_k))):
                            sp.dma_start(st[k][row * DK:(row + n) * DK, :, :],
                                         parts_dram[z, at:at + n, :, :].rearrange("r (d h) t -> (r d) h t", h=H1))\
                              .then_inc(st_in[k], 16)
                if what == "shift":
                    sp.wait_ge(T["ms_sb"], b + 1)
                    for j in range(NSH):
                        sp.dma_start(qst[k][KS + j:KS + j + 1, :, :].rearrange("p h (q t) -> p (h q) t", q=NT),
                                     shift_p[:, j, :]).then_inc(sh_in[k], 16)
            sp.wait_ge(M["scattered"], 16 * TILES)
            for r in range(AHEAD):
                sp.dma_start(rows_in[r], xs_dram[r * P:(r + 1) * P, :]).then_inc(xs_in[r], 16)

            def refill(t, j):
                sp.wait_ge(M["xT_mm"], j + 1)
                if not isinstance(j, int):
                    sp.sem_inc(M["sp_turn"], 1)
                sp.wait_ge(M["ids"], j + 1)
                if not isinstance(j, int):
                    sp.sem_inc(M["sp_turn"], 1)
                sp.dma_start(rows_in[t], xs_dram[bass.ds((j + AHEAD) * P, P), :]).then_inc(xs_in[t], 16)

            def sp_step(i, r, last):
                if not last:
                    refill((r + NUM) % AHEAD, i * AHEAD + r + NUM)

            for t in range(NUM):
                refill(t, t)
            experts(sp, sp_step)
            for r in range(AHEAD):
                sp.wait_ge(ys_out[r], 16 * PASSES)
            for b in range(BATCH):
                rows = y_dram[AHEAD + b * SEQ:AHEAD + (b + 1) * SEQ, :].rearrange("(t p) c -> p t c", p=P)
                sp.dma_start(y_g[:, b * NT:(b + 1) * NT, :], rows).then_inc(gathered[b], 16)
            for b in range(BATCH):
                sp.wait_ge(M["x4"], b + 1)
                rows = out[b * SEQ:(b + 1) * SEQ, :].rearrange("(t p) c -> p t c", p=P)
                sp.dma_start(rows, xr[:, b * NT:(b + 1) * NT, :]).then_inc(S["stored"], 16)
            for r in range(AHEAD):
                sp.wait_ge(xs_in[r], 16 * (PASSES + (r < NUM)))
            sp.wait_ge(S["stored"], 16 * BATCH)

        @block.gpsimd
        def _(pool):
            g = nc.gpsimd
            for name in COUNTED["Pool"]:
                pool.sem_inc(S[name], 1)
            g.memset(zeros, 0.0).then_inc(M["zeros"], 1)
            g.memset(ident[:, :], 0.0).then_inc(S["idn"], 1)
            pool.wait_ge(S["idn"], 1)
            g.affine_select(out=ident[:, :], in_=ident[:, :], compare_op=ALU.not_equal, fill=1.0,
                            base=0, pattern=[[-1, P]], channel_multiplier=1).then_inc(S["idn"], 1)
            g.memset(eps[:, :], EPS)
            g.memset(neg_half[:, :], -0.5).then_inc(S["idn"], 1)
            pool.wait_ge(S["idn"], 3)
            def power(it, n):
                pool.wait_ge(S["ln_mv"], norms(it, n + 1))
                g.tensor_tensor(var_eps[n % 2][:, :], mv[n % 2][:, :, 1], eps[:, 0:NT], ALU.add).then_inc(S["ln_eps"], 1)
                pool.wait_ge(S["ln_eps"], norms(it, n + 1))
                g.tensor_tensor(rstd[n % 2][:, :], var_eps[n % 2][:, :], neg_half[:, 0:NT], ALU.pow)\
                 .then_inc(S["ln_rstd"], 1)

            for b in range(BATCH):
                power(0, b - BATCH)
                if b == 1:
                    g.memset(kz[0].rearrange("p h z t -> p (h z t)"), 0.0).then_inc(S["zero_p"], 1)
            g.memset(kz[1].rearrange("p h z t -> p (h z t)"), 0.0).then_inc(S["zero_p"], 1)
            for s in range(2):
                g.memset(v_off[s].rearrange("p t h d -> p (t h d)"), 0.0).then_inc(S["zero_p"], 1)
                g.memset(v_al[s][:, :, :, DH:VW], 1.0).then_inc(S["zero_p"], 1)
            pool.wait_ge(S["zero_p"], 6)
            with pool.Fori(0, PAIRS) as it:
                for s in range(2):
                    power(it, s)
                for l in range(LAYERS):
                    def clamp(u):
                        n = UT * l + u
                        pool.wait_ge(S["ssq"], after(it, NUT, n + 1))
                        pool.sem_inc(S["norm_turn"], 1)
                        g.tensor_scalar(ssum_c[:, :], ssum[:, :], 1e-24, None, ALU.max).then_inc(S["ssq_c"], 1)

                    def refine(u):
                        n = UT * l + u
                        pool.wait_ge(S["root"], after(it, NUT, n + 1))
                        g.tensor_tensor(newton, root, root, ALU.mult).then_inc(S["newton"], 1)
                        pool.wait_ge(S["newton"], after(it, 3 * NUT, 3 * n + 1))
                        g.tensor_tensor(newton, newton, ssum_c[:, :], ALU.mult).then_inc(S["newton"], 1)
                        pool.wait_ge(S["newton"], after(it, 3 * NUT, 3 * n + 2))
                        pool.sem_inc(S["norm_turn"], 1)
                        g.tensor_scalar(newton, newton, -0.5, 1.5, ALU.mult, ALU.add).then_inc(S["newton"], 1)
                        pool.wait_ge(S["newton"], after(it, 3 * NUT, 3 * n + 3))
                        g.tensor_tensor(rnorm[:, :], newton, root, ALU.mult).then_inc(S["rnormed"], 1)

                    def rotate_half(u, half):
                        t, n = u % NT, UT * l + u
                        src = qn[n % 2].rearrange("p (z h j d) -> p z h j d", z=2, h=HEADS, j=2)[:, :, :, 1 - half, :]
                        dst = rotb[n % 2].rearrange("p (z h j d) -> p z h j d", z=2, h=HEADS, j=2)[:, :, :, half, :]
                        tab = tab_s[:, l, t, :, half * 32:half * 32 + 32].unsqueeze(2).to_broadcast([P, 2, HEADS, 32])
                        g.tensor_tensor(dst, src, tab, ALU.mult).then_inc(S["rot_bb"], 1)

                    clamp(0)
                    refine(0)
                    for u in range(UT):
                        n = UT * l + u
                        pool.wait_ge(S["normed"], after(it, NUT, n + 1))
                        pool.sem_inc(S["norm_turn"], 1)
                        pool.wait_ge(S["rotated"], after(it, NUT, n - 1))
                        rotate_half(u, 0)
                        if u + 1 < UT:
                            clamp(u + 1)
                            refine(u + 1)
                        rotate_half(u, 1)
                    for s in range(2):
                        power(it, ln_ffn(l, s))
                        pool.wait_ge(S["y_out"], after(it, NU, unit(l, s)))
                        pool.wait_ge(S["y_att"], after(it, NU, unit(l, s) + 1))
                        bb = b2[:, l, :].unsqueeze(1).to_broadcast([P, NT, P])
                        last = g.tensor_tensor(ybase[:, :, :], y[s][:, :, :], bb, ALU.add)
                        if l == LAYERS - 1:
                            last.then_inc(S["based_y"], 1)
                            pool.wait_ge(S["based_y"], after(it, 2, s + 1))
                            last = g.tensor_tensor(ybase[:, :, :], ybase[:, :, :], xr_tiles(it, s), ALU.add)
                        last.then_inc(S["based"], 1)

            pool.wait_ge(S["y_out"], after(PAIRS, NU, 0))
            for what, b, i in l1_steps():
                if what == "stat":
                    n = b
                    pool.wait_ge(S["ln_mv"], norms(PAIRS, n + 1))
                    g.tensor_tensor(var_eps[n % 2][:, :], mv[n % 2][:, :, 1], eps[:, 0:NT], ALU.add).then_inc(T["vv"], 1)
                    pool.wait_ge(T["vv"], 2 * b + 1)
                    g.tensor_tensor(var_eps[n % 2][:, :], var_eps[n % 2][:, :], eps[:, 0:NT], ALU.mult).then_inc(T["vv"], 1)
                    pool.wait_ge(T["vv"], 2 * b + 2)
                    g.tensor_tensor(var_eps[n % 2][:, :], var_eps[n % 2][:, :], mv[n % 2][:, :, 1], ALU.add).then_inc(S["ln_eps"], 1)
                    pool.wait_ge(S["ln_eps"], norms(PAIRS, n + 1))
                    g.tensor_tensor(rstd[n % 2][:, :], var_eps[n % 2][:, :], neg_half[:, 0:NT], ALU.pow).then_inc(S["ln_rstd"], 1)
                if (what, b) == ("stat", 0):
                    g.memset(ones_row, 1.0).then_inc(T["ones_row"], 1)
                    for k in range(3):
                        if k == 2:
                            pool.wait_ge(M["zeroed"], 16)
                        g.memset(z_pad(v1[k]), 0.0).then_inc(T["zero"], 1)
                    pool.wait_ge(T["zero"], 3)
                    for k in range(3):
                        g.memset(v1[k][:, :, :, VG:VG + 1], 1.0).then_inc(T["zero"], 1)
                if what == "split":
                    for z in range(2):
                        pool.wait_ge(T["part"], 4 * b + z + 1)
                        g.tensor_tensor(qk_f[z], qk_f[z], part_of(z, 0), ALU.subtract).then_inc(T["rest"], 1)
                    for z in range(2):
                        pool.wait_ge(T["part"], 4 * b + z + 3)
                        g.tensor_tensor(part_of(z, 2), qk_f[z], part_of(z, 1), ALU.subtract).then_inc(T["parts"], 1)
                if what == "rstat":
                    power(PAIRS, BATCH + b)

            pool.wait_ge(M["slots"], 1)
            pool.wait_ge(M["scaled"], BATCH)
            pool.wait_ge(M["zeroed"], 16)
            for t in range(TILES):
                g.indirect_dma_start(out=xs_dram[:, :], out_offset=bass.IndirectOffsetOnAxis(ap=slot_i[:, t:t + 1], axis=0),
                                     in_=rows_m[:, t, :], in_offset=None).then_inc(M["scattered"], 16)

            def number(t, i):
                pool.wait_ge(xs_in[t % AHEAD], i * 16 + 16 * (t // AHEAD + 1))
                pool.sem_inc(M["pool_turn"], 1)
                g.tensor_scalar(slot_id[:, t % AHEAD:t % AHEAD + 1], rows_in[t % AHEAD][:, P:ROW], float(t % AHEAD), None,
                                ALU.max).then_inc(M["ids"], 1)

            for t in range(NUM):
                number(t, 0)

            def pool_step(i, r, last):
                if r >= 2 or not isinstance(i, int) or i:
                    pool.wait_ge(ys_out[(r - 2) % AHEAD], i * 16 + 16 * (r >= 2))
                    pool.sem_inc(M["pool_turn"], 1)
                if not last or r + NUM < AHEAD:
                    number(r + NUM, i)
                pool.wait_ge(M["ids"], i * AHEAD + r + 1)
                pool.sem_inc(M["pool_turn"], 1)
                pool.wait_ge(M["y_sb"], i * AHEAD + r + 3)
                pool.sem_inc(M["pool_turn"], 1)
                g.indirect_dma_start(out=y_dram[:, :],
                                     out_offset=bass.IndirectOffsetOnAxis(ap=slot_id[:, r:r + 1], axis=0),
                                     in_=ys[r], in_offset=None).then_inc(ys_out[r], 16)

            experts(pool, pool_step)

        @block.scalar
        def _(a):
            act_ = nc.scalar.activation
            for name in COUNTED["ACT"]:
                a.sem_inc(S[name], 1)
            a.wait_ge(S["small_in"], 9 * 16)
            a.wait_ge(S["ones_f"], 1)
            with a.Fori(0, PAIRS) as it:
                for l in range(LAYERS):
                    def load_table(function, k):
                        n = 3 * l + k
                        a.wait_ge(S["warm"], after(it, 3 * LAYERS, n))
                        act_(warm, ones_f[:, 0:1], function).then_inc(S["warm"], 1)

                    def lower_half(s):
                        a.wait_ge(S["yT_mm"], after(it, NU, unit(l, s) + 1))
                        act_(hT[s][0:64, :], ps[0:64, 5 * BANK:6 * BANK], ACT.Copy).then_inc(S["hT_lo"], 1)

                    def heads_sb(u):
                        s, t, n = u // NT, u % NT, UT * l + u
                        a.wait_ge(S["qkT_mm"], after(it, NUT, n + 1))
                        cols = slice(t * P, (t + 1) * P)
                        kcols = slice(WIN + t * P, WIN + (t + 1) * P)
                        act_(qT[s][:, :, cols], bank(6).rearrange("p (h t) -> p h t", h=HP), ACT.Copy)
                        kp = bank(7).rearrange("p (h t) -> p h t", h=HP)
                        act_(kz[s][0:64, :, 0, kcols], kp[0:64], ACT.Copy)
                        act_(kz[s][64:P, :, 1, kcols], kp[64:P], ACT.Copy).then_inc(S["qkT_sb"], 1)

                    load_table(ACT.Sqrt, 0)
                    lower_half(0)
                    for u in range(UT):
                        s, t, n = u // NT, u % NT, UT * l + u
                        a.wait_ge(S["qk_mm"], after(it, NUT, n + 1))
                        a.wait_ge(S["ssq"], after(it, NUT, n))
                        act_(sq, bank((n % 2) * 2, of=2), ACT.Square).then_inc(S["squared"], 1)
                        a.wait_ge(S["v_mm"], after(it, NUT, n + 1))
                        act_(v_al[s][:, t, :, 0:DH], bank(4).rearrange("p (h d) -> p h d", h=HEADS),
                             ACT.Copy).then_inc(S["v_sb"], 1)
                        if u == 1:
                            lower_half(1)
                        if u >= HEADS_LAG:
                            heads_sb(u - HEADS_LAG)
                        a.wait_ge(S["ssq_c"], after(it, NUT, n + 1))
                        act_(length, ssum_c[:, :], ACT.Sqrt).then_inc(S["length"], 1)
                    load_table(ACT.Exp, 1)
                    for u in range(UT - HEADS_LAG, UT):
                        heads_sb(u)
                    for u in range(UT):
                        n = UT * l + u
                        a.wait_ge(S["pT_mm"], after(it, NUT, n + 1))
                        a.wait_ge(S["o_mm"], after(it, NUT, n - 1))
                        act_(pts[n % 2].rearrange("p h q -> p (h q)"), bank(4, of=2), ACT.Exp).then_inc(S["exped"], 1)
                    load_table(ACT.Gelu, 2)
                    for s in range(2):
                        for t in range(NT):
                            n = ut(l, s, t)
                            a.wait_ge(S["oT_mm"], after(it, NUT, n + 1))
                            act_(oT[n % 2].rearrange("p c t -> p (c t)"), bank(n % 2), ACT.Copy).then_inc(S["oT_sb"], 1)
                    def normed_sb(s):
                        a.wait_ge(S["hnT_mm"], after(it, NU, unit(l, s) + 1))
                        act_(hnT[s], bank(6 + s), ACT.Identity, scale=ln_gb[:, l, 0:1],
                             bias=ln_gb[:, l, 1:2]).then_inc(S["hnT_sb"], 1)

                    normed_sb(0)
                    for m in range(2 * HC):
                        n = HC * unit(l, 0) + m
                        a.wait_ge(S["up_mm"], after(it, HC * NU, n + 1))
                        a.wait_ge(S["acted"], after(it, HC * NU, n))
                        act_(gel[:, :], ps[0:HW, ((5, 1)[m % 2]) * BANK:((5, 1)[m % 2] + 1) * BANK], ACT.Gelu,
                             bias=b1[:, l, 1, m % HC:m % HC + 1]).then_inc(S["gelued"], 1)
                        if m == HC - 1:
                            normed_sb(1)

            def silu(n):
                a.wait_ge(M["up_mm"], n + 1)
                if n >= 2:
                    a.wait_ge(M["acted"], n - 1)
                act_(silu_s[n % 2], bank(up_banks(n)), ACT.Silu).then_inc(M["silu"], 1)

            a.wait_ge(T["w_in"], 5 * 16)
            a.wait_ge(T["q_bias"], 1)
            for what, b, i in l1_steps():
                if what == "pre":
                    a.wait_ge(T["xn_mm"], b + 1)
                    if b:
                        a.wait_ge(T["v_mm"], b)
                    act_(xn1[:, :], bank(l1_bank[what, b, i]), ACT.Identity, scale=gb1[:, 0:1], bias=gb1[:, 1:2])\
                        .then_inc(T["xn_sb"], 1)
                if what == "qk":
                    if b:
                        a.wait_ge(T["parts"], 2 * b)
                        a.wait_ge(T["stored"], 32 * b)
                    for z, scale in enumerate((DK ** -0.5, 1.0)):
                        a.wait_ge(T["qk_mm"], 2 * b + z + 1)
                        src = bank(l1_bank[what, b, i] + z)
                        act_(qk_f[z], src, ACT.Identity, scale=scale, bias=bqk[:, z:z + 1])
                        last = act_(part_of(z, 0), src, ACT.Identity, scale=scale, bias=bqk[:, z:z + 1])
                        last.then_inc(T["part"], 1)
                if what == "split":
                    for z in range(2):
                        a.wait_ge(T["rest"], 2 * b + z + 1)
                        act_(part_of(z, 1), qk_f[z], ACT.Copy).then_inc(T["part"], 1)
                if (what, b) == ("split", 2):
                    a.wait_ge(S["warm"], after(PAIRS, 3 * LAYERS, 0))
                    act_(warm2, ones_f[:, 0:1], ACT.Exp)
                if what == "probs":
                    a.wait_ge(T["f_mm"], 16 * b + i + 1)
                    if 8 * b + i // 2 - 1 > 0:
                        a.wait_ge(T["pv"], 8 * b + i // 2 - 1)
                    dst = pt[(i // 2) % 2][:, (i % 2) * 2:(i % 2) * 2 + 2, :].rearrange("p h t -> p (h t)")
                    act_(dst, bank(l1_bank[what, b, i], of=2), ACT.Exp).then_inc(T["ex"], 1)
                if (what, i) == ("probs", 10) or what == "end":
                    hg = int(what == "end")
                    a.wait_ge(T["pv"], 8 * b + 4 * (hg + 1))
                    if b:
                        a.wait_ge(T["sel_mm"], b)
                    act_(at_sb[hg], bank(6 + hg), ACT.Copy).then_inc(T["at_sb"], 1)

                if what == "route":
                    a.wait_ge(M["rmax"], b + 1)
                    act_(esc[:, b * NT:(b + 1) * NT], rmax[:, b * NT:(b + 1) * NT], ACT.Exp, scale=-1.0).then_inc(M["esc"], 1)
                if what == "s_up":
                    silu(IC * b + i)
                if what == "rpre":
                    a.wait_ge(M["hT_mm"], b + 1)
                    act_(hT_m[:, b * SEQ:(b + 1) * SEQ], bank(l1_bank[what, b, i]), ACT.Copy).then_inc(M["hT_sb"], 1)

            for n in range(SHARED_EARLY, BATCH * IC):
                silu(n)

            def tokens_sb(t, j):
                a.wait_ge(M["xT_mm"], j + 1)
                if not (isinstance(j, int) and j < 2):
                    a.wait_ge(M["gu_mm"], j - 1)
                act_(xsT[t % 2], bank(t % 2)[:, 0:P], ACT.Copy).then_inc(M["xT_sb"], 1)

            def gate_sb(t, j):
                a.wait_ge(M["gu_mm"], j + 1)
                if not (isinstance(j, int) and j < 2):
                    a.wait_ge(M["r_act"], j - 1)
                act_(silu_r[t % 2], bank(2 + t % 2)[:, 0:INTER], ACT.Silu).then_inc(M["r_silu"], 1)

            def back_sb(t, j):
                a.wait_ge(M["actT_mm"], j + 1)
                if not (isinstance(j, int) and j < 2):
                    a.wait_ge(M["y_mm"], j - 1)
                act_(actT[t % 2], bank(4 + t % 2)[:, 0:INTER], ACT.Copy).then_inc(M["actT_sb"], 1)

            def act_step(i, r, last):
                for lag, do in ((XT, tokens_sb), (UP, gate_sb), (BACK, back_sb)):
                    if not last or r + lag < AHEAD:
                        do(r + lag, i * AHEAD + r + lag)

            for t in range(XT):
                tokens_sb(t, t)
            for t in range(UP):
                gate_sb(t, t)
            back_sb(0, 0)
            experts(a, act_step)

        @block.vector
        def _(v):
            d = nc.vector
            for name in COUNTED["DVE"]:
                v.sem_inc(S[name], 1)

            def norm_stats(it, n, src):
                v.sem_inc(S["ln_turn"], 1)
                v.wait_ge(S["ln_out"], norms(it, n - 1))
                v.sem_inc(S["ln_turn"], 1)
                for t in range(NT):
                    last = d.bn_stats(stats[n % 2][:, t, :], src[:, t, :])
                last.then_inc(S["ln_stats"], 1)
                v.wait_ge(S["ln_stats"], norms(it, n + 1))
                v.sem_inc(S["ln_turn"], 1)
                for t in range(NT):
                    last = d.bn_aggr(mv[n % 2][:, t, :], stats[n % 2][:, t, :])
                last.then_inc(S["ln_mv"], 1)

            def norm_apply(it, n, src, dst):
                v.wait_ge(S["ln_mv"], norms(it, n + 1))
                v.wait_ge(S["ln_rstd"], norms(it, n + 1))
                for t in range(NT):
                    last = d.tensor_scalar(dst[:, t, :], src[:, t, :], mv[n % 2][:, t, 0:1],
                                           rstd[n % 2][:, t:t + 1],
                                           ALU.subtract, ALU.mult)
                last.then_inc(S["ln_out"], 1)

            d.memset(ones_f[:, :], 1.0).then_inc(S["ones_f"], 1)
            for s in range(2):
                d.memset(hT[s][64:P, 0:1], 0.0)
            v.wait_ge(S["x_in"], 16)

            def x_of(b):
                return xr[:, b * NT:(b + 1) * NT, :]

            def front_apply(b):
                if b >= 2:
                    v.wait_ge(S["xnT_mm"], after(0, 0, b - 1))
                norm_apply(0, b - BATCH, x_of(b), y[b % 2])

            def scan(b):
                v.wait_ge(S["xnT_mm"], after(0, 0, b + 1))
                if b >= 2:
                    v.wait_ge(S["bc_mm"], after(0, 0, b - 1))
                d.tensor_tensor_scan(hT_scan[b % 2], a_col[:, 0:1].to_broadcast([P, SEQ]), bank(6 + b % 2), 0.0,
                                     ALU.mult, ALU.add).then_inc(S["scanned"], 1)

            def recurrence_out(b):
                v.wait_ge(S["bc_mm"], after(0, 0, b + 1))
                d.tensor_tensor(x_of(b), x_of(b), bank(2 + b % 2).rearrange("p (t c) -> p t c", t=NT),
                                ALU.add).then_inc(S["x1"], 1)

            def tables():
                for m in range(2):
                    d.tensor_copy(mask_b[:, m, :], mask_f[:, m, :])
                for l in range(LAYERS):
                    for z in range(2):
                        d.tensor_tensor(tab_c[:, l, :, z, :], base_c[:, :, z, :],
                                        scales[:, l, 0, z, :].unsqueeze(1).to_broadcast([P, NT, DH]), ALU.mult)
                        last = d.tensor_tensor(tab_s[:, l, :, z, :], base_s[:, :, z, :],
                                               scales[:, l, 1, z, :].unsqueeze(1).to_broadcast([P, NT, DH]), ALU.mult)
                v.wait_ge(S["idn"], 2)
                last = d.tensor_copy(ident_b[:, :], ident[:, :]).then_inc(S["tabs"], 1)
                v.wait_ge(S["tabs"], 1)

            for b0 in range(0, BATCH, 2):
                for b in (b0, b0 + 1):
                    norm_stats(0, b - BATCH, x_of(b))
                for b in (b0, b0 + 1):
                    front_apply(b)
                if b0:
                    recurrence_out(b0 - 2)
                    recurrence_out(b0 - 1)
                else:
                    v.wait_ge(S["small_in"], 9 * 16)
                for b in (b0, b0 + 1):
                    scan(b)
                if not b0:
                    tables()
            for b in (BATCH - 2, BATCH - 1):
                recurrence_out(b)
            v.wait_ge(S["x1"], after(0, 0, BATCH))
            v.wait_ge(S["xnT_mm"], after(0, 0, BATCH))
            with v.Fori(0, PAIRS) as it:
                for s in range(2):
                    norm_stats(it, s, xr_tiles(it, s))
                for s in range(2):
                    norm_apply(it, s, xr_tiles(it, s), y[s])
                for l in range(LAYERS):
                    def upper_half(s):
                        v.wait_ge(S["yT_mm"], after(it, NU, unit(l, s) + 1))
                        d.tensor_copy(hT[s][64:P, 1:SEQ], ps[64:P, 5 * BANK:6 * BANK - 1]).then_inc(S["hT_hi"], 1)

                    def squares_sum(u):
                        v.wait_ge(S["squared"], after(it, NUT, UT * l + u + 1))
                        d.tensor_reduce(ssum[:, :], sq.rearrange("p (h d) -> p h d", d=DH), AX.X, ALU.add)\
                         .then_inc(S["ssq"], 1)

                    def normalise(u):
                        t, n = u % NT, UT * l + u
                        qk = bank((n % 2) * 2, of=2)
                        v.wait_ge(S["rnormed"], after(it, NUT, n + 1))
                        v.wait_ge(S["rot_bb"], after(it, 2 * NUT, 2 * n - 2))
                        v.wait_ge(S["rot_a"], after(it, NUT, n - 1))
                        d.tensor_tensor(qn[n % 2].rearrange("p (h d) -> p h d", d=DH), qk.rearrange("p (h d) -> p h d", d=DH),
                                        rnorm[:, :].unsqueeze(2).to_broadcast([P, 2 * HEADS, DH]), ALU.mult)\
                         .then_inc(S["normed"], 1)

                    def inverse(u):
                        n = UT * l + u
                        v.wait_ge(S["length"], after(it, NUT, n + 1))
                        v.wait_ge(S["rnormed"], after(it, NUT, n))
                        d.reciprocal(root, length).then_inc(S["root"], 1)

                    def scale_cos(u):
                        t, n = u % NT, UT * l + u
                        v.wait_ge(S["normed"], after(it, NUT, n + 1))
                        v.wait_ge(S["qkT_mm"], after(it, NUT, n - 2))
                        d.tensor_tensor(rot[u % HEADS_LAG].rearrange("p (z h d) -> p z h d", z=2, h=HEADS),
                                        qn[n % 2].rearrange("p (z h d) -> p z h d", z=2, h=HEADS),
                                        tab_c[:, l, t, :, :].unsqueeze(2).to_broadcast([P, 2, HEADS, DH]), ALU.mult)\
                         .then_inc(S["rot_a"], 1)

                    def rotate(u):
                        n = UT * l + u
                        v.wait_ge(S["rot_a"], after(it, NUT, n + 1))
                        v.wait_ge(S["rot_bb"], after(it, 2 * NUT, 2 * n + 2))
                        d.tensor_tensor(rot[u % HEADS_LAG], rot[u % HEADS_LAG], rotb[n % 2], ALU.add).then_inc(S["rotated"], 1)

                    def scores_out(u):
                        n = UT * l + u
                        sc = bank((n % 2) * 2, of=2).rearrange("p (h k) -> p h k", h=HEADS)
                        v.wait_ge(S["s_mm"], after(it, NUT, n + 1))
                        d.tensor_reduce(smx[n % 2][:, :], sc, AX.X, ALU.max).then_inc(S["smax"], 1)
                        v.wait_ge(S["smax"], after(it, NUT, n + 1))
                        v.wait_ge(S["pT_mm"], after(it, NUT, n - 1))
                        d.tensor_tensor(sdiff[n % 2], sc, smx[n % 2][:, :].unsqueeze(2).to_broadcast([P, HEADS, P]),
                                        ALU.subtract).then_inc(S["diffed"], 1)

                    def o_out(u):
                        s, t, n = u // NT, u % NT, UT * l + u
                        ob = bank(6, of=2).rearrange("p (b n) -> p b n", b=2)[:, :, 0:4 * VW]\
                            .rearrange("p b (h d) -> p b h d", h=4)
                        v.wait_ge(S["o_mm"], after(it, NUT, n + 1))
                        d.reciprocal(orec[n % 2][:, :, :], ob[:, :, :, DH]).then_inc(S["o_rec"], 1)
                        v.wait_ge(S["o_rec"], after(it, NUT, n + 1))
                        d.tensor_tensor(o_sb[s][:, t, :].rearrange("p (b h d) -> p b h d", b=2, h=4), ob[:, :, :, 0:DH],
                                        orec[n % 2][:, :, :].unsqueeze(3).to_broadcast([P, 2, 4, DH]), ALU.mult)\
                         .then_inc(S["o_norm"], 1)

                    def y_att(s):
                        v.wait_ge(S["wo_mm"], after(it, NU, unit(l, s) + 1))
                        d.tensor_tensor(y[s][:, :, :], y[s][:, :, :], bank(2 + s).rearrange("p (t c) -> p t c", t=NT),
                                        ALU.add).then_inc(S["y_att"], 1)
                        v.wait_ge(S["y_att"], after(it, NU, unit(l, s) + 1))
                        d.tensor_copy(hs[s][:, :, 0:64], y[s][:, :, 0:64])
                        d.memset(hs[s][0:1, 0:1, 64:P], 0.0).then_inc(S["hs_top"], 1)

                    def hs_stats(s):
                        v.wait_ge(S["hs_top"], after(it, NU, unit(l, s) + 1))
                        v.wait_ge(hs_in[s], it * (LAYERS * 32) + 32 * (l + 1))
                        norm_stats(it, ln_ffn(l, s), hs[s])

                    def gated_l0(m):
                        n = HC * unit(l, 0) + m
                        v.wait_ge(S["gelued"], after(it, HC * NU, n + 1))
                        b0 = (4, 0)[m % 2]
                        d.scalar_tensor_tensor(out=act[m // HC][:, m % HC, :], in0=ps[0:HW, b0 * BANK:(b0 + 1) * BANK],
                                               scalar=b1[:, l, 0, m % HC:m % HC + 1], in1=gel[:, :], op0=ALU.add,
                                               op1=ALU.mult).then_inc(S["acted"], 1)

                    def y_out(s):
                        v.wait_ge(S["down_mm"], after(it, NU, unit(l, s) + 1))
                        v.wait_ge(S["based"], after(it, NU, unit(l, s) + 1))
                        dst = y[s][:, :, :] if l < LAYERS - 1 else xr_tiles(it, s)
                        d.tensor_tensor(dst, ybase[:, :, :], bank(2 + s).rearrange("p (t c) -> p t c", t=NT),
                                        ALU.add).then_inc(S["y_out"], 1)

                    upper_half(0)
                    squares_sum(0)
                    inverse(0)
                    normalise(0)
                    squares_sum(1)
                    scale_cos(0)
                    inverse(1)
                    upper_half(1)
                    for u in range(UT):
                        if u + 1 < UT:
                            normalise(u + 1)
                        if u + 2 < UT:
                            squares_sum(u + 2)
                        if u + 1 < UT:
                            scale_cos(u + 1)
                        else:
                            scores_out(0)
                        if u + 2 < UT:
                            inverse(u + 2)
                        rotate(u)
                    scores_out(1)
                    for u in range(UT):
                        if u + 2 < UT:
                            scores_out(u + 2)
                        o_out(u)
                    y_att(0)
                    hs_stats(0)
                    y_att(1)
                    norm_apply(it, ln_ffn(l, 0), hs[0], hs[0])
                    hs_stats(1)
                    norm_apply(it, ln_ffn(l, 1), hs[1], hs[1])
                    for m in range(2 * HC):
                        gated_l0(m)
                    y_out(0)
                    y_out(1)

            steps = [0]

            def link(ins):
                steps[0] += 1
                ins.then_inc(M["step"], 1)
                v.wait_ge(M["step"], steps[0])

            def choose(b, at):
                def te(x):
                    return x.rearrange("p (t e) -> p t e", t=NT)

                tiles = slice(b * NT, (b + 1) * NT)
                n, lg = NT * EXP, te(ps[:, at:at + NT * EXP])
                top = rmax[:, tiles]
                if b == 0:
                    v.wait_ge(M["w_in"], 5 * 16)
                    d.memset(ones_b, 1.0)
                    d.memset(hot[:, TILES - NT:, :], 0.0)
                    d.tensor_copy(tri, tri_f).then_inc(M["tri"], 1)
                d.tensor_reduce(top, lg, AX.X, ALU.max).then_inc(M["rmax"], 1)
                v.wait_ge(M["rmax"], b + 1)
                d.tensor_tensor(te(m1[:, 0:n]), lg, top.unsqueeze(2).to_broadcast([P, NT, EXP]), ALU.is_equal)\
                 .then_inc(M["lg_used"], 1)
                v.wait_ge(M["lg_used"], b + 1)
                link(d.tensor_tensor(te(m2[:, 0:n]), te(m1[:, 0:n]),
                                     consts[:, 0:EXP].unsqueeze(1).to_broadcast([P, NT, EXP]), ALU.mult))
                link(d.tensor_reduce(rev2[:, tiles], te(m2[:, 0:n]), AX.X, ALU.max))
                if b == BATCH - 1:
                    v.wait_ge(M["ranked"], 1)
                d.tensor_tensor(hot[:, tiles, :], te(m2[:, 0:n]), rev2[:, tiles].unsqueeze(2).to_broadcast([P, NT, EXP]),
                                ALU.is_equal).then_inc(M["hot"], 1)
                v.wait_ge(M["hot"], b + 1)

            def scale_rows(b):
                tiles = slice(b * NT, (b + 1) * NT)
                sc = score[:, tiles]
                v.wait_ge(M["esc"], b + 1)
                link(d.tensor_scalar(sc, esc[:, tiles], 1.0, None, ALU.add))
                link(d.reciprocal(sc, sc))
                v.wait_ge(M["hT_mm"], b + 1)
                d.tensor_copy(rows_m[:, tiles, P:ROW], consts[:, P + b * NT:P + (b + 1) * NT].unsqueeze(2))
                d.tensor_tensor(h_m[:, tiles, :], h_m[:, tiles, :], sc.unsqueeze(2).to_broadcast([P, NT, P]), ALU.mult)\
                 .then_inc(M["scaled"], 1)

            def gate_s(n):
                b, c = n // IC, n % IC
                v.wait_ge(M["silu"], n + 1)
                if b >= 2 and c == 0:
                    v.wait_ge(M["down_mm"], b - 1)
                at = up_banks(n) + 1
                d.tensor_tensor(act_s[b % 2][:, c, :], silu_s[n % 2], bank(at), ALU.mult).then_inc(M["acted"], 1)

            def add_s(b):
                v.wait_ge(M["down_mm"], b + 1)
                xb = xr[:, b * NT:(b + 1) * NT, :]
                d.tensor_tensor(xb, xb, bank(6).rearrange("p (t c) -> p t c", t=NT), ALU.add).then_inc(M["x4s"], 1)

            v.wait_ge(T["w_in"], 5 * 16)
            d.tensor_scalar(bqk[:, 0:1], bqk[:, 0:1], DK ** -0.5, None, ALU.mult).then_inc(T["q_bias"], 1)
            for what, b, i in l1_steps():
                xb = xr[:, b * NT:(b + 1) * NT, :]
                if what == "stat":
                    norm_stats(PAIRS, b, xb)
                if what == "apply":
                    if b:
                        v.wait_ge(T["xn_mm"], b)
                    norm_apply(PAIRS, b, xb, z1)
                if what == "sums":
                    v.wait_ge(T["wv_in"], 32)
                    d.tensor_reduce(wvg, wv_raw.rearrange("p (c j) -> p c j", j=GRP), AX.X, ALU.add)
                    d.tensor_reduce(bvg, bv_raw.rearrange("p (c j) -> p c j", j=GRP), AX.X, ALU.add).then_inc(T["wv"], 1)
                if what == "val":
                    v.wait_ge(T["v_mm"], b + 1)
                    v.wait_ge(T["zero"], 6)
                    if b >= 3:
                        v.wait_ge(T["pv"], 8 * (b - 2))
                    d.tensor_tensor(v1[b % 3][:, :, :, 0:VG], bank(l1_bank[what, b, i]).rearrange("p (t h g) -> p t h g", t=NT, h=H1),
                                    bvg.rearrange("p (h g) -> p h g", h=H1).unsqueeze(1).to_broadcast([P, NT, H1, VG]),
                                    ALU.add).then_inc(T["v_sb"], 1)
                if what == "max":
                    v.wait_ge(T["d_mm"], 16 * b + i + 1)
                    if b >= 2 and i == 0:
                        v.wait_ge(T["ms_mm"], b - 1)
                    d.tensor_reduce(mneg[b % 2][:, 2 * i:2 * i + 2], bank(l1_bank[what, b, i], of=2)
                                    .rearrange("p (q t) -> p q t", q=2), AX.X, ALU.max, negate=True).then_inc(T["mx"], 1)
                if what == "shift":
                    v.wait_ge(T["ms_mm"], b + 1)
                    if b:
                        v.wait_ge(sh_in[(b - 1) % 3], 16 * NSH * ((b - 1) // 3 + 1))
                    src = ps[0:H1 * NT, l1_bank[what, b, i] * BANK:l1_bank[what, b, i] * BANK + P]
                    d.tensor_copy(shift_p[:, 0, :], src).then_inc(T["ms_part"], 1)
                    v.wait_ge(T["ms_part"], 3 * b + 1)
                    d.tensor_tensor(shift_r[:, :], src, shift_p[:, 0, :], ALU.subtract).then_inc(T["ms_part"], 1)
                    v.wait_ge(T["ms_part"], 3 * b + 2)
                    d.tensor_copy(shift_p[:, 1, :], shift_r[:, :]).then_inc(T["ms_part"], 1)
                    v.wait_ge(T["ms_part"], 3 * b + 3)
                    d.tensor_tensor(shift_p[:, 2, :], shift_r[:, :], shift_p[:, 1, :], ALU.subtract).then_inc(T["ms_sb"], 1)
                if what == "end":
                    o = bank(6, of=2).rearrange("p (b n) -> p b n", b=2)[:, :, 0:16 * (VG + 1)]\
                        .rearrange("p b (j g) -> p b j g", j=16)
                    v.wait_ge(T["sel_mm"], b + 1)
                    d.reciprocal(arec[:, :, :], o[:, :, :, VG]).then_inc(T["rec"], 1)
                    v.wait_ge(T["rec"], b + 1)
                    d.tensor_tensor(att[:, :, :].rearrange("p t c -> p (t c)").rearrange("p (b j g) -> p b j g", b=2, j=16),
                                    o[:, :, :, 0:VG], arec[:, :, :].unsqueeze(3).to_broadcast([P, 2, 16, VG]), ALU.mult)\
                     .then_inc(T["att"], 1)
                    v.wait_ge(T["att"], b + 1)
                    xb = xr[:, b * NT:(b + 1) * NT, :]
                    d.tensor_tensor(xb, xb, att[:, :, :], ALU.add).then_inc(T["x3"], 1)

                if what == "rstat":
                    v.wait_ge(T["x3"], b + 1)
                    norm_stats(PAIRS, BATCH + b, xb)
                if what == "rapply":
                    if b == 0:
                        v.wait_ge(T["f_mm"], 32)
                        v.wait_ge(T["xn_mm"], BATCH)
                    norm_apply(PAIRS, BATCH + b, xb, h_m[:, b * NT:(b + 1) * NT, :])
                if what == "s_up":
                    gate_s(IC * b + i)
                if what == "s_down":
                    add_s(b)
                if what == "scale":
                    scale_rows(b)
                if what == "route":
                    v.wait_ge(M["logits"], b + 1)
                    choose(b, l1_bank[what, b, i] * BANK)

            def te(x):
                return x.rearrange("p (t e) -> p t e", t=TILES)

            v.wait_ge(M["rank_mm"], 1)
            cnt = bank(1)[:, 0:EXP]
            link(d.tensor_tensor(m1.rearrange("p (e k) -> p e k", e=EXP), cnt.unsqueeze(2).to_broadcast([P, EXP, TILES]),
                                 consts[:, EXP:EXP + TILES].unsqueeze(1).to_broadcast([P, EXP, TILES]), ALU.is_gt))
            link(d.tensor_reduce(ntile, m1.rearrange("p (e k) -> p e k", e=EXP), AX.X, ALU.add))
            link(d.tensor_tensor_scan(incl, ones_f[:, :], ntile, 0.0, ALU.mult, ALU.add))
            link(d.tensor_tensor(base_e, incl, ntile, ALU.subtract))
            link(d.scalar_tensor_tensor(out=te(m1), in0=base_e.unsqueeze(1).to_broadcast([P, TILES, EXP]), scalar=float(P),
                                        in1=te(bank(7)), op0=ALU.mult, op1=ALU.add))
            link(d.tensor_tensor(te(m2), te(m1), hot, ALU.mult))
            link(d.tensor_reduce(slot_f, te(m2), AX.X, ALU.add))
            d.tensor_copy(slot_i, slot_f).then_inc(M["slots"], 1)
            scale_rows(BATCH - 1)
            for n in range(SHARED_EARLY, SHARED_EARLY + IC):
                gate_s(n)
            add_s(SHARED_EARLY // IC)
            nst = LOOP_TILES + AHEAD
            m3v = m3.rearrange("p (j e) -> p j e", e=EXP)
            link(d.tensor_tensor(m3v, consts[0:1, EXP + TILES:EXP + TILES + nst].unsqueeze(2).to_broadcast([1, nst, EXP]),
                                 incl[0:1, :].unsqueeze(1).to_broadcast([1, nst, EXP]), ALU.is_ge))
            link(d.tensor_reduce(exp_of_f, m3v, AX.X, ALU.add))
            d.tensor_scalar(exp_of, exp_of_f, float(EXP - 1), None, ALU.min).then_inc(M["slots"], 1)
            for b in range(SHARED_EARLY // IC + 1, BATCH):
                for c in range(IC):
                    gate_s(IC * b + c)
                add_s(b)

            def gated(t, j):
                v.wait_ge(M["r_silu"], j + 1)
                if not (isinstance(j, int) and j < 2):
                    v.wait_ge(M["actT_mm"], j - 1)
                d.tensor_tensor(act_r[t % 2], silu_r[t % 2], bank(2 + t % 2)[:, INTER:2 * INTER], ALU.mult)\
                 .then_inc(M["r_act"], 1)

            def dve_step(i, r, last):
                if not last or r + UP < AHEAD:
                    gated(r + UP, i * AHEAD + r + UP)
                v.wait_ge(M["y_mm"], i * AHEAD + r + 1)
                v.wait_ge(M["ids"], i * AHEAD + r + 1)
                d.tensor_copy(ys[r], bank(6 + r % 2)[:, 0:P]).then_inc(M["y_sb"], 1)

            v.sem_inc(M["y_sb"], 2)
            for t in range(UP):
                gated(t, t)
            experts(v, dve_step)
            for b in range(BATCH):
                v.wait_ge(gathered[b], 16)
                xb = xr[:, b * NT:(b + 1) * NT, :]
                d.tensor_tensor(xb, xb, y_g[:, b * NT:(b + 1) * NT, :], ALU.add).then_inc(M["x4"], 1)

        @block.tensor
        def _(pe):
            mm, tr = nc.tensor.matmul, nc.tensor.transpose
            for name in COUNTED["PE"]:
                pe.sem_inc(S[name], 1)
            pe.wait_ge(S["idn"], 2)

            def front_T(b):
                pe.wait_ge(S["ln_out"], norms(0, b - BATCH + 1))
                for t in range(NT):
                    last = tr(bank(6 + b % 2)[:, t * P:(t + 1) * P], y[b % 2][:, t, :], ident[:, :])
                last.then_inc(S["xnT_mm"], 1)

            def recurrence_mm(b):
                pe.wait_ge(S["scanned"], after(0, 0, b + 1))
                if b >= 2:
                    pe.wait_ge(S["x1"], after(0, 0, b - 1))
                for t in range(NT):
                    last = mm(bank(2 + b % 2)[:, t * P:(t + 1) * P], hT_scan[b % 2][:, t * P:(t + 1) * P], bc_w[:, :],
                              start=True, stop=True)
                last.then_inc(S["bc_mm"], 1)

            front_T(0)
            front_T(1)
            for b in range(BATCH):
                recurrence_mm(b)
                if b + 2 < BATCH:
                    front_T(b + 2)
            pe.wait_ge(S["x1"], after(0, 0, BATCH))
            pe.wait_ge(S["tabs"], 1)
            pe.wait_ge(S["zero_p"], 6)
            pe.wait_ge(S["small_in"], 9 * 16)
            pe.wait_ge(S["w_in"], 8 * 16)
            with pe.Fori(0, PAIRS) as it:
                for l in range(LAYERS):
                    def stream_T(s):
                        if s == 0:
                            pe.wait_ge(S["acted"], after(it, HC * NU, HC * unit(l, 0)))
                        else:
                            pe.wait_ge(S["hT_lo"], after(it, NU, unit(l, 0) + 1))
                            pe.wait_ge(S["hT_hi"], after(it, NU, unit(l, 0) + 1))
                        if l == 0:
                            pe.wait_ge(S["ln_out"], norms(it, s + 1))
                        else:
                            pe.wait_ge(S["y_out"], after(it, NU, unit(l - 1, s) + 1))
                        for t in range(NT):
                            last = tr(bank(5)[:, t * P:(t + 1) * P], y[s][:, t, :], ident[:, :])
                        last.then_inc(S["yT_mm"], 1)

                    def project_qkv(u):
                        s, t, n = u // NT, u % NT, UT * l + u
                        if t == 0:
                            pe.wait_ge(S["hT_lo"], after(it, NU, unit(l, s) + 1))
                            pe.wait_ge(S["hT_hi"], after(it, NU, unit(l, s) + 1))
                        if u == 1:
                            pe.wait_ge(S["y_out"], after(it, NU, unit(l, 0)))
                        pe.wait_ge(S["normed"], after(it, NUT, n - 1))
                        lhs = hT[s][:, t * P:(t + 1) * P]
                        mm(bank((n % 2) * 2), lhs, wqkv[l][:, 0:INNER], start=True, stop=True)
                        mm(bank((n % 2) * 2 + 1), lhs, wqkv[l][:, INNER:2 * INNER], start=True, stop=True)\
                            .then_inc(S["qk_mm"], 1)
                        pe.wait_ge(S["v_sb"], after(it, NUT, n))
                        mm(bank(4), lhs, wqkv[l][:, 2 * INNER:3 * INNER], start=True, stop=True).then_inc(S["v_mm"], 1)

                    def heads_T(u):
                        n = UT * l + u
                        pe.wait_ge(S["rotated"], after(it, NUT, n + 1))
                        if u == 0:
                            pe.wait_ge(S["hnT_sb"], after(it, NU, unit(l, 0)))
                        pe.wait_ge(S["qkT_sb"], after(it, NUT, n))
                        for z in range(2):
                            for h in range(HP):
                                last = tr(bank(6 + z)[:, h * P:(h + 1) * P],
                                          rot[u % HEADS_LAG][:, (z * HP + h) * P:(z * HP + h + 1) * P], ident[:, :])
                        last.then_inc(S["qkT_mm"], 1)

                    def scores(u):
                        s, t, n = u // NT, u % NT, UT * l + u
                        if t == 0:
                            pe.wait_ge(S["qkT_sb"], after(it, NUT, n + NT))
                        if u < 2:
                            pe.wait_ge(S["normed"], after(it, NUT, n + UT - 2 + 1))
                        else:
                            pe.wait_ge(S["diffed"], after(it, NUT, n - 1))
                        for b in range(2):
                            bk = (n % 2) * 2 + b
                            mm(bank(bk).rearrange("p (h k) -> p h k", h=4), ident_b[:, :],
                               mask_b[:, 0 if t else 1, :].unsqueeze(1).to_broadcast([P, 4, P]),
                               start=True, stop=True, skip_group_check=True)
                            for w in range(2):
                                for h in range(2):
                                    q0 = t * P + w * WIN
                                    last = mm(ps[w * WIN:(w + 1) * WIN, bk * BANK + h * 256:bk * BANK + (h + 1) * 256],
                                              qT[s][:, 2 * b + h, q0:q0 + WIN], kz[s][:, 2 * b + h, :, q0:q0 + P],
                                              start=False, stop=True, skip_group_check=True)
                        last.then_inc(S["s_mm"], 1)

                    def probs_T(u):
                        n = UT * l + u
                        pe.wait_ge(S["diffed"], after(it, NUT, n + 1))
                        if u == 0:
                            pe.wait_ge(S["v_sb"], after(it, NUT, UT * (l + 1)))
                        pe.wait_ge(S["exped"], after(it, NUT, n))
                        for h in range(HEADS):
                            last = tr(bank(4 + h // 4)[:, (h % 4) * P:(h % 4 + 1) * P], sdiff[n % 2][:, h, :], ident[:, :])
                        last.then_inc(S["pT_mm"], 1)

                    def values(u):
                        s, t, n = u // NT, u % NT, UT * l + u
                        pe.wait_ge(S["exped"], after(it, NUT, n + 1))
                        if u == 0:
                            pe.wait_ge(S["qkT_sb"], after(it, NUT, UT * (l + 1)))
                        if t == 0:
                            pe.wait_ge(v_off_in[s], it * (LAYERS * 32) + 32 * (l + 1))
                        pe.wait_ge(S["o_norm"], after(it, NUT, n))
                        for w in range(2):
                            vals = (v_off if w == 0 else v_al)[s]
                            for h in range(HEADS):
                                c0 = (6 + h // 4) * BANK + (h % 4) * VW
                                last = mm(ps[w * WIN:(w + 1) * WIN, c0:c0 + VW], pts[n % 2][:, h, w * WIN:(w + 1) * WIN],
                                          vals[:, t, h, :], start=True, stop=True)
                        last.then_inc(S["o_mm"], 1)

                    def o_T(u):
                        s, t, n = u // NT, u % NT, UT * l + u
                        pe.wait_ge(S["o_norm"], after(it, NUT, n + 1))
                        if u >= 2:
                            pe.wait_ge(S["oT_sb"], after(it, NUT, n - 1))
                        for c in range(4):
                            last = tr(bank(n % 2)[:, c * P:(c + 1) * P], o_sb[s][:, t, c * P:(c + 1) * P], ident[:, :])
                        last.then_inc(S["oT_mm"], 1)

                    def project_o(u):
                        s, t, n = u // NT, u % NT, UT * l + u
                        pe.wait_ge(S["oT_sb"], after(it, NUT, n + 1))
                        for c in range(4):
                            last = mm(bank(2 + s)[:, t * P:(t + 1) * P], oT[n % 2][:, c, :], wo[l][:, c, :],
                                      start=(c == 0), stop=(c == 3))
                        if t == 3:
                            last.then_inc(S["wo_mm"], 1)

                    def normed_T(s):
                        pe.wait_ge(S["ln_out"], norms(it, ln_ffn(l, s) + 1))
                        for t in range(NT):
                            last = tr(bank(6 + s)[:, t * P:(t + 1) * P], hs[s][:, t, :], ident[:, :])
                        last.then_inc(S["hnT_mm"], 1)

                    def up_l0(m):
                        s, c, n = m // HC, m % HC, HC * unit(l, 0) + m
                        if c == 0:
                            pe.wait_ge(S["hnT_sb"], after(it, NU, unit(l, s) + 1))
                        if m >= 2:
                            pe.wait_ge(S["acted"], after(it, HC * NU, n - 1))
                        b0 = (4, 0)[m % 2]
                        for g in range(2):
                            last = mm(ps[0:HW, (b0 + g) * BANK:(b0 + g + 1) * BANK], w1[l][:, g, c, :], hnT[s],
                                      start=True, stop=True)
                        last.then_inc(S["up_mm"], 1)

                    def down_l0(s):
                        pe.wait_ge(S["acted"], after(it, HC * NU, HC * (unit(l, s) + 1)))
                        for t in range(NT):
                            for c in range(HC):
                                last = mm(bank(2 + s)[:, t * P:(t + 1) * P], act[s][:, c, t * P:(t + 1) * P],
                                          w2[l][0:HW, c, :], start=(c == 0), stop=(c == HC - 1))
                        last.then_inc(S["down_mm"], 1)

                    stream_T(0)
                    for u in range(UT):
                        project_qkv(u)
                        if u == 1:
                            stream_T(1)
                        if u >= HEADS_LAG:
                            heads_T(u - HEADS_LAG)
                    heads_T(UT - 3)
                    scores(0)
                    heads_T(UT - 2)
                    scores(1)
                    heads_T(UT - 1)
                    probs_T(0)
                    for u in range(UT):
                        if u + 2 < UT:
                            scores(u + 2)
                        if u + 1 < UT:
                            probs_T(u + 1)
                        if u == UT - 1:
                            o_T(0)
                        values(u)
                    o_T(1)
                    for u in range(UT):
                        project_o(u)
                        if u + 2 < UT:
                            o_T(u + 2)
                    normed_T(0)
                    for m in range(2 * HC):
                        up_l0(m)
                        if m == HC - 1:
                            normed_T(1)
                    down_l0(0)
                    down_l0(1)
            pe.wait_ge(T["w_in"], 5 * 16)
            ring = [(S["y_out"], after(PAIRS, NU, 0))] * 3

            def pair_of_banks(what, b, i, reader):
                at = l1_bank[what, b, i] // 2
                pe.wait_ge(*ring[at])
                ring[at] = reader
                return 2 * at

            def values1(b, i):
                hg, kt = i // 4, i % 4
                pe.wait_ge(T["ex"], 16 * b + 2 * i + 2)
                if kt == 0:
                    if b:
                        pe.wait_ge(T["att"], b)
                    if i == 0:
                        pe.wait_ge(T["v_sb"], b + 1)
                for h in range(4):
                    last = mm(ps[32 * h:32 * (h + 1), (6 + hg) * BANK:(7 + hg) * BANK],
                              v1[b % 3][:, kt, 4 * hg + h, :], pt[i % 2][:, h, :], start=(kt == 0), stop=(kt == NT - 1),
                              skip_group_check=True)
                last.then_inc(T["pv"], 1)

            def shared_up(n, n0):
                c, b = n % IC, n // IC
                for z, w in enumerate((sg, su)):
                    last = mm(bank(n0 + z), w[:, c * P:(c + 1) * P], hT_m[:, b * SEQ:(b + 1) * SEQ], start=True, stop=True)
                last.then_inc(M["up_mm"], 1)

            def rank(t0, t1):
                own = slice(t0, t1 if t0 else TILES)
                mm(bank(7).rearrange("p (t e) -> p t e", e=EXP)[:, own, :], tri, hot[:, own, :], start=(t0 == 0),
                   stop=True, skip_group_check=True)
                for t in range(t0, min(t1, TILES - 1)):
                    last = mm(bank(7)[:, (t + 1) * EXP:].rearrange("p (t e) -> p t e", e=EXP), ones_b,
                              hot[:, t, :].unsqueeze(1).to_broadcast([P, TILES - 1 - t, EXP]), start=False, stop=True,
                              skip_group_check=True)
                last.then_inc(M["ranked"], 1)

            def shared_down(b):
                pe.wait_ge(M["acted"], IC * (b + 1))
                if b:
                    pe.wait_ge(M["x4s"], b)
                else:
                    pe.wait_ge(T["att"], BATCH)
                for t in range(NT):
                    for c in range(IC):
                        last = mm(bank(6)[:, t * P:(t + 1) * P], act_s[b % 2][:, c, t * P:(t + 1) * P], sd[:, c, :],
                                  start=(c == 0), stop=(c == IC - 1))
                last.then_inc(M["down_mm"], 1)

            for what, b, i in l1_steps():
                k = b % 3
                if what == "s_up":
                    shared_up(IC * b + i, pair_of_banks(what, b, i, (M["acted"], IC * b + i + 1)))
                if what == "s_down":
                    shared_down(b)
                if what == "rank":
                    pe.wait_ge(T["att"], BATCH)
                    pe.wait_ge(M["tri"], 1)
                    pe.wait_ge(M["hot"], BATCH - 1)
                    rank(0, TILES - NT)
                if what == "pre":
                    n0 = pair_of_banks(what, b, i, (T["xn_sb"], b + 1))
                    pe.wait_ge(S["ln_out"], norms(PAIRS, b + 1))
                    for t in range(NT):
                        last = tr(bank(n0)[:, t * P:(t + 1) * P], z1[:, t, :], ident[:, :])
                    last.then_inc(T["xn_mm"], 1)
                if what == "qk":
                    n0 = pair_of_banks(what, b, i, (T["part"], 4 * b + 2))
                    pe.wait_ge(T["xn_sb"], b + 1)
                    mm(bank(n0), wq, xn1[:, :], start=True, stop=True).then_inc(T["qk_mm"], 1)
                    mm(bank(n0 + 1), wk, xn1[:, :], start=True, stop=True).then_inc(T["qk_mm"], 1)
                if what == "val":
                    n0 = pair_of_banks(what, b, i, (T["v_sb"], b + 1))
                    pe.wait_ge(T["wv"], 1)
                    for t in range(NT):
                        last = mm(bank(n0)[:, t * P:(t + 1) * P], xn1[:, t * P:(t + 1) * P], wvg, start=True, stop=True)
                    last.then_inc(T["v_mm"], 1)
                if what == "max":
                    n0 = pair_of_banks(what, b, i, (T["mx"], 16 * b + i + 1))
                    if i == 0:
                        pe.wait_ge(st_in[k], 16 * 2 * len(RUNS) * (b // 3 + 1))
                    h = i // 2
                    for j in range(2):
                        q0 = ((i % 2) * 2 + j) * P
                        last = mm(bank(n0 + j), qst[k][0:KS, h, q0:q0 + P], kst[k][0:KS, h, :], start=True, stop=True)
                    last.then_inc(T["d_mm"], 1)
                if what == "shift":
                    n0 = pair_of_banks(what, b, i, (T["ms_sb"], b + 1))
                    pe.wait_ge(T["mx"], 16 * (b + 1))
                    tr(ps[0:H1 * NT, n0 * BANK:n0 * BANK + P], mneg[b % 2][:, :], ident[:, :]).then_inc(T["ms_mm"], 1)
                if what == "probs":
                    n0 = pair_of_banks(what, b, i, (T["ex"], 16 * b + i + 1))
                    if i == 0:
                        pe.wait_ge(T["ones"], 16 * 3)
                        pe.wait_ge(sh_in[k], 16 * NSH * (b // 3 + 1))
                    kt, h0 = (i % 8) // 2, 4 * (i // 8) + 2 * (i % 2)
                    for j in range(2):
                        last = mm(bank(n0 + j), kst[k][0:KS + NSH, h0 + j, kt * P:(kt + 1) * P],
                                  qst[k][0:KS + NSH, h0 + j, :], start=True, stop=True)
                    last.then_inc(T["f_mm"], 1)
                    if i % 2 == 1 and (b or i > 1):
                        values1(*divmod(8 * b + i // 2 - 1, 8))
                if what == "rpre":
                    n0 = pair_of_banks(what, b, i, (M["hT_sb"], b + 1))
                    pe.wait_ge(S["ln_out"], norms(PAIRS, BATCH + b + 1))
                    for t in range(NT):
                        last = tr(bank(n0)[:, t * P:(t + 1) * P], h_m[:, b * NT + t, :], ident[:, :])
                    last.then_inc(M["hT_mm"], 1)
                if what == "route":
                    n0 = pair_of_banks(what, b, i, (M["lg_used"], b + 1))
                    pe.wait_ge(M["w_gate"], 16)
                    pe.wait_ge(M["hT_sb"], b + 1)
                    for t in range(NT):
                        c0 = b * SEQ + t * P
                        last = mm(bank(n0)[:, t * EXP:(t + 1) * EXP], hT_m[:, c0:c0 + P], gate_w, start=True, stop=True)
                    last.then_inc(M["logits"], 1)
                if what == "end":
                    if b == BATCH - 1:
                        values1(b, 7)
                    for hg in range(2):
                        pe.wait_ge(T["at_sb"], 2 * b + hg + 1)
                        cols = at_sb[hg].rearrange("p (r l) -> p r l", l=GRP)
                        for par in range(2):
                            for l in range(GRP):
                                dst = ps[64 * par:64 * par + 64, (6 + hg) * BANK:(6 + hg) * BANK + 16 * (VG + 1)]\
                                    .rearrange("p (j l g) -> p j l g", j=2, l=GRP)[:, :, l, :]
                                last = mm(dst, cols[:, :, l], sel[:, par, :].rearrange("p (j g) -> p j g", j=2),
                                          start=True, stop=True)
                    last.then_inc(T["sel_mm"], 1)
            pe.wait_ge(T["x3"], BATCH)
            pe.wait_ge(M["w_in"], 5 * 16)
            pe.wait_ge(T["ex"], 16 * BATCH)

            pe.wait_ge(M["hot"], BATCH)
            rank(TILES - NT, TILES)
            for t in range(TILES):
                last = mm(bank(1)[:, 0:EXP], ones_b, hot[:, t, :], start=(t == 0), stop=(t == TILES - 1))
            last.then_inc(M["rank_mm"], 1)
            for b in range(SHARED_EARLY // IC, BATCH):
                for n in range(IC * b, IC * (b + 1)):
                    pe.wait_ge(M["acted"], n - 1)
                    shared_up(n, up_banks(n))
                shared_down(b)

            def tokens_T(t, i):
                pe.wait_ge(xs_in[t % AHEAD], i * 16 + 16 * (t // AHEAD + 1))
                tr(bank(t % 2)[:, 0:P], xs_in_sb[t % AHEAD], ident[:, :]).then_inc(M["xT_mm"], 1)

            def expert_of(t, i):
                return pe.value_load(exp_of[0:1, bass.ds(i * AHEAD + t, 1)], min_val=0, max_val=EXP - 1)

            def gate_up(t, i, e):
                pe.wait_ge(M["xT_sb"], i * AHEAD + t + 1)
                mm(bank(2 + t % 2), xsT[t % 2], wgu[:, bass.ds(e, 1), :].rearrange("p a n -> p (a n)"),
                   start=True, stop=True).then_inc(M["gu_mm"], 1)

            def gated_T(t, i):
                pe.wait_ge(M["r_act"], i * AHEAD + t + 1)
                for c in range(IC):
                    last = tr(bank(4 + t % 2)[:, c * P:(c + 1) * P], act_r[t % 2][:, c * P:(c + 1) * P], ident[:, :])
                last.then_inc(M["actT_mm"], 1)

            def down(t, i, e):
                pe.wait_ge(M["actT_sb"], i * AHEAD + t + 1)
                pe.wait_ge(M["y_sb"], i * AHEAD + t + 1)
                for c in range(IC):
                    last = mm(bank(6 + t % 2)[:, 0:P], actT[t % 2][:, c * P:(c + 1) * P],
                              wd[:, bass.ds(e, 1), c, :].rearrange("p a n -> p (a n)"), start=(c == 0), stop=(c == IC - 1))
                last.then_inc(M["y_mm"], 1)

            held = {}

            def pe_step(i, r, last):
                if r == 0:
                    held.clear()
                if not last or r + UP < AHEAD:
                    held[r + UP] = expert_of(r + UP, i)
                    gate_up(r + UP, i, held[r + UP])
                if not last or r + XT < AHEAD:
                    tokens_T(r + XT, i)
                if not last or r + BACK < AHEAD:
                    gated_T(r + BACK, i)
                down(r, i, held[r] if r in held else expert_of(r, i))

            pe.wait_ge(M["slots"], 2)
            pe.wait_ge(M["x4s"], BATCH)
            pe.wait_ge(M["w_gu"], 16 * 16)
            pe.wait_ge(M["w_d"], 4 * 16)
            tokens_T(0, 0)
            tokens_T(1, 0)
            gate_up(0, 0, expert_of(0, 0))
            tokens_T(2, 0)
            gate_up(1, 0, expert_of(1, 0))
            gated_T(0, 0)
            experts(pe, pe_step)


def rotary_tables(np):
    f = np.float32
    half = np.arange(0, DH, 2, dtype=f)
    inv = (f(1.0) / np.power(f(10000.0), half / f(DH))).astype(f)
    t = np.arange(SEQ, dtype=f)
    fr = t[:, None] * inv[None, :]
    fr = np.concatenate([fr, fr], -1)
    base = (half + f(0.4 * DH)) / f(1.4 * DH)
    power = (t - SEQ // 2) / f(WIN // 2)
    sc = np.power(base[None, :], power[:, None]).astype(f)
    sc = np.concatenate([sc, sc], -1)
    cos, sin = np.cos(fr), np.sin(fr)
    sin = sin * np.concatenate([-np.ones(DH // 2, f), np.ones(DH // 2, f)])
    c = np.stack([cos * sc * f(8.0), cos / sc], 1)
    s = np.stack([sin * sc * f(8.0), sin / sc], 1)

    def lay(x):
        return np.ascontiguousarray(x.reshape(NT, P, 2, DH).transpose(1, 0, 2, 3).astype(f))

    return lay(c), lay(s)


def routing_constants(np):
    row = np.concatenate([EXP - np.arange(EXP), P * np.arange(TILES), np.arange(P - EXP - TILES)])
    ids = AHEAD + P * np.arange(TILES)[None, :] + np.arange(P)[:, None]
    return np.concatenate([np.broadcast_to(row, (P, P)), ids], 1).astype(np.float32)


def selector(np):
    sel = np.zeros((P, 2, 2, VG + 1), np.float32)
    for par in range(2):
        for j in range(2):
            for g in range(VG + 1):
                sel[32 * (2 * j + par) + g, par, j, g] = 1.0
    return sel.reshape(P, 2, 2 * (VG + 1))


def arrays_of(np, i):
    def c(a):
        return np.ascontiguousarray(a)

    def by_dim(a):
        a = np.asarray(a)
        return c(a.reshape(a.shape[:-1] + (H1, DK)).swapaxes(-1, -2).reshape(a.shape))

    tab_c, tab_s = rotary_tables(np)
    q = np.arange(P)[:, None] % WIN
    k = np.arange(P)[None, :]
    inside = (q <= k) & (k <= q + WIN)
    first = inside & ~((np.arange(P)[:, None] < WIN) & (k < WIN))
    f = np.float32
    mask = np.stack([np.where(inside, f(0), f(NEG)), np.where(first, f(0), f(NEG))], 1)
    qs, ks = np.asarray(i["L0_ffn_q_scale"]), np.asarray(i["L0_ffn_k_scale"])

    def swap(a):
        return np.concatenate([a[:, DH // 2:], a[:, :DH // 2]], -1)

    scales = np.stack([np.stack([qs, ks], 1), np.stack([swap(qs), swap(ks)], 1)], 1)
    w1, b1, w2 = (np.asarray(i["L0_ffn_" + n]) for n in ("w1", "b1", "w2"))
    w1 = np.pad(w1.reshape(LAYERS, P, 2, HID), ((0, 0),) * 3 + ((0, HC * HW - HID),)).reshape(LAYERS, P, 2, HC, HW)
    b1 = np.pad(b1.reshape(LAYERS, 2, HID), ((0, 0),) * 2 + ((0, HC * HW - HID),)).reshape(LAYERS, 2, HC, HW)
    w2 = np.pad(w2, ((0, 0), (0, HC * HW - HID), (0, 0))).reshape(LAYERS, HC, HW, P)
    return {
        "x": c(np.asarray(i["L0_attn_inputs"]).reshape(TOK, P)),
        "a": c(np.asarray(i["L0_attn_A"]).reshape(P, 1)),
        "bc": c(i["L0_attn_BC"]),
        "tab_c": tab_c, "tab_s": tab_s, "mask": c(mask.astype(f)),
        "scales": c(scales.reshape(LAYERS, 2, 2, DH)),
        "wqkv": c(i["L0_ffn_wqkv"]), "wo": c(i["L0_ffn_wo"]), "w1": c(w1), "w2": c(w2),
        "b1": c(b1.transpose(3, 0, 1, 2)), "b2": c(i["L0_ffn_b2"]),
        "wq": by_dim(i["L1_attn_Wq"]), "wk": by_dim(i["L1_attn_Wk"]), "wv": c(i["L1_attn_Wv"]), "bv": c(i["L1_attn_bv"]),
        "bqk": c(np.stack([by_dim(i["L1_attn_bq"]), by_dim(i["L1_attn_bk"])], 1)),
        "gb1": c(np.stack([np.asarray(i["L1_attn_gamma"]), np.asarray(i["L1_attn_beta"])], 1)),
        "sel": selector(np),
        "sg": c(i["L1_ffn_shared_gate_w"]), "su": c(i["L1_ffn_shared_up_w"]), "sd": c(i["L1_ffn_shared_down_w"]),
        "gate": c(i["L1_ffn_gate_w"]),
        "wgu": c(np.concatenate([np.asarray(i["L1_ffn_routed_gate_w"]), np.asarray(i["L1_ffn_routed_up_w"])], -1)
                 .transpose(1, 0, 2)),
        "wd": c(np.asarray(i["L1_ffn_routed_down_w"]).reshape(EXP, IC, P, P).transpose(2, 0, 1, 3)),
        "consts": routing_constants(np),
        "tri": c(np.triu(np.ones((P, P), np.float32), 1)),
        "ln_gb": c(np.stack([np.asarray(i["L0_ffn_ln_g"]), np.asarray(i["L0_ffn_ln_b"])], 1).transpose(2, 0, 1)),
    }


def kernel(**inputs):
    import numpy as _np
    import concourse.bacc as _bacc
    from concourse import mybir as _mybir
    from concourse.bass_utils import run_bass_kernel_spmd as _run

    nc = _bacc.Bacc("TRN2", target_bir_lowering=False, num_devices=1)
    arrays = arrays_of(_np, inputs)
    args = {n: nc.dram_tensor(f"in_{n}", a.shape, _mybir.dt.from_np(a.dtype), kind="ExternalInput").ap()
            for n, a in arrays.items()}
    out = nc.dram_tensor("out_0", (TOK, P), _mybir.dt.float32, kind="ExternalOutput").ap()
    build(nc, args, out)
    r = _run(nc, [{f"in_{n}": a for n, a in arrays.items()}], core_ids=[0])
    return r.results[0]["out_0"].reshape(BATCH, SEQ, P)
```
